# Optimizing a Trainium2 kernel written in Bass

```python
import numpy as np
import jax
import jax.numpy as jnp

def _softmax(x, axis=-1):
    return jax.nn.softmax(x, axis=axis)

def _gelu(x):
    return jax.nn.gelu(x, approximate=True)

def _silu(x):
    return jax.nn.silu(x)

def _sigmoid(x):
    return jax.nn.sigmoid(x)

def _layernorm(x, axis=-1, eps=1e-05):
    m = jnp.mean(x, axis=axis, keepdims=True)
    v = jnp.var(x, axis=axis, keepdims=True)
    return (x - m) / jnp.sqrt(v + eps)

def _scatter_add(tgt, idx, src, axis=0):
    return tgt.at[idx].add(src)

def _segment_sum(src, seg, n):
    return jax.ops.segment_sum(src, seg, n)
kernel_name = 'mk_adaln_d1_jaxref_r4_bde05e'

def setup_inputs(seed: int=0):
    np.random.seed(seed)
    _w = jnp.asarray

    def _L0_attn_setup():
        import jax, jax.numpy as jnp
        import numpy as np
        ROPE_THETA = 10000.0

        def _apply_rope(x, theta=ROPE_THETA):
            L, d_k = (x.shape[-2], x.shape[-1])
            inv_freq = 1.0 / theta ** (jnp.arange(0, d_k, 2, dtype=jnp.float32) / d_k)
            ang = jnp.arange(L, dtype=jnp.float32)[:, None] * inv_freq[None, :]
            ang = jnp.repeat(ang, 2, axis=-1)
            xr = x.reshape(x.shape[:-1] + (d_k // 2, 2))
            rot = jnp.stack((-xr[..., 1], xr[..., 0]), axis=-1).reshape(x.shape)
            return x * jnp.cos(ang) + rot * jnp.sin(ang)
        key = jax.random.key(seed)
        k1, k2, k3 = jax.random.split(key, 3)
        B, L, D = (2, 512, 512)
        std_qkv = np.sqrt(2.0 / (D + 3 * D)).astype(np.float32)
        std_o = np.sqrt(2.0 / (D + D)).astype(np.float32)
        return {'x': jax.random.normal(k1, (B, L, D), dtype=jnp.float32), 'W_qkv': jax.random.normal(k2, (3 * D, D), dtype=jnp.float32) * std_qkv, 'W_o': jax.random.normal(k3, (D, D), dtype=jnp.float32) * std_o}
    _L0_attn_in = _L0_attn_setup()

    def _L0_ffn_setup():
        import jax, jax.numpy as jnp
        import numpy as np
        TOP_K = 2
        key = jax.random.key(seed)
        k0, k1, k2, k3 = jax.random.split(key, 4)
        B, S, D, E, H = (4, 256, 512, 16, 256)
        x = jax.random.normal(k0, (B, S, D), jnp.float32) * 0.02
        Wg = jax.random.normal(k1, (E, D), jnp.float32) * 0.02
        balance_bias = jnp.zeros((E,), jnp.float32)
        W1 = jax.random.normal(k2, (E, D, H), jnp.float32) * 0.02
        W2 = jax.random.normal(k3, (E, H, D), jnp.float32) * 0.02
        return {'x': x, 'Wg': Wg, 'balance_bias': balance_bias, 'W1': W1, 'W2': W2}
    _L0_ffn_in = _L0_ffn_setup()
    _L0_c = _w((lambda *s: np.random.randn(*s).astype(np.float32) * 0.05)(4, 512))
    _L0_wmod = _w((lambda *s: np.random.randn(*s).astype(np.float32) * 0.05)(512, 6 * 512) * 512 ** (-0.5))
    _d = {'L0_attn_x': _L0_attn_in['x'], 'L0_attn_W_qkv': _L0_attn_in['W_qkv'], 'L0_attn_W_o': _L0_attn_in['W_o'], 'L0_ffn_Wg': _L0_ffn_in['Wg'], 'L0_ffn_balance_bias': _L0_ffn_in['balance_bias'], 'L0_ffn_W1': _L0_ffn_in['W1'], 'L0_ffn_W2': _L0_ffn_in['W2'], 'L0_c': _L0_c, 'L0_wmod': _L0_wmod}
    _x0 = _d['L0_attn_x']
    _d['L0_attn_x'] = jax.random.normal(jax.random.fold_in(jax.random.key(seed), 1), (4, 1024, 512), dtype=_x0.dtype)
    del _x0
    return _d

def reference(L0_attn_x, L0_attn_W_qkv, L0_attn_W_o, L0_ffn_Wg, L0_ffn_balance_bias, L0_ffn_W1, L0_ffn_W2, L0_c, L0_wmod):

    def _L0_attn_ref(x, W_qkv, W_o):
        import jax, jax.numpy as jnp
        import numpy as np
        ROPE_THETA = 10000.0

        def _apply_rope(x, theta=ROPE_THETA):
            L, d_k = (x.shape[-2], x.shape[-1])
            inv_freq = 1.0 / theta ** (jnp.arange(0, d_k, 2, dtype=jnp.float32) / d_k)
            ang = jnp.arange(L, dtype=jnp.float32)[:, None] * inv_freq[None, :]
            ang = jnp.repeat(ang, 2, axis=-1)
            xr = x.reshape(x.shape[:-1] + (d_k // 2, 2))
            rot = jnp.stack((-xr[..., 1], xr[..., 0]), axis=-1).reshape(x.shape)
            return x * jnp.cos(ang) + rot * jnp.sin(ang)
        B, L, D = x.shape
        H = 16
        dh = D // H
        qkv = jnp.einsum('bld,ed->ble', x, W_qkv)
        q, k, v = jnp.split(qkv, 3, axis=-1)
        q = q.reshape(B, L, H, dh).transpose(0, 2, 1, 3)
        k = k.reshape(B, L, H, dh).transpose(0, 2, 1, 3)
        v = v.reshape(B, L, H, dh).transpose(0, 2, 1, 3)
        q = _apply_rope(q)
        k = _apply_rope(k)
        scale = 1.0 / np.sqrt(dh).astype(np.float32)
        att = jnp.einsum('bhqd,bhkd->bhqk', q, k) * scale
        causal = jnp.tril(jnp.ones((L, L), dtype=bool))
        att = jnp.where(causal, att, -jnp.inf)
        p = jax.nn.softmax(att, axis=-1)
        y = jnp.einsum('bhqk,bhkd->bhqd', p, v)
        y = y.transpose(0, 2, 1, 3).reshape(B, L, D)
        return jnp.einsum('bld,ed->ble', y, W_o)

    def _L0_ffn_ref(x, Wg, balance_bias, W1, W2):
        import jax, jax.numpy as jnp
        import numpy as np
        TOP_K = 2
        B, S, D = x.shape
        E = Wg.shape[0]
        xf = x.reshape(-1, D)
        T = xf.shape[0]
        gate_logits = xf @ Wg.T
        gate_scores = jax.nn.sigmoid(gate_logits + balance_bias)
        topk_scores, topk_idx = jax.lax.top_k(gate_scores, TOP_K)
        topk_scores = topk_scores / (topk_scores.sum(-1, keepdims=True) + 1e-06)
        combine = jnp.zeros((T, E), xf.dtype).at[jnp.arange(T)[:, None], topk_idx].add(topk_scores)
        h = jax.nn.silu(jnp.einsum('td,edh->teh', xf, W1))
        out = jnp.einsum('teh,te,ehd->td', h, combine, W2)
        return out.reshape(B, S, D)
    x = L0_attn_x
    mod = (_silu(L0_c) @ L0_wmod).reshape(L0_c.shape[0], 6, 1, -1)
    sa, ca, ga, sb, cb, gb = (mod[:, 0], mod[:, 1], mod[:, 2], mod[:, 3], mod[:, 4], mod[:, 5])
    ga = (2 * (ga >= 0) - 1) * jnp.maximum(jnp.abs(ga), 0.25)
    gb = (2 * (gb >= 0) - 1) * jnp.maximum(jnp.abs(gb), 0.25)
    h = _layernorm(x, axis=-1) * (1 + ca) + sa
    x = x + ga * _L0_attn_ref(h, L0_attn_W_qkv, L0_attn_W_o)
    h = _layernorm(x, axis=-1) * (1 + cb) + sb
    x = x + gb * _L0_ffn_ref(h, L0_ffn_Wg, L0_ffn_balance_bias, L0_ffn_W1, L0_ffn_W2)
    return x

_drawn_inputs = setup_inputs


def setup_inputs(seed=0):
    import zlib

    import numpy as np

    out = dict(_drawn_inputs(seed))
    spreads = {'L0_ffn_balance_bias': (0.0, 0.8)}
    factors = {'L0_attn_W_qkv': 3.076,
     'L0_attn_W_o': 2.773,
     'L0_ffn_Wg': 4.448,
     'L0_ffn_W1': 4.239,
     'L0_ffn_W2': 4.152}
    for name, (base, spread) in spreads.items():
        noise = np.random.default_rng([zlib.crc32(name.encode()), seed]).standard_normal(out[name].shape)
        drawn = base * np.exp(spread * noise) if base else spread * noise
        out[name] = jnp.asarray(drawn.astype(out[name].dtype))
    for name, factor in factors.items():
        out[name] = (out[name] * factor).astype(out[name].dtype)
    return out
```

```python
import concourse.bass as bass
from concourse import mybir
from contextlib import ExitStack

B, L, D, H = 4, 1024, 512, 16
DH = D // H
E, F = 16, 256
P = 128
NT = L // P
TT = B * NT
C = D // P
HG = 4
G = H // HG
QC = 512
NQC = L // QC
EPS = 1e-5
SCALE = 1.0 / float(DH) ** 0.5
PARTS = 3 * DH
MROW = PARTS
ST_TILES = sum(2 * 4 * (qc + 1) for qc in range(NQC))
SLOTS = -(-(2 * B * L + E * (P - 1)) // P)
assert SLOTS % 4 == 0
SA, CA, GA, SB, CB, GB = range(6)


def adaln_block(nc, x, w_qkv_t, w_o_t, wg_t, bal, w1, w2, c_t, w_mod, ident, masks, rope, k_ones,
                e_count, s_count, tok_ids, earlier_t, out):
    f32, f32r, bf16 = mybir.dt.float32, mybir.dt.float32r, mybir.dt.bfloat16
    i32, u32 = mybir.dt.int32, mybir.dt.uint32
    ALU, ACT, AX = mybir.AluOpType, mybir.ActivationFunctionType, mybir.AxisListType
    ds = bass.ds

    mod_dram = nc.dram_tensor("mod_dram", [6, B, D], f32, kind="Internal").ap()
    x1_dram = nc.dram_tensor("x1_dram", [TT, P, D], f32, kind="Internal").ap()
    h2_dram = nc.dram_tensor("h2_dram", [TT * P, D], f32, kind="Internal").ap()
    x_tiles = x.rearrange("b (t p) d -> (b t) p d", p=P)

    ctx = ExitStack()
    with ctx:
        def sem(name):
            return ctx.enter_context(nc.semaphore(name))

        def wait_apart(eng, semaphore, value):
            eng.wait_ge(semaphore, value)
            eng.sem_inc(waited, 1)

        waited = sem("waited")

        def keep(name, shape, dt=f32):
            return ctx.enter_context(nc.sbuf_tensor(name, shape, dt))

        ident_f = keep("ident_f", [P, P])
        logits = keep("logits", [P, TT, E])

        with ExitStack() as part:
            def sb(name, shape, dt=f32):
                return part.enter_context(nc.sbuf_tensor(name, shape, dt))

            w_hi = sb("w_hi", [P, C, G, 384], f32r)
            w_lo = sb("w_lo", [P, C, G, 384], f32r)
            h_hi = sb("h_hi", [P, C, L], f32r)
            h_lo = sb("h_lo", [P, C, L], f32r)
            stack_t = sb("stack_t", [P, 2, HG, L], f32r)
            v_tok = sb("v_tok", [P, NT, HG, DH])
            probs = sb("probs", [P, 2, 2, QC])
            y_t = sb("y_t", [P, G, L])
            w_out = sb("w_out", [P, G, D])
            w_gate = sb("w_gate", [P, C, E])
            trig = sb("trig", [P, 2, NT, DH])
            masks_f = sb("masks_f", [P, 2, P])
            masks_b = sb("masks_b", [P, 2, P], bf16)
            ident_b = sb("ident_b", [P, P], bf16)
            k_ones_sb = sb("k_ones_sb", [P, HG])
            ones = sb("ones", [P, DH])
            neg_half = sb("neg_half", [P, 1])
            mod_b = sb("mod_b", [P, 5, D])
            x_in = sb("x_in", [P, 2, D])
            x_hat = sb("x_hat", [P, 2, D])
            stats = sb("stats", [P, 2, 6])
            mean_var = sb("mean_var", [P, 2, 2])
            rstd = sb("rstd", [P, 2, 2])
            rope_a = sb("rope_a", [P, 2, 256])
            rope_b = sb("rope_b", [P, 2, 256])
            parts_tok = sb("parts_tok", [P, 2, 2, HG, PARTS], f32r)
            neg_max = sb("neg_max", [P, NT, HG])
            neg_max2 = sb("neg_max2", [P, NT // 2, HG])
            max_tok = sb("max_tok", [P, NT, 32])
            max_row = sb("max_row", [P, L])
            r_den = sb("r_den", [P, QC])
            x1 = sb("x1", [P, 2, D])
            h2_t = sb("h2_t", [P, 2, C, P])
            c_sb = sb("c_sb", [P, C, B])
            c_exp = sb("c_exp", [P, C, B])
            c_den = sb("c_den", [P, C, B])

            ring = part.enter_context(nc.psum_tensor("ring", [P, 2, 512], f32))
            pair = part.enter_context(nc.psum_tensor("pair", [P, 2, 2, 512], f32))
            y_ps = part.enter_context(nc.psum_tensor("y_ps", [P, QC], f32))
            den_ps = part.enter_context(nc.psum_tensor("den_ps", [P, QC], f32))

            raw_w = y_t[:, :, :].rearrange("p g l -> p (g l)")[:, 0:2 * 1536].rearrange("p (c n) -> p c n", c=2)
            raw_mod = [probs[:, :, :, :].rearrange("p a b q -> p (a b) q"),
                       mod_b[:, 0:4, :]]
            mod_row = [buf[0:B, k, :] for buf in (x_in, x_hat, x1) for k in range(2)]
            mod_sign, mod_size = r_den[0:B, :], h2_t[0:B, 0, :, :].rearrange("p c n -> p (c n)")

            const_in, gate_in = sem("const_in"), sem("gate_in")
            raw_w_in, w_split_hi, w_split = sem("raw_w_in"), sem("w_split_hi"), sem("w_split")
            raw_mod_in = [sem("raw_mod_in0"), sem("raw_mod_in1")]
            const_ready = sem("const_ready")
            silu_step, mod_ps, mod_step, mod_ready, mod_out = (
                sem("silu_step"), sem("mod_ps"), sem("mod_step"), sem("mod_ready"), sem("mod_out"))

            with nc.Block() as block:
                @block.sync
                def _(sp):
                    for k, (dst, src) in enumerate([(ident_f[:, :], ident), (masks_f[:, :, :], masks),
                                                    (trig[:, :, :, :], rope), (k_ones_sb[:, :], k_ones),
                                                    (w_out[:, :, :], w_o_t), (w_gate[:, :, :], wg_t),
                                                    (c_sb[:, :, :], c_t)]):
                        sp.dma_start(dst, src).then_inc(const_in, 16)
                    for k in range(6):
                        if k >= 2:
                            sp.wait_ge(mod_ps, k - 1)
                        sp.dma_start(raw_mod[k % 2], w_mod[:, :, k, :]).then_inc(raw_mod_in[k % 2], 16)
                    for k in range(6):
                        sp.wait_ge(mod_ready, k + 1)
                        sp.dma_start(mod_dram[k, :, :], mod_row[k]).then_inc(mod_out, 16)
                    sp.wait_ge(mod_out, 96)

                @block.gpsimd
                def _(pool):
                    nc.gpsimd.memset(ones[:, :], 1.0).then_inc(const_ready, 1)
                    nc.gpsimd.memset(neg_half[:, :], -0.5).then_inc(const_ready, 1)
                    for half in range(2):
                        if half:
                            pool.wait_ge(w_split, 1)
                        pool.dma_start(raw_w, w_qkv_t[:, 2 * half:2 * half + 2, :]).then_inc(raw_w_in, 16)
                        pool.wait_ge(w_split_hi, half + 1)
                        dst = slice(2 * half, 2 * half + 2)
                        nc.gpsimd.tensor_tensor(w_lo[:, dst, :, :].rearrange("p c g n -> p c (g n)"), raw_w,
                                                w_hi[:, dst, :, :].rearrange("p c g n -> p c (g n)").bitcast(f32),
                                                ALU.subtract).then_inc(w_split, 1)

                @block.scalar
                def _(act):
                    act.wait_ge(const_in, 112)
                    nc.scalar.activation(c_exp[:, :, :], c_sb[:, :, :], ACT.Exp, scale=-1.0).then_inc(silu_step, 1)
                    for half in range(2):
                        act.wait_ge(raw_w_in, 16 * (half + 1))
                        dst = slice(2 * half, 2 * half + 2)
                        nc.scalar.copy(w_hi[:, dst, :, :].rearrange("p c g n -> p c (g n)"), raw_w)\
                            .then_inc(w_split_hi, 1)

                @block.vector
                def _(dve):
                    nc.vector.memset(max_tok[:, :, :], 0.0).then_inc(const_ready, 1)
                    nc.vector.memset(stack_t[MROW:P, 0, :, :].bitcast(u32), 0).then_inc(const_ready, 1)
                    dve.wait_ge(const_in, 112)
                    nc.vector.tensor_copy(masks_b[:, :, :], masks_f[:, :, :]).then_inc(const_ready, 1)
                    nc.vector.tensor_copy(ident_b[:, :], ident_f[:, :]).then_inc(const_ready, 1)
                    for h in range(HG):
                        nc.vector.tensor_copy(stack_t[MROW:P, 1, h, :],
                                              k_ones_sb[MROW:P, h:h + 1].to_broadcast([P - MROW, L]))\
                            .then_inc(const_ready, 1)
                    dve.wait_ge(silu_step, 1)
                    nc.vector.tensor_scalar_add(c_den[:, :, :], c_exp[:, :, :], 1.0).then_inc(silu_step, 1)
                    dve.wait_ge(silu_step, 2)
                    nc.vector.reciprocal(c_exp[:, :, :], c_den[:, :, :]).then_inc(silu_step, 1)
                    dve.wait_ge(silu_step, 3)
                    nc.vector.tensor_tensor(c_den[:, :, :], c_exp[:, :, :], c_sb[:, :, :], ALU.mult)\
                        .then_inc(silu_step, 1)
                    step = 0
                    for k in range(6):
                        dve.wait_ge(mod_ps, k + 1)
                        row, ps = mod_row[k], ring[0:B, k % 2, :]
                        if k in (CA, CB):
                            nc.vector.tensor_scalar_add(row, ps, 1.0).then_inc(mod_ready, 1)
                        elif k in (SA, SB):
                            nc.vector.tensor_copy(row, ps).then_inc(mod_ready, 1)
                        else:
                            if step:
                                dve.wait_ge(mod_ready, k)
                            sign, size = mod_sign, mod_size
                            nc.vector.tensor_scalar(sign, ps, 0.0, 2.0, ALU.is_ge, ALU.mult).then_inc(mod_step, 1)
                            nc.vector.tensor_scalar(size, ps, -1.0, None, ALU.mult).then_inc(mod_step, 1)
                            step += 2
                            dve.wait_ge(mod_step, step)
                            nc.vector.scalar_tensor_tensor(out=size, in0=size, scalar=0.25, in1=ps,
                                                           op0=ALU.max, op1=ALU.max).then_inc(mod_step, 1)
                            step += 1
                            dve.wait_ge(mod_step, step)
                            nc.vector.scalar_tensor_tensor(out=row, in0=sign, scalar=-1.0, in1=size,
                                                           op0=ALU.add, op1=ALU.mult).then_inc(mod_ready, 1)

                @block.tensor
                def _(pe):
                    pe.wait_ge(silu_step, 4)
                    for k in range(6):
                        pe.wait_ge(raw_mod_in[k % 2], 16 * (k // 2 + 1))
                        if k >= 2:
                            pe.wait_ge(mod_ready, k - 1)
                        for c in range(C):
                            mm = nc.tensor.matmul(ring[0:B, k % 2, :], c_den[:, c, :], raw_mod[k % 2][:, c, :],
                                                  start=(c == 0), stop=(c == C - 1))
                        mm.then_inc(mod_ps, 1)

            PRIMED = 1
            mod_in = sem("mod_in")
            x_in_s = [sem("x_in0"), sem("x_in1")]
            stat_step, rstd_step, rstd_ready = sem("stat_step"), sem("rstd_step"), sem("rstd_ready")
            stat_ready, x_hat_ready, x_hat_scaled, h_ready = (
                sem("stat_ready"), sem("x_hat_ready"), sem("x_hat_scaled"), sem("h_ready"))
            ht_ps, ht_hi, ht_lo = sem("ht_ps"), sem("ht_hi"), sem("ht_lo")
            qkv_ps, rope_terms, v_ready = sem("qkv_ps"), sem("rope_terms"), sem("v_ready")
            roped, hi_ready, parts_ready = sem("roped"), sem("hi_ready"), sem("parts_ready")
            stack_ps, stack_ready = sem("stack_ps"), sem("stack_ready")
            s_ps, s_read, max_step, max_cols, max_rows, max_in = (
                sem("s_ps"), sem("s_read"), sem("max_step"), sem("max_cols"), sem("max_rows"), sem("max_in"))
            st_ps, exp_ready, pv_done, den_step, y_ready = (
                sem("st_ps"), sem("exp_ready"), sem("pv_done"), sem("den_step"), sem("y_ready"))
            o_ps, o_gated, x1_ready = sem("o_ps"), sem("o_gated"), sem("x1_ready")
            res_in = [sem("res_in0"), sem("res_in1")]
            stat2_step, stat2_ready, rstd2_step, rstd2_ready = (
                sem("stat2_step"), sem("stat2_ready"), sem("rstd2_step"), sem("rstd2_ready"))
            x_hat2, x_hat2_scaled, h2_ready = sem("x_hat2"), sem("x_hat2_scaled"), sem("h2_ready")
            h2t_ps, h2t_ready, logit_ps, logit_ready = (
                sem("h2t_ps"), sem("h2t_ready"), sem("logit_ps"), sem("logit_ready"))
            x1_out = [sem("x1_out0"), sem("x1_out1")]
            h2_out = [sem("h2_out0"), sem("h2_out1")]

            MAXES = [(h, qt, kc) for h in range(HG) for qt in range(NT) for kc in range(qt // 4 + 1)]
            NM = len(MAXES)
            PAIRS = [(qc, kt, hp) for qc in range(NQC) for kt in range(4 * (qc + 1)) for hp in range(2)]
            NP = len(PAIRS)

            with nc.Block() as block:
                @block.sync
                def _(sp):
                    for primed in (max_in, *x1_out, *h2_out):
                        sp.sem_inc(primed, PRIMED)
                    with sp.Fori(0, B) as b:
                        sp.wait_ge(h2_ready, PRIMED + b * NT)
                        for k in range(5):
                            sp.dma_start(mod_b[:, k, :], mod_dram[k, ds(b, 1), :].to_broadcast([P, D]))\
                                .then_inc(mod_in, 16)
                        for t in range(NT):
                            if t >= 2:
                                sp.wait_ge(x_hat_ready, b * NT + t - 1)
                            sp.dma_start(x_in[:, t % 2, :], x_tiles[ds(b * NT + t, 1), :, :].squeeze(0))\
                                .then_inc(x_in_s[t % 2], 16)
                        with sp.Fori(0, G) as g:
                            sp.wait_ge(max_rows, 4 * (b * G + g) + 4)
                            sp.dma_start(stack_t[MROW:MROW + 2 * HG, 0, :, :].bitcast(f32),
                                         max_row[MROW:MROW + 2 * HG, :].unsqueeze(1).to_broadcast([2 * HG, HG, L]))\
                                .then_inc(max_in, 16)
                        for t in range(NT + 2):
                            if t < NT:
                                if t < 2:
                                    sp.wait_ge(x_hat_ready, b * NT + NT)
                                else:
                                    sp.wait_ge(x1_ready, PRIMED + b * NT + t - 1)
                                sp.dma_start(x_in[:, t % 2, :], x_tiles[ds(b * NT + t, 1), :, :].squeeze(0))\
                                    .then_inc(res_in[t % 2], 16)
                            if t >= 2:
                                u = t - 2
                                sp.wait_ge(x1_ready, PRIMED + b * NT + u + 1)
                                sp.dma_start(x1_dram[ds(b * NT + u, 1), :, :].squeeze(0), x1[:, u % 2, :])\
                                    .then_inc(x1_out[u % 2], 16)
                                sp.wait_ge(h2_ready, PRIMED + b * NT + u + 1)
                                sp.dma_start(h2_dram[ds((b * NT + u) * P, P), :], x_hat[:, u % 2, :])\
                                    .then_inc(h2_out[u % 2], 16)
                    for k in range(2):
                        sp.wait_ge(x1_out[k], PRIMED + 16 * (TT // 2))
                        sp.wait_ge(h2_out[k], PRIMED + 16 * (TT // 2))

                @block.vector
                def _(dve):
                    for primed in (x1_ready, s_read, y_ready):
                        dve.sem_inc(primed, PRIMED)
                    with dve.Fori(0, B) as b:
                        def statistics(t):
                            if t >= 2:
                                dve.wait_ge(rstd_ready, b * NT + t - 1)
                                dve.wait_ge(x_hat_ready, b * NT + t - 1)
                            dve.wait_ge(x_in_s[t % 2], 16 * (b * (NT // 2) + t // 2 + 1))
                            nc.vector.bn_stats(stats[:, t % 2, :], x_in[:, t % 2, :]).then_inc(stat_step, 1)
                            wait_apart(dve, stat_step, b * NT + t + 1)
                            nc.vector.bn_aggr(mean_var[:, t % 2, :], stats[:, t % 2, :]).then_inc(stat_ready, 1)

                        def low_part(t):
                            dve.wait_ge(ht_hi, b * NT + t + 1)
                            cols = slice(t * P, t * P + P)
                            nc.vector.tensor_tensor(h_lo[:, :, cols], ring[:, t % 2, :].rearrange("p (c n) -> p c n", c=C),
                                                    h_hi[:, :, cols].bitcast(f32), ALU.subtract).then_inc(ht_lo, 1)

                        statistics(0)
                        for t in range(NT):
                            if t + 1 < NT:
                                statistics(t + 1)
                            dve.wait_ge(rstd_ready, b * NT + t + 1)
                            if t >= 2:
                                dve.wait_ge(ht_ps, b * NT + t - 1)
                            nc.vector.tensor_scalar(x_hat[:, t % 2, :], x_in[:, t % 2, :], mean_var[:, t % 2, 0:1],
                                                    rstd[:, t % 2, 1:2], ALU.subtract, ALU.mult)\
                                .then_inc(x_hat_ready, 1)
                            if t >= 1:
                                low_part(t - 1)
                        low_part(NT - 1)

                        with dve.Fori(0, G) as g:
                            i = dve.snap(b * G + g)
                            for t in range(NT):
                                dve.wait_ge(qkv_ps, i * NT + t + 1)
                                if t >= 2:
                                    dve.wait_ge(parts_ready, 2 * (i * NT + t - 1))
                                qk = ring[:, t % 2, 0:256]
                                nc.vector.tensor_tensor(rope_a[:, t % 2, :].rearrange("p (h d) -> p h d", d=DH),
                                                        qk.rearrange("p (h d) -> p h d", d=DH),
                                                        trig[:, 0, t, :].unsqueeze(1).to_broadcast([P, 2 * HG, DH]),
                                                        ALU.mult).then_inc(rope_terms, 1)
                                for half in range(2):
                                    lo, src = 16 * half, 16 * (1 - half)
                                    nc.vector.tensor_tensor(
                                        rope_b[:, t % 2, :].rearrange("p (h d) -> p h d", d=DH)[:, :, lo:lo + 16],
                                        qk.rearrange("p (h d) -> p h d", d=DH)[:, :, src:src + 16],
                                        trig[:, 1, t, lo:lo + 16].unsqueeze(1).to_broadcast([P, 2 * HG, 16]),
                                        ALU.mult).then_inc(rope_terms, 1)
                            for u, (h, qt, kc) in enumerate(MAXES):
                                width = min((qt + 1) * P - kc * 512, 512)
                                dst = neg_max2[:, qt - 4, h:h + 1] if kc else neg_max[:, qt, h:h + 1]
                                dve.wait_ge(s_ps, i * NM + u + 1)
                                nc.vector.tensor_reduce(dst, ring[:, u % 2, 0:width], AX.X, ALU.max, negate=True)\
                                    .then_inc(s_read, 1)
                            dve.wait_ge(s_read, PRIMED + i * NM + NM)
                            nc.vector.tensor_tensor(neg_max[:, NT // 2:NT, :], neg_max[:, NT // 2:NT, :],
                                                    neg_max2[:, :, :], ALU.min).then_inc(max_step, 1)
                            dve.wait_ge(max_step, 3 * i + 1)
                            nc.vector.tensor_copy(max_tok[:, :, 0:2 * HG:2].bitcast(f32r), neg_max[:, :, :]).then_inc(max_step, 1)
                            dve.wait_ge(max_step, 3 * i + 2)
                            nc.vector.tensor_tensor(max_tok[:, :, 1:2 * HG:2], neg_max[:, :, :],
                                                    max_tok[:, :, 0:2 * HG:2], ALU.subtract)\
                                .then_inc(max_step, 1)
                            dve.wait_ge(max_step, 3 * i + 3)
                            dve.wait_ge(max_in, PRIMED + 16 * i)
                            for q in range(4):
                                nc.vector.transpose(
                                    max_row[MROW:P, :].rearrange("p (t q n) -> p t q n", q=4, n=32)[:, :, q, :],
                                    max_tok[32 * q:32 * q + 32, :, :]).then_inc(max_rows, 1)
                            for qc in range(NQC):
                                last = sum(1 for p in PAIRS if p[0] <= qc)
                                dve.wait_ge(pv_done, i * NP + last)
                                for k in range(2):
                                    nc.vector.reciprocal(r_den[64 * k:64 * k + 64, :],
                                                         den_ps[64 - 64 * k:128 - 64 * k, :]).then_inc(den_step, 1)
                                dve.wait_ge(den_step, i * 2 * NQC + 2 * qc + 2)
                                nc.vector.tensor_tensor(y_t[:, ds(g, 1), qc * QC:(qc + 1) * QC].squeeze(1), y_ps[:, :],
                                                        r_den[:, :], ALU.mult).then_inc(y_ready, 1)

                        def residual(t):
                            dve.wait_ge(o_ps, b * NT + t + 1)
                            if t >= 2:
                                dve.wait_ge(x1_out[t % 2], PRIMED + 16 * (b * (NT // 2) + t // 2))
                                dve.wait_ge(x_hat2, b * NT + t - 1)
                            else:
                                dve.wait_ge(x1_out[t % 2], PRIMED + 16 * (b * (NT // 2)))
                            nc.vector.tensor_tensor(x1[:, t % 2, :], ring[:, t % 2, :], mod_b[:, GA, :], ALU.mult)\
                                .then_inc(o_gated, 1)
                            dve.wait_ge(res_in[t % 2], 16 * (b * (NT // 2) + t // 2 + 1))
                            dve.wait_ge(o_gated, b * NT + t + 1)
                            nc.vector.tensor_tensor(x1[:, t % 2, :], x1[:, t % 2, :], x_in[:, t % 2, :], ALU.add)\
                                .then_inc(x1_ready, 1)
                            dve.wait_ge(x1_ready, PRIMED + b * NT + t + 1)
                            if t >= 2:
                                dve.wait_ge(rstd2_ready, b * NT + t - 1)
                            nc.vector.bn_stats(stats[:, t % 2, :], x1[:, t % 2, :]).then_inc(stat2_step, 1)
                            wait_apart(dve, stat2_step, b * NT + t + 1)
                            nc.vector.bn_aggr(mean_var[:, t % 2, :], stats[:, t % 2, :]).then_inc(stat2_ready, 1)

                        residual(0)
                        for t in range(NT):
                            if t + 1 < NT:
                                residual(t + 1)
                            dve.wait_ge(rstd2_ready, b * NT + t + 1)
                            if t >= 2:
                                dve.wait_ge(h2_out[t % 2], PRIMED + 16 * (b * (NT // 2) + t // 2))
                                dve.wait_ge(h2t_ps, b * NT + t - 1)
                            nc.vector.tensor_scalar(x_hat[:, t % 2, :], x1[:, t % 2, :], mean_var[:, t % 2, 0:1],
                                                    rstd[:, t % 2, 1:2], ALU.subtract, ALU.mult)\
                                .then_inc(x_hat2, 1)
                        for k in range(2):
                            dve.wait_ge(h2_out[k], PRIMED + 16 * (b + 1) * (NT // 2))
                        dve.wait_ge(h2t_ps, b * NT + NT)

                @block.gpsimd
                def _(pool):
                    pool.sem_inc(h2_ready, PRIMED)
                    with pool.Fori(0, B) as b:
                        pool.wait_ge(mod_in, 80 * b + 80)

                        def inverse_deviation(t, got, step, done):
                            wait_apart(pool, got, b * NT + t + 1)
                            nc.gpsimd.tensor_scalar(rstd[:, t % 2, 0:1], mean_var[:, t % 2, 1:2], EPS, None, ALU.add)\
                                .then_inc(step, 1)
                            pool.wait_ge(step, b * NT + t + 1)
                            nc.gpsimd.tensor_tensor(rstd[:, t % 2, 1:2], rstd[:, t % 2, 0:1], neg_half[:, :], ALU.pow)\
                                .then_inc(done, 1)

                        def modulate(t, got, factor, shift, step, done):
                            pool.wait_ge(got, b * NT + t + 1)
                            nc.gpsimd.tensor_tensor(x_hat[:, t % 2, :], x_hat[:, t % 2, :], mod_b[:, factor, :],
                                                    ALU.mult).then_inc(step, 1)
                            pool.wait_ge(step, b * NT + t + 1)
                            nc.gpsimd.tensor_tensor(x_hat[:, t % 2, :], x_hat[:, t % 2, :], mod_b[:, shift, :],
                                                    ALU.add).then_inc(done, 1)

                        inverse_deviation(0, stat_ready, rstd_step, rstd_ready)
                        for t in range(NT):
                            if t + 1 < NT:
                                inverse_deviation(t + 1, stat_ready, rstd_step, rstd_ready)
                            modulate(t, x_hat_ready, CA, SA, x_hat_scaled, h_ready)

                        with pool.Fori(0, G) as g:
                            i = pool.snap(b * G + g)
                            for t in range(NT):
                                qk = rope_a[:, t % 2, :].rearrange("p (s h d) -> p s h d", s=2, d=DH)
                                out_q = parts_tok[:, t % 2, 0, :, :].rearrange("p h (s d) -> p h s d", d=DH)
                                out_k = parts_tok[:, t % 2, 1, :, :].rearrange("p h (s d) -> p h s d", d=DH)
                                pool.wait_ge(rope_terms, 3 * (i * NT + t + 1))
                                nc.gpsimd.tensor_tensor(rope_a[:, t % 2, :], rope_a[:, t % 2, :], rope_b[:, t % 2, :],
                                                        ALU.add).then_inc(roped, 1)
                                wait_apart(pool, roped, i * NT + t + 1)
                                if t >= 2:
                                    wait_apart(pool, stack_ps, i * NT + t - 1)
                                nc.gpsimd.tensor_copy(out_q[:, :, 0:2, :],
                                                      qk[:, 0, :, :].unsqueeze(2).to_broadcast([P, HG, 2, DH]))\
                                    .then_inc(hi_ready, 1)
                                nc.gpsimd.tensor_copy(out_k[:, :, 0:3:2, :],
                                                      qk[:, 1, :, :].unsqueeze(2).to_broadcast([P, HG, 2, DH]))\
                                    .then_inc(hi_ready, 1)
                                pool.wait_ge(hi_ready, 2 * (i * NT + t + 1))
                                nc.gpsimd.tensor_tensor(out_q[:, :, 2, :], qk[:, 0, :, :],
                                                        out_q[:, :, 0, :].bitcast(f32), ALU.subtract)\
                                    .then_inc(parts_ready, 1)
                                nc.gpsimd.tensor_tensor(out_k[:, :, 1, :], qk[:, 1, :, :],
                                                        out_k[:, :, 0, :].bitcast(f32), ALU.subtract)\
                                    .then_inc(parts_ready, 1)

                        inverse_deviation(0, stat2_ready, rstd2_step, rstd2_ready)
                        for t in range(NT):
                            if t + 1 < NT:
                                inverse_deviation(t + 1, stat2_ready, rstd2_step, rstd2_ready)
                            modulate(t, x_hat2, CB - 0, SB, x_hat2_scaled, h2_ready)

                @block.scalar
                def _(act):
                    for primed in (exp_ready, logit_ready):
                        act.sem_inc(primed, PRIMED)
                    with act.Fori(0, B) as b:
                        for t in range(NT):
                            act.wait_ge(ht_ps, b * NT + t + 1)
                            nc.scalar.copy(h_hi[:, :, t * P:t * P + P],
                                           ring[:, t % 2, :].rearrange("p (c n) -> p c n", c=C)).then_inc(ht_hi, 1)
                        with act.Fori(0, G) as g:
                            i = act.snap(b * G + g)
                            for t in range(NT + 1):
                                if t < NT:
                                    act.wait_ge(qkv_ps, i * NT + t + 1)
                                    act.wait_ge(rope_terms, 3 * (i * NT + t + 1))
                                    nc.scalar.copy(v_tok[:, t, :, :].rearrange("p h d -> p (h d)"),
                                                   ring[:, t % 2, 256:384]).then_inc(v_ready, 1)
                                if t >= 1:
                                    u = t - 1
                                    act.wait_ge(stack_ps, i * NT + u + 1)
                                    nc.scalar.copy(stack_t[0:PARTS, :, :, u * P:u * P + P],
                                                   pair[0:PARTS, u % 2, :, :].rearrange("p s (h n) -> p s h n", h=HG))\
                                        .then_inc(stack_ready, 1)
                            for n, (qc, kt, hp) in enumerate(PAIRS):
                                q0 = max(0, kt * P - qc * QC)
                                act.wait_ge(st_ps, i * NP + n + 1)
                                if n >= 2:
                                    act.wait_ge(pv_done, i * NP + n - 1)
                                nc.scalar.activation(probs[:, n % 2, :, q0:QC], pair[:, n % 2, :, q0:QC], ACT.Exp,
                                                     scale=SCALE).then_inc(exp_ready, 1)
                        for t in range(NT + 1):
                            if t < NT:
                                act.wait_ge(h2t_ps, b * NT + t + 1)
                                if t >= 2:
                                    act.wait_ge(logit_ps, b * NT + t - 1)
                                nc.scalar.copy(h2_t[:, t % 2, :, :].rearrange("p c n -> p (c n)"),
                                               pair[:, t % 2, 0, :]).then_inc(h2t_ready, 1)
                            if t >= 1:
                                u = t - 1
                                act.wait_ge(logit_ps, b * NT + u + 1)
                                nc.scalar.copy(logits[:, ds(b * NT + u, 1), :].squeeze(1), pair[:, u % 2, 1, 0:E])\
                                    .then_inc(logit_ready, 1)

                @block.tensor
                def _(pe):
                    with pe.Fori(0, B) as b:
                        for t in range(NT):
                            pe.wait_ge(h_ready, b * NT + t + 1)
                            if t >= 2:
                                pe.wait_ge(ht_lo, b * NT + t - 1)
                            elif t == 0:
                                pe.wait_ge(x1_ready, PRIMED + b * NT)
                            for c in range(C):
                                mm = nc.tensor.transpose(ring[:, t % 2, c * P:c * P + P],
                                                         x_hat[:, t % 2, c * P:c * P + P], ident_f[:, :])
                            mm.then_inc(ht_ps, 1)
                        with pe.Fori(0, G) as g:
                            i = pe.snap(b * G + g)
                            pe.wait_ge(ht_lo, b * NT + NT)
                            w_hi_g = w_hi[:, :, ds(g, 1), :]
                            w_lo_g = w_lo[:, :, ds(g, 1), :]
                            for t in range(NT + 2):
                                if t < NT:
                                    if t >= 2:
                                        pe.wait_ge(v_ready, i * NT + t - 1)
                                    elif t == 0:
                                        pe.wait_ge(s_read, PRIMED + i * NM)
                                    cols = slice(t * P, t * P + P)
                                    n = 0
                                    for c in range(C):
                                        for lhs, rhs in ((h_hi, w_hi_g), (h_hi, w_lo_g), (h_lo, w_hi_g)):
                                            mm = nc.tensor.matmul(ring[:, t % 2, 0:384], lhs[:, c, cols],
                                                                  rhs[:, c, :, :].squeeze(1),
                                                                  start=(n == 0), stop=(n == 3 * C - 1))
                                            n += 1
                                    mm.then_inc(qkv_ps, 1)
                                if t >= 2:
                                    u = t - 2
                                    pe.wait_ge(parts_ready, 2 * (i * NT + u + 1))
                                    if u >= 2:
                                        pe.wait_ge(stack_ready, i * NT + u - 1)
                                    elif u == 0:
                                        pe.wait_ge(exp_ready, PRIMED + i * NP)
                                        pe.wait_ge(logit_ready, PRIMED + b * NT)
                                    for s in range(2):
                                        for h in range(HG):
                                            mm = nc.tensor.transpose(pair[0:PARTS, u % 2, s, h * P:h * P + P],
                                                                     parts_tok[:, u % 2, s, h, :].bitcast(f32),
                                                                     ident_f[:, :])
                                    mm.then_inc(stack_ps, 1)
                            pe.wait_ge(stack_ready, i * NT + NT)
                            pe.wait_ge(v_ready, i * NT + NT)
                            for u, (h, qt, kc) in enumerate(MAXES):
                                width = min((qt + 1) * P - kc * 512, 512)
                                diagonal = kc == qt // 4
                                if u >= 2:
                                    pe.wait_ge(s_read, PRIMED + i * NM + u - 1)
                                mm = nc.tensor.matmul(ring[:, u % 2, 0:width], stack_t[0:PARTS, 0, h, qt * P:qt * P + P],
                                                      stack_t[0:PARTS, 1, h, kc * 512:kc * 512 + width],
                                                      start=True, stop=not diagonal)
                                if diagonal:
                                    mm = nc.tensor.matmul(ring[:, u % 2, width - P:width], ident_b[:, :],
                                                          masks_b[:, 0, :], start=False, stop=True)
                                mm.then_inc(s_ps, 1)
                            pe.wait_ge(max_in, PRIMED + 16 * i + 16)

                            def values(n):
                                qc, kt, hp = PAIRS[n]
                                q0 = max(0, kt * P - qc * QC)
                                first, last = kt == 0, kt == 4 * qc + 3
                                pe.wait_ge(exp_ready, PRIMED + i * NP + n + 1)
                                if kt == 0 and hp == 0:
                                    pe.wait_ge(y_ready, PRIMED + i * NQC + qc)
                                for j in range(2):
                                    at = 32 * (2 * hp + j)
                                    nc.tensor.matmul(y_ps[at:at + 32, q0:QC], v_tok[:, kt, 2 * hp + j, :],
                                                     probs[:, n % 2, j, q0:QC], start=first, stop=last)
                                for j in range(2):
                                    at = (32 * (2 * hp + j) + 64) % P
                                    mm = nc.tensor.matmul(den_ps[at:at + 32, q0:QC], ones[:, :],
                                                          probs[:, n % 2, j, q0:QC], start=first, stop=last)
                                mm.then_inc(pv_done, 1)

                            for n, (qc, kt, hp) in enumerate(PAIRS):
                                q0 = max(0, kt * P - qc * QC)
                                diagonal = kt * P >= qc * QC
                                if n >= 2:
                                    pe.wait_ge(exp_ready, PRIMED + i * NP + n - 1)
                                for j in range(2):
                                    h = 2 * hp + j
                                    mm = nc.tensor.matmul(pair[:, n % 2, j, q0:QC], stack_t[:, 1, h, kt * P:kt * P + P],
                                                          stack_t[:, 0, h, qc * QC + q0:(qc + 1) * QC],
                                                          start=True, stop=not diagonal)
                                    if diagonal:
                                        mm = nc.tensor.matmul(pair[:, n % 2, j, q0:q0 + P], ident_b[:, :],
                                                              masks_b[:, 1, :], start=False, stop=True)
                                mm.then_inc(st_ps, 1)
                                if n >= 1:
                                    values(n - 1)
                            values(NP - 1)

                        pe.wait_ge(y_ready, PRIMED + (b + 1) * G * NQC)

                        def logits_of(t):
                            pe.wait_ge(h2t_ready, b * NT + t + 1)
                            if t >= 2:
                                pe.wait_ge(logit_ready, PRIMED + b * NT + t - 1)
                            for c in range(C):
                                mm = nc.tensor.matmul(pair[:, t % 2, 1, 0:E], h2_t[:, t % 2, c, :], w_gate[:, c, :],
                                                      start=(c == 0), stop=(c == C - 1))
                            mm.then_inc(logit_ps, 1)

                        for t in range(NT + 3):
                            if t < NT:
                                if t >= 2:
                                    pe.wait_ge(o_gated, b * NT + t - 1)
                                for g in range(G):
                                    mm = nc.tensor.matmul(ring[:, t % 2, :], y_t[:, g, t * P:t * P + P], w_out[:, g, :],
                                                          start=(g == 0), stop=(g == G - 1))
                                mm.then_inc(o_ps, 1)
                            if 2 <= t < NT + 2:
                                u = t - 2
                                pe.wait_ge(h2_ready, PRIMED + b * NT + u + 1)
                                if u >= 2:
                                    pe.wait_ge(h2t_ready, b * NT + u - 1)
                                for c in range(C):
                                    mm = nc.tensor.transpose(pair[:, u % 2, 0, c * P:c * P + P],
                                                             x_hat[:, u % 2, c * P:c * P + P], ident_f[:, :])
                                mm.then_inc(h2t_ps, 1)
                            if t >= 3:
                                logits_of(t - 3)
        tok_dram = nc.dram_tensor("tok_dram", [P * SLOTS, 1], i32, kind="Internal").ap()
        y_dram = nc.dram_tensor("y_dram", [SLOTS * P, D], f32, kind="Internal").ap()

        with ExitStack() as part:
            def sb(name, shape, dt=f32):
                return part.enter_context(nc.sbuf_tensor(name, shape, dt))

            def ps(name, shape):
                return part.enter_context(nc.psum_tensor(name, shape, f32))

            TE = TT * E
            w1_sb = sb("w1_sb", [P, E, C, F])
            w2_sb = sb("w2_sb", [P, E, F // P, D])
            slot_of = sb("slot_of", [P, TT, 2], i32)
            place_of = sb("place_of", [P, TT, 2], i32)
            weight = sb("weight", [P, TT, 2])
            expert_of = sb("expert_of", [1, SLOTS], i32)
            tokens = sb("tokens", [P, SLOTS], i32)
            gb_b = sb("gb_b", [P, B, D])

            w_in = [sem("w1_in"), sem("w2_in")]
            tab_in, zero_out, zeroed = sem("tab_in"), sem("zero_out"), sem("zeroed")
            r_dve, r_act, r_pe, pos_ready, experts_ready = (
                sem("r_dve"), sem("r_act"), sem("r_pe"), sem("pos_ready"), sem("experts_ready"))
            ids_out, tokens_in, gb_in = sem("ids_out"), sem("tokens_in"), sem("gb_in")

            with ExitStack() as inner:
                def tmp(name, shape, dt=f32):
                    return inner.enter_context(nc.sbuf_tensor(name, shape, dt))

                bal_b = tmp("bal_b", [P, E])
                count_e = tmp("count_e", [P, E])
                count_s = tmp("count_s", [P, SLOTS])
                ids = tmp("ids", [P, TT], i32)
                earlier = tmp("earlier", [P, P])
                all_ones = tmp("all_ones", [P, P])
                restart = tmp("restart", [P, E, TT])
                z = tmp("z", [P, TT, E])
                score = tmp("score", [P, TT, E])
                top = tmp("top", [P, TT, 8])
                top_at = tmp("top_at", [P, TT, 8], u32)
                at_f = tmp("at_f", [P, TT, 2])
                pick = tmp("pick", [P, 2, TT, E])
                both = tmp("both", [P, TT, E])
                upto = tmp("upto", [P, E, TT])
                slot_e = tmp("slot_e", [P, E, TT])
                cnt_i = tmp("cnt_i", [P, E], i32)
                tiles = tmp("tiles", [P, E])
                upto_e = tmp("upto_e", [P, E])
                base = tmp("base", [P, E])
                total = tmp("total", [P, TT])
                slot_f = tmp("slot_f", [P, TT, 2])
                row_i = tmp("row_i", [P, TT, 2], i32)
                row_f = tmp("row_f", [P, TT, 2])
                cmp = tmp("cmp", [1, SLOTS, E])
                exp_f = tmp("exp_f", [1, SLOTS])
                zeros = tmp("zeros", [P, SLOTS], i32)
                before_ps = inner.enter_context(nc.psum_tensor("before_ps", [P, E, TT], f32))
                all_ps = inner.enter_context(nc.psum_tensor("all_ps", [P, E, TT], f32))

                with nc.Block() as block:
                    @block.sync
                    def _(sp):
                        sp.dma_start(bal_b[:, :], bal.to_broadcast([P, E])).then_inc(tab_in, 16)
                        sp.dma_start(count_e[:, :], e_count).then_inc(tab_in, 16)
                        sp.dma_start(count_s[:, :], s_count).then_inc(tab_in, 16)
                        sp.dma_start(ids[:, :], tok_ids).then_inc(tab_in, 16)
                        sp.dma_start(earlier[:, :], earlier_t).then_inc(tab_in, 16)
                        sp.wait_ge(zeroed, 3)
                        sp.dma_start(tok_dram.rearrange("(p s) o -> p (s o)", p=P), zeros[:, :]).then_inc(zero_out, 16)
                        for b in range(B):
                            sp.dma_start(gb_b[:, b, :], mod_dram[GB, b:b + 1, :].to_broadcast([P, D]))\
                                .then_inc(gb_in, 16)
                        sp.wait_ge(ids_out, 16 * 2 * TT)
                        sp.dma_start(tokens[:, :], tok_dram.rearrange("(p s) o -> p (s o)", p=P)).then_inc(tokens_in, 16)
                        sp.wait_ge(tokens_in, 16)
                        sp.wait_ge(gb_in, 16 * B)

                    @block.scalar
                    def _(act):
                        act.dma_start(w1_sb[:, :, :, :], w1).then_inc(w_in[0], 16)
                        act.dma_start(w2_sb[:, :, :, :], w2).then_inc(w_in[1], 16)
                        act.wait_ge(r_dve, 1)
                        nc.scalar.activation(score[:, :, :], z[:, :, :], ACT.Exp, scale=-1.0).then_inc(r_act, 1)

                    @block.tensor
                    def _(pe):
                        pe.wait_ge(r_dve, 11)
                        pe.wait_ge(tab_in, 80)
                        pe.wait_ge(zeroed, 3)
                        nc.tensor.matmul(before_ps[:, :, :], earlier[:, :], both[:, :, :].rearrange("p t e -> p e t"),
                                         start=True, stop=True).then_inc(r_pe, 1)
                        nc.tensor.matmul(all_ps[:, :, :], all_ones[:, :], both[:, :, :].rearrange("p t e -> p e t"),
                                         start=True, stop=True).then_inc(r_pe, 1)

                    @block.gpsimd
                    def _(pool):
                        nc.gpsimd.memset(zeros[:, :], 0).then_inc(zeroed, 1)
                        nc.gpsimd.memset(all_ones[:, :], 1.0).then_inc(zeroed, 1)
                        nc.gpsimd.memset(restart[:, :, :], 1.0).then_inc(zeroed, 1)
                        pool.wait_ge(pos_ready, 1)
                        pool.wait_ge(zero_out, 16)
                        pool.wait_ge(tab_in, 80)
                        for t in range(TT):
                            for k in range(2):
                                pool.indirect_dma_start(
                                    out=tok_dram, out_offset=bass.IndirectOffsetOnAxis(ap=place_of[:, t, k:k + 1], axis=0),
                                    in_=ids[:, t:t + 1], in_offset=None).then_inc(ids_out, 16)

                    @block.vector
                    def _(dve):
                        step = [0]

                        def done(instruction):
                            step[0] += 1
                            instruction.then_inc(r_dve, 1)
                            dve.wait_ge(r_dve, step[0])

                        v = nc.vector
                        dve.wait_ge(tab_in, 80)
                        done(v.tensor_tensor(z[:, :, :], logits[:, :, :], bal_b[:, :].unsqueeze(1).to_broadcast([P, TT, E]),
                                             ALU.add))
                        dve.wait_ge(r_act, 1)
                        done(v.tensor_scalar_add(z[:, :, :], score[:, :, :], 1.0))
                        done(v.reciprocal(score[:, :, :], z[:, :, :]))
                        for t in range(TT):
                            last = v.max(top[:, t, :], score[:, t, :])
                        done(last)
                        for t in range(TT):
                            last = v.max_index(top_at[:, t, :], top[:, t, :], score[:, t, :])
                        done(last)
                        done(v.tensor_copy(at_f[:, :, :], top_at[:, :, 0:2]))
                        for k in range(2):
                            last = v.tensor_tensor(pick[:, k, :, :], count_e[:, :].unsqueeze(1).to_broadcast([P, TT, E]),
                                                   at_f[:, :, k:k + 1].to_broadcast([P, TT, E]), ALU.is_equal)
                        done(last)
                        done(v.tensor_tensor(total[:, :], top[:, :, 0], top[:, :, 1], ALU.add))
                        done(v.tensor_scalar_add(total[:, :], total[:, :], 1e-6))
                        done(v.reciprocal(total[:, :], total[:, :]))
                        done(v.tensor_tensor(both[:, :, :], pick[:, 0, :, :], pick[:, 1, :, :], ALU.add))
                        done(v.tensor_tensor(weight[:, :, :], top[:, :, 0:2], total[:, :].unsqueeze(2).to_broadcast([P, TT, 2]),
                                             ALU.mult))
                        dve.wait_ge(zeroed, 3)
                        done(v.memset(restart[:, :, 0:1], 0.0))
                        dve.wait_ge(r_pe, 2)
                        done(v.tensor_tensor_scan(upto[:, :, :].rearrange("p e t -> p (e t)"),
                                                  restart[:, :, :].rearrange("p e t -> p (e t)"),
                                                  all_ps[:, :, :].rearrange("p e t -> p (e t)"), 0.0, ALU.mult, ALU.add))
                        done(v.tensor_scalar_add(cnt_i[:, :], upto[:, :, TT - 1], float(P - 1)))
                        done(v.tensor_scalar(cnt_i[:, :], cnt_i[:, :], 7, None, ALU.arith_shift_right))
                        done(v.tensor_copy(tiles[:, :], cnt_i[:, :]))
                        done(v.tensor_tensor_scan(upto_e[:, :], all_ones[:, 0:E], tiles[:, :], 0.0, ALU.mult, ALU.add))
                        done(v.tensor_tensor(base[:, :], upto_e[:, :], tiles[:, :], ALU.subtract))
                        done(v.tensor_scalar(base[:, :], base[:, :], float(P), None, ALU.mult))
                        done(v.tensor_tensor(upto[:, :, :], upto[:, :, :], all_ps[:, :, :], ALU.subtract))
                        done(v.tensor_tensor(upto[:, :, :], upto[:, :, :], before_ps[:, :, :], ALU.add))
                        done(v.tensor_tensor(slot_e[:, :, :], upto[:, :, :],
                                             base[:, :].unsqueeze(2).to_broadcast([P, E, TT]), ALU.add))
                        for k in range(2):
                            done(v.tensor_tensor(pick[:, k, :, :], pick[:, k, :, :],
                                                 slot_e[:, :, :].rearrange("p e t -> p t e"), ALU.mult))
                            done(v.tensor_reduce(slot_f[:, :, k:k + 1], pick[:, k, :, :], AX.X, ALU.add))
                        done(v.tensor_copy(slot_of[:, :, :], slot_f[:, :, :]))
                        done(v.tensor_scalar(row_i[:, :, :], slot_of[:, :, :], 7, None, ALU.arith_shift_right))
                        done(v.tensor_copy(row_f[:, :, :], row_i[:, :, :]))
                        done(v.tensor_scalar(slot_f[:, :, :], slot_f[:, :, :], float(SLOTS), None, ALU.mult))
                        done(v.scalar_tensor_tensor(out=place_of[:, :, :], in0=row_f[:, :, :], scalar=float(1 - P * SLOTS),
                                                    in1=slot_f[:, :, :], op0=ALU.mult, op1=ALU.add))
                        v.engine_nop().then_inc(pos_ready, 1)
                        done(v.tensor_tensor(cmp[:, :, :], upto_e[0:1, :].unsqueeze(1).to_broadcast([1, SLOTS, E]),
                                             count_s[0:1, :].unsqueeze(2).to_broadcast([1, SLOTS, E]), ALU.is_le))
                        done(v.tensor_reduce(exp_f[:, :].unsqueeze(2), cmp[:, :, :], AX.X, ALU.add))
                        v.tensor_scalar_min(expert_of[:, :], exp_f[:, :], float(E - 1)).then_inc(experts_ready, 1)

            xg = sb("xg", [P, 4, D])
            idx = sb("idx", [P, 4], i32)
            xg_t = sb("xg_t", [P, 2, C, P])
            e_neg = sb("e_neg", [P, 2, F])
            den = sb("den", [P, 2, F])
            hid = sb("hid", [P, 2, F])
            hid_t = sb("hid_t", [P, 2, F // P, P])
            y_sb = sb("y_sb", [P, 4, D])

            idx_ready = sem("idx_ready")
            xg_in = [sem(f"xg_in{k}") for k in range(4)]
            y_out = [sem(f"y_out{k}") for k in range(4)]
            xt_ps_r, xt_read, up_r, exp_r, den_r, rec_r, hid_r, ht_ps_r, ht_read, y_ps_r, y_read = (
                sem(n) for n in ("xt_ps_r", "xt_read", "up_r", "exp_r", "den_r", "rec_r", "hid_r", "ht_ps_r", "ht_read",
                                 "y_ps_r", "y_read"))

            with ExitStack() as inner:
                def ips(name, shape):
                    return inner.enter_context(nc.psum_tensor(name, shape, f32))

                xt_ps = ips("xt_ps", [P, 2, 512])
                up_ps = ips("up_ps", [P, 2, 512])
                ht_ps_ = ips("ht_ps_", [P, 2, 512])
                yo_ps = ips("yo_ps", [P, 2, 512])

                LAST = 3

                def steps(eng, body):
                    for s in range(4):
                        body(s, s, range(s + 1))
                    with eng.Fori(1, SLOTS // 4) as i:
                        s0 = eng.snap(i * 4)
                        for k in range(4):
                            body(s0 + k, k, range(4))
                    for s in range(SLOTS, SLOTS + LAST):
                        body(s, s % 4, range(s - SLOTS + 1, 4))

                with nc.Block() as block:
                    @block.gpsimd
                    def _(pool):
                        def body(s, k, ages):
                            if 0 in ages:
                                if 3 in ages:
                                    wait_apart(pool, xt_ps_r, s - 3)
                                nc.gpsimd.tensor_copy(idx[:, k:k + 1], tokens[:, ds(s, 1)]).then_inc(idx_ready, 1)
                                wait_apart(pool, idx_ready, s + 1)
                                pool.indirect_dma_start(
                                    out=xg[:, k, :], out_offset=None, in_=h2_dram,
                                    in_offset=bass.IndirectOffsetOnAxis(ap=idx[:, k:k + 1], axis=0))\
                                    .then_inc(xg_in[k], 16)
                        steps(pool, body)

                    @block.tensor
                    def _(pe):
                        for k in range(2):
                            pe.wait_ge(w_in[k], 16)

                        def body(s, k, ages):
                            if 0 in ages:
                                pe.wait_ge(xg_in[k], 4 * (s - k) + 16)
                                if 2 in ages:
                                    pe.wait_ge(xt_read, s - 1)
                                for c in range(C):
                                    mm = nc.tensor.transpose(xt_ps[:, k % 2, c * P:c * P + P], xg[:, k, c * P:c * P + P],
                                                             ident_f[:, :])
                                mm.then_inc(xt_ps_r, 1)
                            if 1 in ages:
                                e = pe.value_load(expert_of[0:1, ds(s - 1, 1)], min_val=0, max_val=E - 1)
                                j = (k + 1) % 2
                                pe.wait_ge(xt_read, s)
                                if 3 in ages:
                                    pe.wait_ge(hid_r, s - 2)
                                for c in range(C):
                                    mm = nc.tensor.matmul(up_ps[:, j, 0:F], xg_t[:, j, c, :],
                                                          w1_sb[:, ds(e, 1), c, :].squeeze(1),
                                                          start=(c == 0), stop=(c == C - 1))
                                mm.then_inc(up_r, 1)
                            if 2 in ages:
                                j = k % 2
                                pe.wait_ge(hid_r, s - 1)
                                for c in range(F // P):
                                    mm = nc.tensor.transpose(ht_ps_[:, j, c * P:c * P + P], hid[:, j, c * P:c * P + P],
                                                             ident_f[:, :])
                                mm.then_inc(ht_ps_r, 1)
                            if 3 in ages:
                                e = pe.value_load(expert_of[0:1, ds(s - 3, 1)], min_val=0, max_val=E - 1)
                                j = (k + 1) % 2
                                pe.wait_ge(ht_read, s - 2)
                                pe.wait_ge(y_read, PRIMED + s - 4)
                                for c in range(F // P):
                                    mm = nc.tensor.matmul(yo_ps[:, j, :], hid_t[:, j, c, :],
                                                          w2_sb[:, ds(e, 1), c, :].squeeze(1),
                                                          start=(c == 0), stop=(c == F // P - 1))
                                mm.then_inc(y_ps_r, 1)
                        steps(pe, body)

                    @block.scalar
                    def _(act):
                        def body(s, k, ages):
                            if 0 in ages:
                                j = k % 2
                                act.wait_ge(xt_ps_r, s + 1)
                                if 2 in ages:
                                    act.wait_ge(up_r, s - 1)
                                nc.scalar.copy(xg_t[:, j, :, :].rearrange("p c n -> p (c n)"), xt_ps[:, j, :])\
                                    .then_inc(xt_read, 1)
                            if 1 in ages:
                                j = (k + 1) % 2
                                act.wait_ge(up_r, s)
                                if 3 in ages:
                                    act.wait_ge(den_r, s - 2)
                                nc.scalar.activation(e_neg[:, j, :], up_ps[:, j, 0:F], ACT.Exp, scale=-1.0)\
                                    .then_inc(exp_r, 1)
                            if 2 in ages:
                                j = k % 2
                                act.wait_ge(ht_ps_r, s - 1)
                                if 3 in ages:
                                    act.wait_ge(y_ps_r, PRIMED + s - 4)
                                nc.scalar.copy(hid_t[:, j, :, :].rearrange("p c n -> p (c n)"), ht_ps_[:, j, 0:F])\
                                    .then_inc(ht_read, 1)
                        steps(act, body)

                    @block.vector
                    def _(dve):
                        dve.sem_inc(y_read, PRIMED)

                        def body(s, k, ages):
                            if 1 in ages:
                                j = (k + 1) % 2
                                dve.wait_ge(exp_r, s)
                                nc.vector.tensor_scalar_add(den[:, j, :], e_neg[:, j, :], 1.0).then_inc(den_r, 1)
                                dve.wait_ge(den_r, s)
                                nc.vector.reciprocal(den[:, j, :], den[:, j, :]).then_inc(rec_r, 1)
                                dve.wait_ge(rec_r, s)
                                if 3 in ages:
                                    dve.wait_ge(ht_ps_r, s - 2)
                                nc.vector.tensor_tensor(hid[:, j, :], den[:, j, :], up_ps[:, j, 0:F], ALU.mult)\
                                    .then_inc(hid_r, 1)
                            if 3 in ages:
                                dve.wait_ge(y_ps_r, PRIMED + s - 3)
                                dve.wait_ge(y_out[(k + 1) % 4], PRIMED + 4 * (s - 3 - (k + 1) % 4))
                                nc.vector.tensor_copy(y_sb[:, (k + 1) % 4, :], yo_ps[:, (k + 1) % 2, :])\
                                    .then_inc(y_read, 1)
                        steps(dve, body)

                    @block.sync
                    def _(sp):
                        for k in range(4):
                            sp.sem_inc(y_out[k], PRIMED)
                        with sp.Fori(0, SLOTS // 4) as i:
                            for k in range(4):
                                sp.wait_ge(y_read, PRIMED + i * 4 + k + 1)
                                sp.dma_start(y_dram[ds((i * 4 + k) * P, P), :], y_sb[:, k, :]).then_inc(y_out[k], 16)
                        for k in range(4):
                            sp.wait_ge(y_out[k], PRIMED + 16 * (SLOTS // 4))

            ya = sb("ya", [P, 4, D])
            yb = sb("yb", [P, 4, D])
            xr = sb("xr", [P, 4, D])
            res = sb("res", [P, 4, D])
            yab_in = [[sem(f"y{n}_in{k}") for k in range(4)] for n in "ab"]
            xr_in = [sem(f"xr_in{k}") for k in range(4)]
            out_s = [sem(f"out_s{k}") for k in range(4)]
            m_a, m_b, m_g, m_x = sem("m_a"), sem("m_b"), sem("m_g"), sem("m_x")
            out_tiles = out.rearrange("b (t p) d -> (b t) p d", p=P)

            with nc.Block() as block:
                @block.gpsimd
                def _(pool):
                    for t in range(TT):
                        for n, dst in enumerate((ya, yb)):
                            if t >= 4:
                                pool.wait_ge(m_b, t - 3)
                            pool.indirect_dma_start(
                                out=dst[:, t % 4, :], out_offset=None, in_=y_dram,
                                in_offset=bass.IndirectOffsetOnAxis(ap=slot_of[:, t, n:n + 1], axis=0))\
                                .then_inc(yab_in[n][t % 4], 16)

                @block.sync
                def _(sp):
                    for t in range(TT):
                        if t >= 4:
                            sp.wait_ge(m_x, t - 3)
                        sp.dma_start(xr[:, t % 4, :], x1_dram[t, :, :]).then_inc(xr_in[t % 4], 16)

                @block.scalar
                def _(act):
                    for t in range(TT):
                        act.wait_ge(m_x, t + 1)
                        act.dma_start(out_tiles[t, :, :], res[:, t % 4, :]).then_inc(out_s[t % 4], 16)
                    for k in range(4):
                        act.wait_ge(out_s[k], 16 * (TT // 4))

                @block.vector
                def _(dve):
                    for t in range(TT):
                        k = t % 4
                        dve.wait_ge(yab_in[0][k], 16 * (t // 4 + 1))
                        if t >= 4:
                            dve.wait_ge(out_s[k], 16 * (t // 4))
                        nc.vector.tensor_scalar(res[:, k, :], ya[:, k, :], weight[:, t, 0:1], None, ALU.mult)\
                            .then_inc(m_a, 1)
                        dve.wait_ge(yab_in[1][k], 16 * (t // 4 + 1))
                        dve.wait_ge(m_a, t + 1)
                        nc.vector.scalar_tensor_tensor(out=res[:, k, :], in0=yb[:, k, :], scalar=weight[:, t, 1:2],
                                                       in1=res[:, k, :], op0=ALU.mult, op1=ALU.add).then_inc(m_b, 1)
                        dve.wait_ge(m_b, t + 1)
                        nc.vector.tensor_tensor(res[:, k, :], res[:, k, :], gb_b[:, t // NT, :], ALU.mult)\
                            .then_inc(m_g, 1)
                        dve.wait_ge(m_g, t + 1)
                        dve.wait_ge(xr_in[k], 16 * (t // 4 + 1))
                        nc.vector.tensor_tensor(res[:, k, :], res[:, k, :], xr[:, k, :], ALU.add).then_inc(m_x, 1)


def _constants(np):
    ident = np.eye(P, dtype=np.float32)
    later = np.triu(np.ones((P, P), np.float32), 1) * np.float32(-1e30)
    masks = np.ascontiguousarray(np.stack([later, later.T], 1))
    inv = np.float32(1.0) / np.float32(10000.0) ** (np.arange(0, DH, 2, dtype=np.float32) / np.float32(DH))
    angle = np.arange(L, dtype=np.float32)[:, None] * inv[None, :]
    cos, sin = np.cos(angle), np.sin(angle)
    rope = np.stack([np.concatenate([cos, cos], 1), np.concatenate([-sin, sin], 1)])
    rope = np.ascontiguousarray(rope.reshape(2, NT, P, DH).transpose(2, 0, 1, 3).astype(np.float32))
    k_ones = np.zeros((P, HG), np.float32)
    for h in range(HG):
        k_ones[MROW + 2 * h:MROW + 2 * h + 2, h] = 1.0
    rows = lambda n: np.ascontiguousarray(np.broadcast_to(np.arange(n, dtype=np.float32), (P, n)))
    tok_ids = np.ascontiguousarray(np.arange(TT * P, dtype=np.int32).reshape(TT, P).T)
    earlier = np.triu(np.ones((P, P), np.float32), 1)
    return dict(ident=ident, masks=masks, rope=rope, k_ones=k_ones, e_count=rows(E), s_count=rows(SLOTS),
                tok_ids=tok_ids, earlier_t=earlier)


def _layout(np, i):
    w = i["L0_attn_W_qkv"].reshape(3, G, HG, DH, D)
    even_odd = w.reshape(3, G, HG, DH // 2, 2, D).transpose(0, 1, 2, 4, 3, 5).reshape(3, G, HG, DH, D)
    w = np.concatenate([even_odd[:2], w[2:]], 0).transpose(1, 0, 2, 3, 4).reshape(3 * D, D)
    chunks = lambda a: np.ascontiguousarray(a.reshape(C, P, *a.shape[1:]).transpose(1, 0, *range(2, a.ndim + 1)))
    return dict(
        x=np.ascontiguousarray(i["L0_attn_x"]),
        w_qkv_t=chunks(w.T), w_o_t=chunks(i["L0_attn_W_o"].T), wg_t=chunks(i["L0_ffn_Wg"].T),
        bal=np.ascontiguousarray(i["L0_ffn_balance_bias"].reshape(1, E)),
        w1=np.ascontiguousarray(i["L0_ffn_W1"].reshape(E, C, P, F).transpose(2, 0, 1, 3)),
        w2=np.ascontiguousarray(i["L0_ffn_W2"].reshape(E, F // P, P, D).transpose(2, 0, 1, 3)),
        c_t=chunks(i["L0_c"].T), w_mod=chunks(i["L0_wmod"].reshape(D, 6, D)))


def kernel(**inputs):
    import numpy as _np
    import concourse.bacc as _bacc
    from concourse import mybir as _mybir
    from concourse.bass_utils import run_bass_kernel_spmd as _run

    nc = _bacc.Bacc("TRN2", target_bir_lowering=False, num_devices=1)
    arrays = {**_layout(_np, {k: _np.asarray(v) for k, v in inputs.items()}), **_constants(_np)}
    aps = {name: nc.dram_tensor(name, a.shape, _mybir.dt.from_np(a.dtype), kind="ExternalInput").ap()
           for name, a in arrays.items()}
    out = nc.dram_tensor("out", [B, L, D], _mybir.dt.float32, kind="ExternalOutput").ap()
    adaln_block(nc, **aps, out=out)
    r = _run(nc, [arrays], core_ids=[0])
    return r.results[0]["out"]
```

```python
import concourse.bass as bass
from concourse import mybir
from contextlib import ExitStack

B, L, D, H = 4, 1024, 512, 16
DH = D // H
E, F = 16, 256
P = 128
NT = L // P
TT = B * NT
C = D // P
HG = 4
G = H // HG
QC = 512
NQC = L // QC
EPS = 1e-5
SCALE = 1.0 / float(DH) ** 0.5
PARTS = 3 * DH
MROW = PARTS
ST_TILES = sum(2 * 4 * (qc + 1) for qc in range(NQC))
SLOTS = -(-(2 * B * L + E * (P - 1)) // P)
assert SLOTS % 4 == 0
SA, CA, GA, SB, CB, GB = range(6)


def adaln_block(nc, x, w_qkv_t, w_o_t, wg_t, bal, w1, w2, c_t, w_mod, ident, masks, rope, k_ones,
                e_count, s_count, tok_ids, earlier_t, out):
    f32, f32r, bf16 = mybir.dt.float32, mybir.dt.float32r, mybir.dt.bfloat16
    i32, u32 = mybir.dt.int32, mybir.dt.uint32
    ALU, ACT, AX = mybir.AluOpType, mybir.ActivationFunctionType, mybir.AxisListType
    ds = bass.ds

    mod_dram = nc.dram_tensor("mod_dram", [6, B, D], f32, kind="Internal").ap()
    w_dram = nc.dram_tensor("w_dram", [2, G, P, C, 384], f32, kind="Internal").ap()
    x1_dram = nc.dram_tensor("x1_dram", [TT, P, D], f32, kind="Internal").ap()
    h2_dram = nc.dram_tensor("h2_dram", [TT * P, D], f32, kind="Internal").ap()
    x_tiles = x.rearrange("b (t p) d -> (b t) p d", p=P)

    ctx = ExitStack()
    with ctx:
        def sem(name):
            return ctx.enter_context(nc.semaphore(name))

        def wait_apart(eng, semaphore, value):
            eng.wait_ge(semaphore, value)
            eng.sem_inc(waited, 1)

        waited = sem("waited")

        def keep(name, shape, dt=f32):
            return ctx.enter_context(nc.sbuf_tensor(name, shape, dt))

        ident_f = keep("ident_f", [P, P])
        logits = keep("logits", [P, TT, E])

        with ExitStack() as part:
            def sb(name, shape, dt=f32):
                return part.enter_context(nc.sbuf_tensor(name, shape, dt))

            w_parts = sb("w_parts", [P, 2, 2, C, 384], f32r)
            h_hi = sb("h_hi", [P, C, L], f32r)
            h_lo = sb("h_lo", [P, C, L], f32r)
            stack_t = sb("stack_t", [P, 2, 2, HG, L], f32r)
            v_tok = sb("v_tok", [P, 2, NT, HG, DH])
            probs = sb("probs", [P, 2, 2, QC])
            y_t = sb("y_t", [P, G, L])
            w_out = sb("w_out", [P, G, D])
            w_gate = sb("w_gate", [P, C, E])
            trig = sb("trig", [P, 2, NT, DH])
            masks_f = sb("masks_f", [P, 2, P])
            masks_b = sb("masks_b", [P, 2, P], bf16)
            ident_b = sb("ident_b", [P, P], bf16)
            k_ones_sb = sb("k_ones_sb", [P, HG])
            ones = sb("ones", [P, DH])
            neg_half = sb("neg_half", [P, 1])
            mod_b = sb("mod_b", [P, 5, D])
            x_in = sb("x_in", [P, 2, D])
            x_hat = sb("x_hat", [P, 2, D])
            stats = sb("stats", [P, 2, 6])
            mean_var = sb("mean_var", [P, 2, 2])
            rstd = sb("rstd", [P, 2, 2])
            rope_a, rope_b = x_hat[:, :, 0:256], x_hat[:, :, 256:512]
            parts_tok = sb("parts_tok", [P, 2, 2, HG, PARTS])
            neg_max = sb("neg_max", [P, NT, HG])
            neg_max2 = sb("neg_max2", [P, NT // 2, HG])
            max_tok = sb("max_tok", [P, NT, 32])
            r_den = sb("r_den", [P, QC])
            x1 = sb("x1", [P, 2, D])
            max_row = x1[:, :, :].rearrange("p a d -> p (a d)")
            x_hat_2 = probs[:, 0, :, :]
            h2_t = probs[:, 1, :, :].rearrange("p a (c n) -> p a c n", c=C)
            c_sb = sb("c_sb", [P, C, B])
            c_exp = sb("c_exp", [P, C, B])
            c_den = sb("c_den", [P, C, B])

            ring = part.enter_context(nc.psum_tensor("ring", [P, 2, 512], f32))
            pair = part.enter_context(nc.psum_tensor("pair", [P, 2, 2, 512], f32))
            y_ps = part.enter_context(nc.psum_tensor("y_ps", [P, QC], f32))
            den_ps = part.enter_context(nc.psum_tensor("den_ps", [P, QC], f32))
            o_acc = [y_ps[:, :], den_ps[:, :]]

            raw_w = y_t[:, :, :].rearrange("p g l -> p (g l)")[:, 0:2 * 1536].rearrange("p (c n) -> p c n", c=2)
            w_stage = [stack_t[:, k, :, :, :].rearrange("p s h l -> p (s h l)")[:, 0:C * 1536]
                       .rearrange("p (c n) -> p c n", c=C) for k in range(2)]
            raw_mod = [probs[:, :, :, :].rearrange("p a b q -> p (a b) q"),
                       mod_b[:, 0:4, :]]
            mod_row = [buf[0:B, k, :] for buf in (x_in, x_hat, x1) for k in range(2)]
            mod_sign, mod_size = r_den[0:B, :], parts_tok[0:B, :, :, :, :].rearrange("p a s h d -> p (a s h d)")[:, 0:D]

            const_in, gate_in = sem("const_in"), sem("gate_in")
            raw_w_in, w_split_hi, w_split = sem("raw_w_in"), sem("w_split_hi"), sem("w_split")
            raw_mod_in = [sem("raw_mod_in0"), sem("raw_mod_in1")]
            const_ready, w_out_s = sem("const_ready"), sem("w_out_s")
            silu_step, mod_ps, mod_step, mod_ready, mod_out = (
                sem("silu_step"), sem("mod_ps"), sem("mod_step"), sem("mod_ready"), sem("mod_out"))

            with nc.Block() as block:
                @block.sync
                def _(sp):
                    for k, (dst, src) in enumerate([(ident_f[:, :], ident), (masks_f[:, :, :], masks),
                                                    (trig[:, :, :, :], rope), (k_ones_sb[:, :], k_ones),
                                                    (w_out[:, :, :], w_o_t), (w_gate[:, :, :], wg_t),
                                                    (c_sb[:, :, :], c_t)]):
                        sp.dma_start(dst, src).then_inc(const_in, 16)
                    for k in range(6):
                        if k >= 2:
                            sp.wait_ge(mod_ps, k - 1)
                        sp.dma_start(raw_mod[k % 2], w_mod[:, :, k, :]).then_inc(raw_mod_in[k % 2], 16)
                    for k in range(6):
                        sp.wait_ge(mod_ready, k + 1)
                        sp.dma_start(mod_dram[k, :, :], mod_row[k]).then_inc(mod_out, 16)
                    sp.wait_ge(mod_out, 96)

                @block.gpsimd
                def _(pool):
                    nc.gpsimd.memset(ones[:, :], 1.0).then_inc(const_ready, 1)
                    nc.gpsimd.memset(neg_half[:, :], -0.5).then_inc(const_ready, 1)
                    for half in range(2):
                        if half:
                            pool.wait_ge(w_split, 1)
                        pool.dma_start(raw_w, w_qkv_t[:, 2 * half:2 * half + 2, :]).then_inc(raw_w_in, 16)
                        pool.wait_ge(w_split_hi, half + 1)
                        nc.gpsimd.tensor_tensor(w_stage[1][:, 2 * half:2 * half + 2, :], raw_w,
                                                w_stage[0][:, 2 * half:2 * half + 2, :].bitcast(f32),
                                                ALU.subtract).then_inc(w_split, 1)

                @block.scalar
                def _(act):
                    act.wait_ge(const_in, 112)
                    nc.scalar.activation(c_exp[:, :, :], c_sb[:, :, :], ACT.Exp, scale=-1.0).then_inc(silu_step, 1)
                    for half in range(2):
                        act.wait_ge(raw_w_in, 16 * (half + 1))
                        nc.scalar.copy(w_stage[0][:, 2 * half:2 * half + 2, :], raw_w).then_inc(w_split_hi, 1)
                    act.wait_ge(w_split, 2)
                    for k in range(2):
                        for g in range(G):
                            act.dma_start(w_dram[k, g, :, :, :],
                                          w_stage[k][:, :, 384 * g:384 * g + 384].bitcast(f32)).then_inc(w_out_s, 16)
                    act.wait_ge(w_out_s, 16 * 2 * G)

                @block.vector
                def _(dve):
                    nc.vector.memset(max_tok[:, :, :], 0.0).then_inc(const_ready, 1)
                    dve.wait_ge(const_in, 112)
                    nc.vector.tensor_copy(masks_b[:, :, :], masks_f[:, :, :]).then_inc(const_ready, 1)
                    nc.vector.tensor_copy(ident_b[:, :], ident_f[:, :]).then_inc(const_ready, 1)
                    dve.wait_ge(silu_step, 1)
                    nc.vector.tensor_scalar_add(c_den[:, :, :], c_exp[:, :, :], 1.0).then_inc(silu_step, 1)
                    dve.wait_ge(silu_step, 2)
                    nc.vector.reciprocal(c_exp[:, :, :], c_den[:, :, :]).then_inc(silu_step, 1)
                    dve.wait_ge(silu_step, 3)
                    nc.vector.tensor_tensor(c_den[:, :, :], c_exp[:, :, :], c_sb[:, :, :], ALU.mult)\
                        .then_inc(silu_step, 1)
                    step = 0
                    for k in range(6):
                        dve.wait_ge(mod_ps, k + 1)
                        row, ps = mod_row[k], ring[0:B, k % 2, :]
                        if k in (CA, CB):
                            nc.vector.tensor_scalar_add(row, ps, 1.0).then_inc(mod_ready, 1)
                        elif k in (SA, SB):
                            nc.vector.tensor_copy(row, ps).then_inc(mod_ready, 1)
                        else:
                            if step:
                                dve.wait_ge(mod_ready, k)
                            sign, size = mod_sign, mod_size
                            nc.vector.tensor_scalar(sign, ps, 0.0, 2.0, ALU.is_ge, ALU.mult).then_inc(mod_step, 1)
                            nc.vector.tensor_scalar(size, ps, -1.0, None, ALU.mult).then_inc(mod_step, 1)
                            step += 2
                            dve.wait_ge(mod_step, step)
                            nc.vector.scalar_tensor_tensor(out=size, in0=size, scalar=0.25, in1=ps,
                                                           op0=ALU.max, op1=ALU.max).then_inc(mod_step, 1)
                            step += 1
                            dve.wait_ge(mod_step, step)
                            nc.vector.scalar_tensor_tensor(out=row, in0=sign, scalar=-1.0, in1=size,
                                                           op0=ALU.add, op1=ALU.mult).then_inc(mod_ready, 1)
                    dve.wait_ge(w_out_s, 16 * 2 * G)
                    for parity in range(2):
                        nc.vector.memset(stack_t[MROW:P, parity, 0, :, :].bitcast(u32), 0).then_inc(const_ready, 1)
                    for h in range(HG):
                        for parity in range(2):
                            nc.vector.tensor_copy(stack_t[MROW:P, parity, 1, h, :],
                                                  k_ones_sb[MROW:P, h:h + 1].to_broadcast([P - MROW, L]))\
                                .then_inc(const_ready, 1)

                @block.tensor
                def _(pe):
                    pe.wait_ge(silu_step, 4)
                    for k in range(6):
                        pe.wait_ge(raw_mod_in[k % 2], 16 * (k // 2 + 1))
                        if k >= 2:
                            pe.wait_ge(mod_ready, k - 1)
                        for c in range(C):
                            mm = nc.tensor.matmul(ring[0:B, k % 2, :], c_den[:, c, :], raw_mod[k % 2][:, c, :],
                                                  start=(c == 0), stop=(c == C - 1))
                        mm.then_inc(mod_ps, 1)

            PRIMED = 1
            mod1_in, mod2_in = sem("mod1_in"), sem("mod2_in")
            w_parts_in = [sem("w_parts_in0"), sem("w_parts_in1")]
            x_in_s = [sem("x_in0"), sem("x_in1")]
            stat_step, rstd_step, rstd_ready = sem("stat_step"), sem("rstd_step"), sem("rstd_ready")
            stat_ready, x_hat_ready, x_hat_scaled, h_ready = (
                sem("stat_ready"), sem("x_hat_ready"), sem("x_hat_scaled"), sem("h_ready"))
            ht_ps, ht_hi, ht_lo = sem("ht_ps"), sem("ht_hi"), sem("ht_lo")
            qkv_ps, rope_terms, v_ready = sem("qkv_ps"), sem("rope_terms"), sem("v_ready")
            roped, hi_ready, k_hi_ready, parts_ready = sem("roped"), sem("hi_ready"), sem("k_hi_ready"), sem("parts_ready")
            stack_ps, stack_ready = sem("stack_ps"), sem("stack_ready")
            s_ps, s_read, max_step, max_cols, max_rows, max_in = (
                sem("s_ps"), sem("s_read"), sem("max_step"), sem("max_cols"), sem("max_rows"), sem("max_in"))
            st_ps, exp_ready, pv_done, y_taken, den_step, y_ready = (
                sem("st_ps"), sem("exp_ready"), sem("pv_done"), sem("y_taken"), sem("den_step"), sem("y_ready"))
            o_ps, o_gated, x1_ready = sem("o_ps"), sem("o_gated"), sem("x1_ready")
            res_in = [sem("res_in0"), sem("res_in1")]
            stat2_step, stat2_ready, rstd2_step, rstd2_ready = (
                sem("stat2_step"), sem("stat2_ready"), sem("rstd2_step"), sem("rstd2_ready"))
            x_hat2, x_hat2_scaled, h2_ready = sem("x_hat2"), sem("x_hat2_scaled"), sem("h2_ready")
            h2t_ps, h2t_ready, logit_ps, logit_ready = (
                sem("h2t_ps"), sem("h2t_ready"), sem("logit_ps"), sem("logit_ready"))
            x1_out = [sem("x1_out0"), sem("x1_out1")]
            h2_out = [sem("h2_out0"), sem("h2_out1")]

            MAXES = [(h, qt, kc) for qt in range(NT) for h in range(HG) for kc in range(qt // 4 + 1)]
            NM = len(MAXES)
            PAIRS = [(qc, kt, hp) for qc in range(NQC) for kt in range(4 * (qc + 1)) for hp in range(2)]
            NP = len(PAIRS)
            PROJECT_AT = {t: t for t in range(NT)}
            TURN_AT = {t + 2: t for t in range(NT)}
            FIRST_MAX, LAST_MAX = NT + 2, NP - 3
            MAXES_AT = [range((n - FIRST_MAX) * NM // (LAST_MAX + 1 - FIRST_MAX),
                              (n + 1 - FIRST_MAX) * NM // (LAST_MAX + 1 - FIRST_MAX))
                        if FIRST_MAX <= n <= LAST_MAX else range(0) for n in range(NP)]
            NORM_AT = {3 * t + 1: t for t in range(NT)}

            NORM2_STEPS = NT + 3

            def entries(eng, body):
                with eng.Fori(0, B - 1) as b:
                    body(b, True)
                body(B - 1, False)

            def first_group(eng, b):
                return b * G if isinstance(b, int) else eng.snap(b * G)

            def uses_of(n):
                return (([("stack", 2 * TURN_AT[n])] if n in TURN_AT else [])
                        + ([("qkv", PROJECT_AT[n])] if n in PROJECT_AT else [])
                        + ([("stack", 2 * TURN_AT[n] + 1)] if n in TURN_AT else [])
                        + [("max", u) for u in MAXES_AT[n]])

            RING = [use for n in range(NP) for use in uses_of(n)]
            BANK = {use: k % 2 for k, use in enumerate(RING)}
            assert len(RING) % 2 == 0

            with nc.Block() as block:
                @block.sync
                def _(sp):
                    def load_w(b, g):
                        for k in range(2):
                            sp.dma_start(w_parts[:, g % 2, k, :, :].bitcast(f32), w_dram[k, g, :, :, :])\
                                .then_inc(w_parts_in[g % 2], 16)

                    for primed in (max_in, *x1_out, *h2_out):
                        sp.sem_inc(primed, PRIMED)

                    def load_entry(b, first):
                        if not first:
                            sp.wait_ge(h_ready, b * NT)
                            sp.wait_ge(x1_ready, PRIMED + (b - 1) * NT)
                        for k in (SA, CA):
                            sp.dma_start(mod_b[:, k, :], mod_dram[k, ds(b, 1), :].to_broadcast([P, D]))\
                                .then_inc(mod1_in, 16)
                        for t in range(NT):
                            if t >= 2:
                                sp.wait_ge(x_hat_ready, b * NT + t - 1)
                            sp.dma_start(x_in[:, t % 2, :], x_tiles[ds(b * NT + t, 1), :, :].squeeze(0))\
                                .then_inc(x_in_s[t % 2], 16)

                    load_w(0, 0)
                    load_entry(0, True)

                    def entry(b, more):
                        sp.wait_ge(h2_ready, PRIMED + b * NT)
                        for k in (GA, SB, CB):
                            sp.dma_start(mod_b[:, k, :], mod_dram[k, ds(b, 1), :].to_broadcast([P, D]))\
                                .then_inc(mod2_in, 16)
                        for g in range(G):
                            if g + 1 < G or more:
                                sp.wait_ge(qkv_ps, PRIMED + (b * G + g) * NT)
                                load_w(b, (g + 1) % G)
                            sp.wait_ge(max_rows, 4 * (b * G + g) + 4)
                            sp.dma_start(stack_t[MROW:MROW + 2 * HG, g % 2, 0, :, :].bitcast(f32),
                                         max_row[MROW:MROW + 2 * HG, :].unsqueeze(1).to_broadcast([2 * HG, HG, L]))\
                                .then_inc(max_in, 16)
                        if more:
                            load_entry(b + 1, False)
                        for t in range(NT + 2):
                            if t < NT:
                                if t < 2:
                                    sp.wait_ge(x_hat_ready, (b + 1 + int(more)) * NT)
                                else:
                                    sp.wait_ge(x1_ready, PRIMED + b * NT + t - 1)
                                sp.dma_start(x_in[:, t % 2, :], x_tiles[ds(b * NT + t, 1), :, :].squeeze(0))\
                                    .then_inc(res_in[t % 2], 16)
                            if t >= 2:
                                u = t - 2
                                sp.wait_ge(x1_ready, PRIMED + b * NT + u + 1)
                                sp.dma_start(x1_dram[ds(b * NT + u, 1), :, :].squeeze(0), x1[:, u % 2, :])\
                                    .then_inc(x1_out[u % 2], 16)
                                sp.wait_ge(h2_ready, PRIMED + b * NT + u + 1)
                                sp.dma_start(h2_dram[ds((b * NT + u) * P, P), :], x_hat_2[:, u % 2, :])\
                                    .then_inc(h2_out[u % 2], 16)

                    entries(sp, entry)
                    for k in range(2):
                        sp.wait_ge(x1_out[k], PRIMED + 16 * (TT // 2))
                        sp.wait_ge(h2_out[k], PRIMED + 16 * (TT // 2))

                @block.vector
                def _(dve):
                    for primed in (x1_ready, s_read, y_ready):
                        dve.sem_inc(primed, PRIMED)

                    def first_norm(b, t):
                        def statistics(t):
                            if t >= 2:
                                dve.wait_ge(rstd_ready, b * NT + t - 1)
                                dve.wait_ge(x_hat_ready, b * NT + t - 1)
                            dve.wait_ge(x_in_s[t % 2], 16 * (b * (NT // 2) + t // 2 + 1))
                            nc.vector.bn_stats(stats[:, t % 2, :], x_in[:, t % 2, :]).then_inc(stat_step, 1)
                            wait_apart(dve, stat_step, b * NT + t + 1)
                            nc.vector.bn_aggr(mean_var[:, t % 2, :], stats[:, t % 2, :]).then_inc(stat_ready, 1)

                        def low_part(t):
                            dve.wait_ge(ht_hi, b * NT + t + 1)
                            cols = slice(t * P, t * P + P)
                            nc.vector.tensor_tensor(h_lo[:, :, cols], ring[:, t % 2, :].rearrange("p (c n) -> p c n", c=C),
                                                    h_hi[:, :, cols].bitcast(f32), ALU.subtract).then_inc(ht_lo, 1)

                        if t == 0:
                            statistics(0)
                        if t < NT:
                            if t + 1 < NT:
                                statistics(t + 1)
                            dve.wait_ge(rstd_ready, b * NT + t + 1)
                            if t >= 2:
                                dve.wait_ge(ht_ps, b * NT + t - 1)
                            nc.vector.tensor_scalar(x_hat[:, t % 2, :], x_in[:, t % 2, :], mean_var[:, t % 2, 0:1],
                                                    rstd[:, t % 2, 1:2], ALU.subtract, ALU.mult)\
                                .then_inc(x_hat_ready, 1)
                        if t >= 1:
                            low_part(t - 1)

                    for t in range(NT + 1):
                        first_norm(0, t)

                    def rope(i, t):
                        dve.wait_ge(qkv_ps, PRIMED + i * NT + t + 1)
                        if t >= 2:
                            dve.wait_ge(parts_ready, 2 * (i * NT + t - 1))
                        qk = ring[:, BANK["qkv", t], 0:256].rearrange("p (h d) -> p h d", d=DH)
                        nc.vector.tensor_tensor(rope_a[:, t % 2, :].rearrange("p (h d) -> p h d", d=DH), qk,
                                                trig[:, 0, t, :].unsqueeze(1).to_broadcast([P, 2 * HG, DH]),
                                                ALU.mult).then_inc(rope_terms, 1)
                        for half in range(2):
                            lo, src = 16 * half, 16 * (1 - half)
                            nc.vector.tensor_tensor(
                                rope_b[:, t % 2, :].rearrange("p (h d) -> p h d", d=DH)[:, :, lo:lo + 16],
                                qk[:, :, src:src + 16],
                                trig[:, 1, t, lo:lo + 16].unsqueeze(1).to_broadcast([P, 2 * HG, 16]),
                                ALU.mult).then_inc(rope_terms, 1)

                    def maximum(i, u):
                        h, qt, kc = MAXES[u]
                        width = min((qt + 1) * P - kc * 512, 512)
                        dst = neg_max2[:, qt - 4, h:h + 1] if kc else neg_max[:, qt, h:h + 1]
                        dve.wait_ge(s_ps, i * NM + u + 1)
                        nc.vector.tensor_reduce(dst, ring[:, BANK["max", u], 0:width], AX.X, ALU.max, negate=True)\
                            .then_inc(s_read, 1)

                    def max_to_rows(b, i):
                        dve.wait_ge(s_read, PRIMED + i * NM + NM)
                        nc.vector.tensor_tensor(neg_max[:, NT // 2:NT, :], neg_max[:, NT // 2:NT, :],
                                                neg_max2[:, :, :], ALU.min).then_inc(max_step, 1)
                        dve.wait_ge(max_step, 3 * i + 1)
                        nc.vector.tensor_copy(max_tok[:, :, 0:2 * HG:2].bitcast(f32r), neg_max[:, :, :])\
                            .then_inc(max_step, 1)
                        dve.wait_ge(max_step, 3 * i + 2)
                        nc.vector.tensor_tensor(max_tok[:, :, 1:2 * HG:2], neg_max[:, :, :],
                                                max_tok[:, :, 0:2 * HG:2], ALU.subtract).then_inc(max_step, 1)
                        dve.wait_ge(max_step, 3 * i + 3)
                        dve.wait_ge(max_in, PRIMED + 16 * i)
                        for k in range(2):
                            dve.wait_ge(x1_out[k], PRIMED + 16 * b * (NT // 2))
                        for q in range(4):
                            nc.vector.transpose(
                                max_row[MROW:P, :].rearrange("p (t q n) -> p t q n", q=4, n=32)[:, :, q, :],
                                max_tok[32 * q:32 * q + 32, :, :]).then_inc(max_rows, 1)

                    def normalise(i, g, qc):
                        part_of_y = y_t[:, g, qc * QC:(qc + 1) * QC]
                        dve.wait_ge(y_taken, PRIMED + 3 * (i * NQC + qc + 1))
                        nc.vector.reciprocal(r_den[:, :], r_den[:, :]).then_inc(den_step, 1)
                        dve.wait_ge(den_step, i * NQC + qc + 1)
                        nc.vector.tensor_tensor(part_of_y, part_of_y, r_den[:, :], ALU.mult).then_inc(y_ready, 1)

                    def prepare(b, i, n):
                        for kind, u in uses_of(n):
                            if kind == "qkv":
                                rope(i, u)
                            elif kind == "max":
                                maximum(i, u)
                        if n == LAST_MAX:
                            max_to_rows(b, i)

                    for n in range(NP):
                        prepare(0, 0, n)

                    def entry(b, more):
                        i0 = first_group(dve, b)
                        for g in range(G):
                            for n in range(NP):
                                if g + 1 < G:
                                    prepare(b, i0 + g + 1, n)
                                if n in (NT, NP - 1):
                                    normalise(i0 + g, g, int(n == NP - 1))
                                if g == G - 1 and more and n in NORM_AT:
                                    first_norm(b + 1, NORM_AT[n])
                        if more:
                            first_norm(b + 1, NT)

                        def residual(t):
                            dve.wait_ge(o_ps, b * NT + t + 1)
                            if t >= 2:
                                dve.wait_ge(x1_out[t % 2], PRIMED + 16 * (b * (NT // 2) + t // 2))
                                dve.wait_ge(x_hat2, b * NT + t - 1)
                            else:
                                dve.wait_ge(x1_out[t % 2], PRIMED + 16 * (b * (NT // 2)))
                            nc.vector.tensor_tensor(x1[:, t % 2, :], o_acc[t % 2], mod_b[:, GA, :], ALU.mult)\
                                .then_inc(o_gated, 1)
                            dve.wait_ge(res_in[t % 2], 16 * (b * (NT // 2) + t // 2 + 1))
                            dve.wait_ge(o_gated, b * NT + t + 1)
                            nc.vector.tensor_tensor(x1[:, t % 2, :], x1[:, t % 2, :], x_in[:, t % 2, :], ALU.add)\
                                .then_inc(x1_ready, 1)
                            dve.wait_ge(x1_ready, PRIMED + b * NT + t + 1)
                            if t >= 2:
                                dve.wait_ge(rstd2_ready, b * NT + t - 1)
                            nc.vector.bn_stats(stats[:, t % 2, :], x1[:, t % 2, :]).then_inc(stat2_step, 1)
                            wait_apart(dve, stat2_step, b * NT + t + 1)
                            nc.vector.bn_aggr(mean_var[:, t % 2, :], stats[:, t % 2, :]).then_inc(stat2_ready, 1)

                        dve.wait_ge(mod2_in, 48 * (b + 1))
                        def second_norm(k):
                            if k < NT:
                                residual(k)
                            if not 1 <= k <= NT:
                                return
                            t = k - 1
                            dve.wait_ge(rstd2_ready, b * NT + t + 1)
                            if t >= 2:
                                dve.wait_ge(h2_out[t % 2], PRIMED + 16 * (b * (NT // 2) + t // 2))
                                dve.wait_ge(h2t_ps, b * NT + t - 1)
                            nc.vector.tensor_scalar(x_hat_2[:, t % 2, :], x1[:, t % 2, :], mean_var[:, t % 2, 0:1],
                                                    rstd[:, t % 2, 1:2], ALU.subtract, ALU.mult)\
                                .then_inc(x_hat2, 1)

                        for n in range(NP if more else NORM2_STEPS):
                            if n < NORM2_STEPS:
                                second_norm(n)
                            if more:
                                prepare(b + 1, i0 + G, n)

                    entries(dve, entry)

                @block.gpsimd
                def _(pool):
                    pool.sem_inc(h2_ready, PRIMED)

                    def normalising(b):
                        def inverse_deviation(t, got, step, done):
                            wait_apart(pool, got, b * NT + t + 1)
                            nc.gpsimd.tensor_scalar(rstd[:, t % 2, 0:1], mean_var[:, t % 2, 1:2], EPS, None, ALU.add)\
                                .then_inc(step, 1)
                            pool.wait_ge(step, b * NT + t + 1)
                            nc.gpsimd.tensor_tensor(rstd[:, t % 2, 1:2], rstd[:, t % 2, 0:1], neg_half[:, :], ALU.pow)\
                                .then_inc(done, 1)

                        def modulate(t, normal, got, factor, shift, step, done):
                            pool.wait_ge(got, b * NT + t + 1)
                            nc.gpsimd.tensor_tensor(normal[:, t % 2, :], normal[:, t % 2, :], mod_b[:, factor, :],
                                                    ALU.mult).then_inc(step, 1)
                            pool.wait_ge(step, b * NT + t + 1)
                            nc.gpsimd.tensor_tensor(normal[:, t % 2, :], normal[:, t % 2, :], mod_b[:, shift, :],
                                                    ALU.add).then_inc(done, 1)
                        return inverse_deviation, modulate

                    def first_norm(b):
                        inverse_deviation, modulate = normalising(b)
                        wait_apart(pool, mod1_in, 32 * (b + 1))
                        inverse_deviation(0, stat_ready, rstd_step, rstd_ready)
                        for t in range(NT):
                            if t + 1 < NT:
                                inverse_deviation(t + 1, stat_ready, rstd_step, rstd_ready)
                            modulate(t, x_hat, x_hat_ready, CA, SA, x_hat_scaled, h_ready)

                    def split(i, t):
                        qk = rope_a[:, t % 2, :].rearrange("p (s h d) -> p s h d", s=2, d=DH)
                        out_q = parts_tok[:, t % 2, 0, :, :].rearrange("p h (s d) -> p h s d", d=DH)
                        out_k = parts_tok[:, t % 2, 1, :, :].rearrange("p h (s d) -> p h s d", d=DH)
                        pool.wait_ge(rope_terms, 3 * (i * NT + t + 1))
                        nc.gpsimd.tensor_tensor(rope_a[:, t % 2, :], rope_a[:, t % 2, :], rope_b[:, t % 2, :],
                                                ALU.add).then_inc(roped, 1)
                        wait_apart(pool, roped, i * NT + t + 1)
                        if t >= 2:
                            wait_apart(pool, stack_ps, 2 * (i * NT + t - 1))
                        nc.gpsimd.tensor_copy(out_q[:, :, 0:2, :].bitcast(f32r),
                                              qk[:, 0, :, :].unsqueeze(2).to_broadcast([P, HG, 2, DH]))\
                            .then_inc(hi_ready, 1)
                        pool.wait_ge(hi_ready, i * NT + t + 1)
                        nc.gpsimd.tensor_tensor(out_q[:, :, 2, :], qk[:, 0, :, :],
                                                out_q[:, :, 0, :], ALU.subtract)\
                            .then_inc(parts_ready, 1)
                        pool.wait_ge(k_hi_ready, i * NT + t + 1)
                        nc.gpsimd.tensor_tensor(out_k[:, :, 1, :], qk[:, 1, :, :],
                                                out_k[:, :, 0, :], ALU.subtract)\
                            .then_inc(parts_ready, 1)


                    first_norm(0)
                    for t in range(NT):
                        split(0, t)

                    def entry(b, more):
                        i0 = first_group(pool, b)
                        for g in range(1, G):
                            for t in range(NT):
                                split(i0 + g, t)

                        if more:
                            first_norm(b + 1)
                        inverse_deviation, modulate = normalising(b)
                        wait_apart(pool, mod2_in, 48 * (b + 1))

                        def second_norm(k):
                            if k < NT:
                                inverse_deviation(k, stat2_ready, rstd2_step, rstd2_ready)
                            if 1 <= k <= NT:
                                modulate(k - 1, x_hat_2, x_hat2, CB, SB, x_hat2_scaled, h2_ready)

                        for n in range(NP if more else NORM2_STEPS):
                            if n < NORM2_STEPS:
                                second_norm(n)
                            if more and n in PROJECT_AT:
                                split(i0 + G, PROJECT_AT[n])

                    entries(pool, entry)

                @block.scalar
                def _(act):
                    for primed in (exp_ready, logit_ready, y_taken):
                        act.sem_inc(primed, PRIMED)

                    def first_norm(b, t):
                        act.wait_ge(ht_ps, b * NT + t + 1)
                        nc.scalar.copy(h_hi[:, :, t * P:t * P + P],
                                       ring[:, t % 2, :].rearrange("p (c n) -> p c n", c=C)).then_inc(ht_hi, 1)

                    for t in range(NT):
                        first_norm(0, t)

                    def stack_part(i, g, t, s):
                        act.wait_ge(stack_ps, 2 * (i * NT + t) + s + 1)
                        nc.scalar.copy(stack_t[0:PARTS, g % 2, s, :, t * P:t * P + P],
                                       ring[0:PARTS, BANK["stack", 2 * t + s], :].rearrange("p (h n) -> p h n", h=HG))\
                            .then_inc(stack_ready, 1)

                    def keys_hi(i, t):
                        act.wait_ge(roped, i * NT + t + 1)
                        if t >= 2:
                            act.wait_ge(stack_ps, 2 * (i * NT + t - 1))
                        out_k = parts_tok[:, t % 2, 1, :, :].rearrange("p h (s d) -> p h s d", d=DH)
                        nc.scalar.copy(out_k[:, :, 0:3:2, :].bitcast(f32r),
                                       rope_a[:, t % 2, 128:256].rearrange("p (h d) -> p h d", d=DH)
                                       .unsqueeze(2).to_broadcast([P, HG, 2, DH])).then_inc(k_hi_ready, 1)

                    def prepare(i, g, n):
                        for kind, u in uses_of(n):
                            if kind == "stack":
                                stack_part(i, g, u // 2, u % 2)
                            elif kind == "qkv":
                                act.wait_ge(qkv_ps, PRIMED + i * NT + u + 1)
                                act.wait_ge(rope_terms, 3 * (i * NT + u + 1))
                                nc.scalar.copy(v_tok[:, g % 2, u, :, :].rearrange("p h d -> p (h d)"),
                                               ring[:, BANK["qkv", u], 256:384]).then_inc(v_ready, 1)
                        if n in PROJECT_AT:
                            keys_hi(i, PROJECT_AT[n])

                    for n in range(NP):
                        prepare(0, 0, n)

                    def entry(b, more):
                        i0 = first_group(act, b)

                        def exponentials(i, g, n):
                            qc, kt, hp = PAIRS[n]
                            q0 = max(0, kt * P - qc * QC)
                            act.wait_ge(st_ps, i * NP + n + 1)
                            if n >= 2:
                                act.wait_ge(pv_done, i * NP + n - 1)
                            if g == 0 and n == 0:
                                for k in range(2):
                                    act.wait_ge(h2_out[k], PRIMED + 16 * b * (NT // 2))
                            nc.scalar.activation(probs[:, n % 2, :, q0:QC], pair[:, n % 2, :, q0:QC], ACT.Exp,
                                                 scale=SCALE).then_inc(exp_ready, 1)

                        def take_output(i, g, qc):
                            last = sum(1 for p in PAIRS if p[0] <= qc)
                            act.wait_ge(pv_done, i * NP + last)
                            act.wait_ge(y_ready, PRIMED + i * NQC + qc)
                            if g == 0 and qc == 0:
                                act.wait_ge(x1_ready, PRIMED + b * NT)
                            for k in range(2):
                                nc.scalar.copy(r_den[64 * k:64 * k + 64, :], den_ps[64 - 64 * k:128 - 64 * k, :])\
                                    .then_inc(y_taken, 1)
                            nc.scalar.copy(y_t[:, g, qc * QC:(qc + 1) * QC], y_ps[:, :]).then_inc(y_taken, 1)

                        for g in range(G):
                            for n in range(NP):
                                exponentials(i0 + g, g, n)
                                if g + 1 < G:
                                    prepare(i0 + g + 1, g + 1, n)
                                if n in (NT, NP - 1):
                                    take_output(i0 + g, g, int(n == NP - 1))
                                if g == G - 1 and more and n in NORM_AT:
                                    first_norm(b + 1, NORM_AT[n])

                        def second_norm(k):
                            t, u = k - 2, k - 3
                            if 0 <= t < NT:
                                act.wait_ge(h2t_ps, b * NT + t + 1)
                                if t >= 2:
                                    act.wait_ge(logit_ps, b * NT + t - 1)
                                nc.scalar.copy(h2_t[:, t % 2, :, :].rearrange("p c n -> p (c n)"),
                                               pair[:, t % 2, 0, :]).then_inc(h2t_ready, 1)
                            if u >= 0:
                                act.wait_ge(logit_ps, b * NT + u + 1)
                                nc.scalar.copy(logits[:, ds(b * NT + u, 1), :].squeeze(1), pair[:, u % 2, 1, 0:E])\
                                    .then_inc(logit_ready, 1)

                        for n in range(NP if more else NORM2_STEPS):
                            if n < NORM2_STEPS:
                                second_norm(n)
                            if more:
                                prepare(i0 + G, 0, n)

                    entries(act, entry)

                @block.tensor
                def _(pe):
                    pe.sem_inc(qkv_ps, PRIMED)

                    def first_norm(b, t, first):
                        pe.wait_ge(h_ready, b * NT + t + 1)
                        if t >= 2:
                            pe.wait_ge(ht_lo, b * NT + t - 1)
                        elif t == 0 and not first:
                            pe.wait_ge(s_read, PRIMED + b * G * NM)
                        for c in range(C):
                            mm = nc.tensor.transpose(ring[:, t % 2, c * P:c * P + P],
                                                     x_hat[:, t % 2, c * P:c * P + P], ident_f[:, :])
                        mm.then_inc(ht_ps, 1)

                    for t in range(NT):
                        first_norm(0, t, True)

                    def bank_free(i, use):
                        k = RING.index(use) - 2
                        kind, u = RING[k] if k >= 0 else ("before", 0)
                        if kind == "qkv":
                            pe.wait_ge(v_ready, i * NT + u + 1)
                        elif kind == "stack":
                            pe.wait_ge(stack_ready, i * 2 * NT + u + 1)
                        elif kind == "max":
                            pe.wait_ge(s_read, PRIMED + i * NM + u + 1)
                        else:
                            pe.wait_ge(s_read, PRIMED + i * NM)

                    def project(b, i, g, t):
                        bank_free(i, ("qkv", t))
                        if t == 0:
                            pe.wait_ge(w_parts_in[g % 2], 32 * (2 * b + g // 2 + 1))
                        w_hi, w_lo = w_parts[:, g % 2, 0, :, :], w_parts[:, g % 2, 1, :, :]
                        cols = slice(t * P, t * P + P)
                        products = [(lhs, rhs, c) for c in range(C)
                                    for lhs, rhs in ((h_hi, w_hi), (h_hi, w_lo), (h_lo, w_hi))]
                        for k, (lhs, rhs, c) in enumerate(products):
                            mm = nc.tensor.matmul(ring[:, BANK["qkv", t], 0:384], lhs[:, c, cols], rhs[:, c, :],
                                                  start=(k == 0), stop=(k == len(products) - 1))
                        mm.then_inc(qkv_ps, 1)

                    def turn_parts(i, t, s):
                        bank_free(i, ("stack", 2 * t + s))
                        pe.wait_ge(parts_ready, 2 * (i * NT + t + 1))
                        for h in range(HG):
                            mm = nc.tensor.transpose(ring[0:PARTS, BANK["stack", 2 * t + s], h * P:h * P + P],
                                                     parts_tok[:, t % 2, s, h, :], ident_f[:, :])
                        mm.then_inc(stack_ps, 1)

                    def score_rows(i, g, u):
                        h, qt, kc = MAXES[u]
                        width = min((qt + 1) * P - kc * 512, 512)
                        diagonal = kc == qt // 4
                        if u == 0 or MAXES[u - 1][1] < qt:
                            pe.wait_ge(stack_ready, i * 2 * NT + 2 * (qt + 1))
                        bank_free(i, ("max", u))
                        mm = nc.tensor.matmul(ring[:, BANK["max", u], 0:width],
                                              stack_t[0:PARTS, g % 2, 0, h, qt * P:qt * P + P],
                                              stack_t[0:PARTS, g % 2, 1, h, kc * 512:kc * 512 + width],
                                              start=True, stop=not diagonal)
                        if diagonal:
                            mm = nc.tensor.matmul(ring[:, BANK["max", u], width - P:width], ident_b[:, :],
                                                  masks_b[:, 0, :], start=False, stop=True)
                        mm.then_inc(s_ps, 1)

                    def prepare(b, i, g, use):
                        kind, u = use
                        if kind == "stack":
                            turn_parts(i, u // 2, u % 2)
                        elif kind == "qkv":
                            project(b, i, g, u)
                        else:
                            score_rows(i, g, u)

                    pe.wait_ge(ht_lo, NT)
                    for n in range(NP):
                        for use in uses_of(n):
                            prepare(0, 0, 0, use)

                    def entry(b, more):
                        wait_apart(pe, x1_ready, PRIMED + b * NT)
                        i0 = first_group(pe, b)

                        def score_columns(i, g, n, j):
                            qc, kt, hp = PAIRS[n]
                            q0 = max(0, kt * P - qc * QC)
                            diagonal = kt * P >= qc * QC
                            if n == 0 and j == 0:
                                pe.wait_ge(max_in, PRIMED + 16 * i + 16)
                                pe.wait_ge(v_ready, (i + 1) * NT)
                                if g == 0:
                                    pe.wait_ge(logit_ready, PRIMED + b * NT)
                            if j == 0:
                                pe.wait_ge(exp_ready, PRIMED + i * NP + max(n - 1, 0))
                            h = 2 * hp + j
                            mm = nc.tensor.matmul(pair[:, n % 2, j, q0:QC],
                                                  stack_t[:, g % 2, 1, h, kt * P:kt * P + P],
                                                  stack_t[:, g % 2, 0, h, qc * QC + q0:(qc + 1) * QC],
                                                  start=True, stop=not diagonal)
                            if diagonal:
                                mm = nc.tensor.matmul(pair[:, n % 2, j, q0:q0 + P], ident_b[:, :],
                                                      masks_b[:, 1, :], start=False, stop=True)
                            if j == 1:
                                mm.then_inc(st_ps, 1)

                        def values(i, g, n):
                            qc, kt, hp = PAIRS[n]
                            q0 = max(0, kt * P - qc * QC)
                            first, last = kt == 0, kt == 4 * qc + 3
                            pe.wait_ge(exp_ready, PRIMED + i * NP + n + 1)
                            if kt == 0 and hp == 0:
                                pe.wait_ge(y_taken, PRIMED + 3 * (i * NQC + qc))
                            for j in range(2):
                                at = 32 * (2 * hp + j)
                                nc.tensor.matmul(y_ps[at:at + 32, q0:QC], v_tok[:, g % 2, kt, 2 * hp + j, :],
                                                 probs[:, n % 2, j, q0:QC], start=first, stop=last)
                            for j in range(2):
                                at = (32 * (2 * hp + j) + 64) % P
                                mm = nc.tensor.matmul(den_ps[at:at + 32, q0:QC], ones[:, :],
                                                      probs[:, n % 2, j, q0:QC], start=first, stop=last)
                            mm.then_inc(pv_done, 1)

                        for g in range(G):
                            for n in range(NP):
                                uses = uses_of(n) if g + 1 < G else []
                                pieces = [lambda: score_columns(i0 + g, g, n, 0), lambda: score_columns(i0 + g, g, n, 1)]
                                if n >= 1:
                                    pieces.append(lambda: values(i0 + g, g, n - 1))
                                if n == 0 and uses:
                                    prepare(b, i0 + g + 1, g + 1, uses.pop(0))
                                for k in range(max(len(uses), len(pieces))):
                                    if k < len(pieces):
                                        pieces[k]()
                                    if k < len(uses):
                                        prepare(b, i0 + g + 1, g + 1, uses[k])
                                if g == G - 1 and more and n in NORM_AT:
                                    first_norm(b + 1, NORM_AT[n], False)
                            values(i0 + g, g, NP - 1)

                        pe.wait_ge(y_ready, PRIMED + (b + 1) * G * NQC)
                        if more:
                            pe.wait_ge(ht_lo, (b + 2) * NT)

                        def logits_of(t):
                            pe.wait_ge(h2t_ready, b * NT + t + 1)
                            if t >= 2:
                                pe.wait_ge(logit_ready, PRIMED + b * NT + t - 1)
                            for c in range(C):
                                mm = nc.tensor.matmul(pair[:, t % 2, 1, 0:E], h2_t[:, t % 2, c, :], w_gate[:, c, :],
                                                      start=(c == 0), stop=(c == C - 1))
                            mm.then_inc(logit_ps, 1)

                        def second_norm(t):
                            if t < NT:
                                if t >= 2:
                                    pe.wait_ge(o_gated, b * NT + t - 1)
                                for g in range(G):
                                    mm = nc.tensor.matmul(o_acc[t % 2], y_t[:, g, t * P:t * P + P], w_out[:, g, :],
                                                          start=(g == 0), stop=(g == G - 1))
                                mm.then_inc(o_ps, 1)
                            if 2 <= t < NT + 2:
                                u = t - 2
                                pe.wait_ge(h2_ready, PRIMED + b * NT + u + 1)
                                if u >= 2:
                                    pe.wait_ge(h2t_ready, b * NT + u - 1)
                                for c in range(C):
                                    mm = nc.tensor.transpose(pair[:, u % 2, 0, c * P:c * P + P],
                                                             x_hat_2[:, u % 2, c * P:c * P + P], ident_f[:, :])
                                mm.then_inc(h2t_ps, 1)
                            if t >= 3:
                                logits_of(t - 3)

                        for n in range(NP if more else NORM2_STEPS):
                            if n < NORM2_STEPS:
                                second_norm(n)
                            if more:
                                for use in uses_of(n):
                                    prepare(b + 1, i0 + G, 0, use)

                    entries(pe, entry)

        tok_dram = nc.dram_tensor("tok_dram", [P * SLOTS, 1], i32, kind="Internal").ap()
        y_dram = nc.dram_tensor("y_dram", [SLOTS * P, D], f32, kind="Internal").ap()

        with ExitStack() as part:
            def sb(name, shape, dt=f32):
                return part.enter_context(nc.sbuf_tensor(name, shape, dt))

            def ps(name, shape):
                return part.enter_context(nc.psum_tensor(name, shape, f32))

            TE = TT * E
            w1_sb = sb("w1_sb", [P, E, C, F])
            w2_sb = sb("w2_sb", [P, E, F // P, D])
            slot_of = sb("slot_of", [P, TT, 2], i32)
            place_of = sb("place_of", [P, TT, 2], i32)
            weight = sb("weight", [P, TT, 2])
            expert_of = sb("expert_of", [1, SLOTS], i32)
            tokens = sb("tokens", [P, SLOTS], i32)
            gb_b = sb("gb_b", [P, B, D])

            w_in = [sem("w1_in"), sem("w2_in")]
            tab_in, zero_out, zeroed = sem("tab_in"), sem("zero_out"), sem("zeroed")
            r_dve, r_act, r_pe, pos_ready, experts_ready = (
                sem("r_dve"), sem("r_act"), sem("r_pe"), sem("pos_ready"), sem("experts_ready"))
            ids_out, tokens_in, gb_in = sem("ids_out"), sem("tokens_in"), sem("gb_in")

            with ExitStack() as inner:
                def tmp(name, shape, dt=f32):
                    return inner.enter_context(nc.sbuf_tensor(name, shape, dt))

                bal_b = tmp("bal_b", [P, E])
                count_e = tmp("count_e", [P, E])
                count_s = tmp("count_s", [P, SLOTS])
                ids = tmp("ids", [P, TT], i32)
                earlier = tmp("earlier", [P, P])
                all_ones = tmp("all_ones", [P, P])
                restart = tmp("restart", [P, E, TT])
                z = tmp("z", [P, TT, E])
                score = tmp("score", [P, TT, E])
                top = tmp("top", [P, TT, 8])
                top_at = tmp("top_at", [P, TT, 8], u32)
                at_f = tmp("at_f", [P, TT, 2])
                pick = tmp("pick", [P, 2, TT, E])
                both = tmp("both", [P, TT, E])
                upto = tmp("upto", [P, E, TT])
                slot_e = tmp("slot_e", [P, E, TT])
                cnt_i = tmp("cnt_i", [P, E], i32)
                tiles = tmp("tiles", [P, E])
                upto_e = tmp("upto_e", [P, E])
                base = tmp("base", [P, E])
                total = tmp("total", [P, TT])
                slot_f = tmp("slot_f", [P, TT, 2])
                row_i = tmp("row_i", [P, TT, 2], i32)
                row_f = tmp("row_f", [P, TT, 2])
                cmp = tmp("cmp", [1, SLOTS, E])
                exp_f = tmp("exp_f", [1, SLOTS])
                zeros = tmp("zeros", [P, SLOTS], i32)
                before_ps = inner.enter_context(nc.psum_tensor("before_ps", [P, E, TT], f32))
                all_ps = inner.enter_context(nc.psum_tensor("all_ps", [P, E, TT], f32))

                with nc.Block() as block:
                    @block.sync
                    def _(sp):
                        sp.dma_start(bal_b[:, :], bal.to_broadcast([P, E])).then_inc(tab_in, 16)
                        sp.dma_start(count_e[:, :], e_count).then_inc(tab_in, 16)
                        sp.dma_start(count_s[:, :], s_count).then_inc(tab_in, 16)
                        sp.dma_start(ids[:, :], tok_ids).then_inc(tab_in, 16)
                        sp.dma_start(earlier[:, :], earlier_t).then_inc(tab_in, 16)
                        sp.wait_ge(zeroed, 3)
                        sp.dma_start(tok_dram.rearrange("(p s) o -> p (s o)", p=P), zeros[:, :]).then_inc(zero_out, 16)
                        for b in range(B):
                            sp.dma_start(gb_b[:, b, :], mod_dram[GB, b:b + 1, :].to_broadcast([P, D]))\
                                .then_inc(gb_in, 16)
                        sp.wait_ge(ids_out, 16 * 2 * TT)
                        sp.dma_start(tokens[:, :], tok_dram.rearrange("(p s) o -> p (s o)", p=P)).then_inc(tokens_in, 16)
                        sp.wait_ge(tokens_in, 16)
                        sp.wait_ge(gb_in, 16 * B)

                    @block.scalar
                    def _(act):
                        act.wait_ge(tab_in, 80)
                        act.wait_ge(zero_out, 16)
                        act.dma_start(w1_sb[:, :, :, :], w1).then_inc(w_in[0], 16)
                        act.dma_start(w2_sb[:, :, :, :], w2).then_inc(w_in[1], 16)
                        act.wait_ge(r_dve, 1)
                        nc.scalar.activation(score[:, :, :], z[:, :, :], ACT.Exp, scale=-1.0).then_inc(r_act, 1)

                    @block.tensor
                    def _(pe):
                        pe.wait_ge(r_dve, 11)
                        pe.wait_ge(tab_in, 80)
                        pe.wait_ge(zeroed, 3)
                        nc.tensor.matmul(before_ps[:, :, :], earlier[:, :], both[:, :, :].rearrange("p t e -> p e t"),
                                         start=True, stop=True).then_inc(r_pe, 1)
                        nc.tensor.matmul(all_ps[:, :, :], all_ones[:, :], both[:, :, :].rearrange("p t e -> p e t"),
                                         start=True, stop=True).then_inc(r_pe, 1)

                    @block.gpsimd
                    def _(pool):
                        nc.gpsimd.memset(zeros[:, :], 0).then_inc(zeroed, 1)
                        nc.gpsimd.memset(all_ones[:, :], 1.0).then_inc(zeroed, 1)
                        nc.gpsimd.memset(restart[:, :, :], 1.0).then_inc(zeroed, 1)
                        pool.wait_ge(pos_ready, 1)
                        pool.wait_ge(zero_out, 16)
                        pool.wait_ge(tab_in, 80)
                        for t in range(TT):
                            for k in range(2):
                                pool.indirect_dma_start(
                                    out=tok_dram, out_offset=bass.IndirectOffsetOnAxis(ap=place_of[:, t, k:k + 1], axis=0),
                                    in_=ids[:, t:t + 1], in_offset=None).then_inc(ids_out, 16)

                    @block.vector
                    def _(dve):
                        step = [0]

                        def done(instruction):
                            step[0] += 1
                            instruction.then_inc(r_dve, 1)
                            dve.wait_ge(r_dve, step[0])

                        v = nc.vector
                        dve.wait_ge(tab_in, 80)
                        done(v.tensor_tensor(z[:, :, :], logits[:, :, :], bal_b[:, :].unsqueeze(1).to_broadcast([P, TT, E]),
                                             ALU.add))
                        dve.wait_ge(r_act, 1)
                        done(v.tensor_scalar_add(z[:, :, :], score[:, :, :], 1.0))
                        done(v.reciprocal(score[:, :, :], z[:, :, :]))
                        for t in range(TT):
                            last = v.max(top[:, t, :], score[:, t, :])
                        done(last)
                        for t in range(TT):
                            last = v.max_index(top_at[:, t, :], top[:, t, :], score[:, t, :])
                        done(last)
                        done(v.tensor_copy(at_f[:, :, :], top_at[:, :, 0:2]))
                        for k in range(2):
                            last = v.tensor_tensor(pick[:, k, :, :], count_e[:, :].unsqueeze(1).to_broadcast([P, TT, E]),
                                                   at_f[:, :, k:k + 1].to_broadcast([P, TT, E]), ALU.is_equal)
                        done(last)
                        done(v.tensor_tensor(total[:, :], top[:, :, 0], top[:, :, 1], ALU.add))
                        done(v.tensor_scalar_add(total[:, :], total[:, :], 1e-6))
                        done(v.reciprocal(total[:, :], total[:, :]))
                        done(v.tensor_tensor(both[:, :, :], pick[:, 0, :, :], pick[:, 1, :, :], ALU.add))
                        done(v.tensor_tensor(weight[:, :, :], top[:, :, 0:2], total[:, :].unsqueeze(2).to_broadcast([P, TT, 2]),
                                             ALU.mult))
                        dve.wait_ge(zeroed, 3)
                        done(v.memset(restart[:, :, 0:1], 0.0))
                        dve.wait_ge(r_pe, 2)
                        done(v.tensor_tensor_scan(upto[:, :, :].rearrange("p e t -> p (e t)"),
                                                  restart[:, :, :].rearrange("p e t -> p (e t)"),
                                                  all_ps[:, :, :].rearrange("p e t -> p (e t)"), 0.0, ALU.mult, ALU.add))
                        done(v.tensor_scalar_add(cnt_i[:, :], upto[:, :, TT - 1], float(P - 1)))
                        done(v.tensor_scalar(cnt_i[:, :], cnt_i[:, :], 7, None, ALU.arith_shift_right))
                        done(v.tensor_copy(tiles[:, :], cnt_i[:, :]))
                        done(v.tensor_tensor_scan(upto_e[:, :], all_ones[:, 0:E], tiles[:, :], 0.0, ALU.mult, ALU.add))
                        done(v.tensor_tensor(base[:, :], upto_e[:, :], tiles[:, :], ALU.subtract))
                        done(v.tensor_scalar(base[:, :], base[:, :], float(P), None, ALU.mult))
                        done(v.tensor_tensor(upto[:, :, :], upto[:, :, :], all_ps[:, :, :], ALU.subtract))
                        done(v.tensor_tensor(upto[:, :, :], upto[:, :, :], before_ps[:, :, :], ALU.add))
                        done(v.tensor_tensor(slot_e[:, :, :], upto[:, :, :],
                                             base[:, :].unsqueeze(2).to_broadcast([P, E, TT]), ALU.add))
                        for k in range(2):
                            done(v.tensor_tensor(pick[:, k, :, :], pick[:, k, :, :],
                                                 slot_e[:, :, :].rearrange("p e t -> p t e"), ALU.mult))
                            done(v.tensor_reduce(slot_f[:, :, k:k + 1], pick[:, k, :, :], AX.X, ALU.add))
                        done(v.tensor_copy(slot_of[:, :, :], slot_f[:, :, :]))
                        done(v.tensor_scalar(row_i[:, :, :], slot_of[:, :, :], 7, None, ALU.arith_shift_right))
                        done(v.tensor_copy(row_f[:, :, :], row_i[:, :, :]))
                        done(v.tensor_scalar(slot_f[:, :, :], slot_f[:, :, :], float(SLOTS), None, ALU.mult))
                        done(v.scalar_tensor_tensor(out=place_of[:, :, :], in0=row_f[:, :, :], scalar=float(1 - P * SLOTS),
                                                    in1=slot_f[:, :, :], op0=ALU.mult, op1=ALU.add))
                        v.engine_nop().then_inc(pos_ready, 1)
                        done(v.tensor_tensor(cmp[:, :, :], upto_e[0:1, :].unsqueeze(1).to_broadcast([1, SLOTS, E]),
                                             count_s[0:1, :].unsqueeze(2).to_broadcast([1, SLOTS, E]), ALU.is_le))
                        done(v.tensor_reduce(exp_f[:, :].unsqueeze(2), cmp[:, :, :], AX.X, ALU.add))
                        v.tensor_scalar_min(expert_of[:, :], exp_f[:, :], float(E - 1)).then_inc(experts_ready, 1)

            xg = sb("xg", [P, 4, D])
            idx = sb("idx", [P, 4], i32)
            xg_t = sb("xg_t", [P, 2, C, P])
            e_neg = sb("e_neg", [P, 2, F])
            den = sb("den", [P, 2, F])
            hid = sb("hid", [P, 2, F])
            hid_t = sb("hid_t", [P, 2, F // P, P])
            y_sb = sb("y_sb", [P, 4, D])

            idx_ready = sem("idx_ready")
            xg_in = [sem(f"xg_in{k}") for k in range(4)]
            y_out = [sem(f"y_out{k}") for k in range(4)]
            xt_ps_r, xt_read, up_r, exp_r, den_r, rec_r, hid_r, ht_ps_r, ht_read, y_ps_r, y_read = (
                sem(n) for n in ("xt_ps_r", "xt_read", "up_r", "exp_r", "den_r", "rec_r", "hid_r", "ht_ps_r", "ht_read",
                                 "y_ps_r", "y_read"))

            with ExitStack() as inner:
                def ips(name, shape):
                    return inner.enter_context(nc.psum_tensor(name, shape, f32))

                xt_ps = ips("xt_ps", [P, 2, 512])
                up_ps = ips("up_ps", [P, 2, 512])
                ht_ps_ = ips("ht_ps_", [P, 2, 512])
                yo_ps = ips("yo_ps", [P, 2, 512])

                LAST = 3

                def steps(eng, body):
                    for s in range(4):
                        body(s, s, range(s + 1))
                    with eng.Fori(1, SLOTS // 4) as i:
                        s0 = eng.snap(i * 4)
                        for k in range(4):
                            body(s0 + k, k, range(4))
                    for s in range(SLOTS, SLOTS + LAST):
                        body(s, s % 4, range(s - SLOTS + 1, 4))

                with nc.Block() as block:
                    @block.gpsimd
                    def _(pool):
                        def body(s, k, ages):
                            if 0 in ages:
                                if 3 in ages:
                                    wait_apart(pool, xt_ps_r, s - 3)
                                nc.gpsimd.tensor_copy(idx[:, k:k + 1], tokens[:, ds(s, 1)]).then_inc(idx_ready, 1)
                                wait_apart(pool, idx_ready, s + 1)
                                pool.indirect_dma_start(
                                    out=xg[:, k, :], out_offset=None, in_=h2_dram,
                                    in_offset=bass.IndirectOffsetOnAxis(ap=idx[:, k:k + 1], axis=0))\
                                    .then_inc(xg_in[k], 16)
                        steps(pool, body)

                    @block.tensor
                    def _(pe):
                        for k in range(2):
                            pe.wait_ge(w_in[k], 16)

                        def body(s, k, ages):
                            if 0 in ages:
                                pe.wait_ge(xg_in[k], 4 * (s - k) + 16)
                                if 2 in ages:
                                    pe.wait_ge(xt_read, s - 1)
                                for c in range(C):
                                    mm = nc.tensor.transpose(xt_ps[:, k % 2, c * P:c * P + P], xg[:, k, c * P:c * P + P],
                                                             ident_f[:, :])
                                mm.then_inc(xt_ps_r, 1)
                            if 1 in ages:
                                e = pe.value_load(expert_of[0:1, ds(s - 1, 1)], min_val=0, max_val=E - 1)
                                j = (k + 1) % 2
                                pe.wait_ge(xt_read, s)
                                if 3 in ages:
                                    pe.wait_ge(hid_r, s - 2)
                                for c in range(C):
                                    mm = nc.tensor.matmul(up_ps[:, j, 0:F], xg_t[:, j, c, :],
                                                          w1_sb[:, ds(e, 1), c, :].squeeze(1),
                                                          start=(c == 0), stop=(c == C - 1))
                                mm.then_inc(up_r, 1)
                            if 2 in ages:
                                j = k % 2
                                pe.wait_ge(hid_r, s - 1)
                                for c in range(F // P):
                                    mm = nc.tensor.transpose(ht_ps_[:, j, c * P:c * P + P], hid[:, j, c * P:c * P + P],
                                                             ident_f[:, :])
                                mm.then_inc(ht_ps_r, 1)
                            if 3 in ages:
                                e = pe.value_load(expert_of[0:1, ds(s - 3, 1)], min_val=0, max_val=E - 1)
                                j = (k + 1) % 2
                                pe.wait_ge(ht_read, s - 2)
                                pe.wait_ge(y_read, PRIMED + s - 4)
                                for c in range(F // P):
                                    mm = nc.tensor.matmul(yo_ps[:, j, :], hid_t[:, j, c, :],
                                                          w2_sb[:, ds(e, 1), c, :].squeeze(1),
                                                          start=(c == 0), stop=(c == F // P - 1))
                                mm.then_inc(y_ps_r, 1)
                        steps(pe, body)

                    @block.scalar
                    def _(act):
                        def body(s, k, ages):
                            if 0 in ages:
                                j = k % 2
                                act.wait_ge(xt_ps_r, s + 1)
                                if 2 in ages:
                                    act.wait_ge(up_r, s - 1)
                                nc.scalar.copy(xg_t[:, j, :, :].rearrange("p c n -> p (c n)"), xt_ps[:, j, :])\
                                    .then_inc(xt_read, 1)
                            if 1 in ages:
                                j = (k + 1) % 2
                                act.wait_ge(up_r, s)
                                if 3 in ages:
                                    act.wait_ge(den_r, s - 2)
                                nc.scalar.activation(e_neg[:, j, :], up_ps[:, j, 0:F], ACT.Exp, scale=-1.0)\
                                    .then_inc(exp_r, 1)
                            if 2 in ages:
                                j = k % 2
                                act.wait_ge(ht_ps_r, s - 1)
                                if 3 in ages:
                                    act.wait_ge(y_ps_r, PRIMED + s - 4)
                                nc.scalar.copy(hid_t[:, j, :, :].rearrange("p c n -> p (c n)"), ht_ps_[:, j, 0:F])\
                                    .then_inc(ht_read, 1)
                        steps(act, body)

                    @block.vector
                    def _(dve):
                        dve.sem_inc(y_read, PRIMED)

                        def body(s, k, ages):
                            if 1 in ages:
                                j = (k + 1) % 2
                                dve.wait_ge(exp_r, s)
                                nc.vector.tensor_scalar_add(den[:, j, :], e_neg[:, j, :], 1.0).then_inc(den_r, 1)
                                dve.wait_ge(den_r, s)
                                nc.vector.reciprocal(den[:, j, :], den[:, j, :]).then_inc(rec_r, 1)
                                dve.wait_ge(rec_r, s)
                                if 3 in ages:
                                    dve.wait_ge(ht_ps_r, s - 2)
                                nc.vector.tensor_tensor(hid[:, j, :], den[:, j, :], up_ps[:, j, 0:F], ALU.mult)\
                                    .then_inc(hid_r, 1)
                            if 3 in ages:
                                dve.wait_ge(y_ps_r, PRIMED + s - 3)
                                dve.wait_ge(y_out[(k + 1) % 4], PRIMED + 4 * (s - 3 - (k + 1) % 4))
                                nc.vector.tensor_copy(y_sb[:, (k + 1) % 4, :], yo_ps[:, (k + 1) % 2, :])\
                                    .then_inc(y_read, 1)
                        steps(dve, body)

                    @block.sync
                    def _(sp):
                        for k in range(4):
                            sp.sem_inc(y_out[k], PRIMED)
                        with sp.Fori(0, SLOTS // 4) as i:
                            for k in range(4):
                                sp.wait_ge(y_read, PRIMED + i * 4 + k + 1)
                                sp.dma_start(y_dram[ds((i * 4 + k) * P, P), :], y_sb[:, k, :]).then_inc(y_out[k], 16)
                        for k in range(4):
                            sp.wait_ge(y_out[k], PRIMED + 16 * (SLOTS // 4))

            ya = sb("ya", [P, 4, D])
            yb = sb("yb", [P, 4, D])
            xr = sb("xr", [P, 4, D])
            res = sb("res", [P, 4, D])
            yab_in = [[sem(f"y{n}_in{k}") for k in range(4)] for n in "ab"]
            xr_in = [sem(f"xr_in{k}") for k in range(4)]
            out_s = [sem(f"out_s{k}") for k in range(4)]
            m_a, m_b, m_g, m_x = sem("m_a"), sem("m_b"), sem("m_g"), sem("m_x")
            out_tiles = out.rearrange("b (t p) d -> (b t) p d", p=P)

            with nc.Block() as block:
                @block.gpsimd
                def _(pool):
                    for t in range(TT):
                        for n, dst in enumerate((ya, yb)):
                            if t >= 4:
                                pool.wait_ge(m_b, t - 3)
                            pool.indirect_dma_start(
                                out=dst[:, t % 4, :], out_offset=None, in_=y_dram,
                                in_offset=bass.IndirectOffsetOnAxis(ap=slot_of[:, t, n:n + 1], axis=0))\
                                .then_inc(yab_in[n][t % 4], 16)

                @block.sync
                def _(sp):
                    for t in range(TT):
                        if t >= 4:
                            sp.wait_ge(m_x, t - 3)
                        sp.dma_start(xr[:, t % 4, :], x1_dram[t, :, :]).then_inc(xr_in[t % 4], 16)

                @block.scalar
                def _(act):
                    for t in range(TT):
                        act.wait_ge(m_x, t + 1)
                        act.dma_start(out_tiles[t, :, :], res[:, t % 4, :]).then_inc(out_s[t % 4], 16)
                    for k in range(4):
                        act.wait_ge(out_s[k], 16 * (TT // 4))

                @block.vector
                def _(dve):
                    for t in range(TT):
                        k = t % 4
                        dve.wait_ge(yab_in[0][k], 16 * (t // 4 + 1))
                        if t >= 4:
                            dve.wait_ge(out_s[k], 16 * (t // 4))
                        nc.vector.tensor_scalar(res[:, k, :], ya[:, k, :], weight[:, t, 0:1], None, ALU.mult)\
                            .then_inc(m_a, 1)
                        dve.wait_ge(yab_in[1][k], 16 * (t // 4 + 1))
                        dve.wait_ge(m_a, t + 1)
                        nc.vector.scalar_tensor_tensor(out=res[:, k, :], in0=yb[:, k, :], scalar=weight[:, t, 1:2],
                                                       in1=res[:, k, :], op0=ALU.mult, op1=ALU.add).then_inc(m_b, 1)
                        dve.wait_ge(m_b, t + 1)
                        nc.vector.tensor_tensor(res[:, k, :], res[:, k, :], gb_b[:, t // NT, :], ALU.mult)\
                            .then_inc(m_g, 1)
                        dve.wait_ge(m_g, t + 1)
                        dve.wait_ge(xr_in[k], 16 * (t // 4 + 1))
                        nc.vector.tensor_tensor(res[:, k, :], res[:, k, :], xr[:, k, :], ALU.add).then_inc(m_x, 1)


def _constants(np):
    ident = np.eye(P, dtype=np.float32)
    later = np.triu(np.ones((P, P), np.float32), 1) * np.float32(-1e30)
    masks = np.ascontiguousarray(np.stack([later, later.T], 1))
    inv = np.float32(1.0) / np.float32(10000.0) ** (np.arange(0, DH, 2, dtype=np.float32) / np.float32(DH))
    angle = np.arange(L, dtype=np.float32)[:, None] * inv[None, :]
    cos, sin = np.cos(angle), np.sin(angle)
    rope = np.stack([np.concatenate([cos, cos], 1), np.concatenate([-sin, sin], 1)])
    rope = np.ascontiguousarray(rope.reshape(2, NT, P, DH).transpose(2, 0, 1, 3).astype(np.float32))
    k_ones = np.zeros((P, HG), np.float32)
    for h in range(HG):
        k_ones[MROW + 2 * h:MROW + 2 * h + 2, h] = 1.0
    rows = lambda n: np.ascontiguousarray(np.broadcast_to(np.arange(n, dtype=np.float32), (P, n)))
    tok_ids = np.ascontiguousarray(np.arange(TT * P, dtype=np.int32).reshape(TT, P).T)
    earlier = np.triu(np.ones((P, P), np.float32), 1)
    return dict(ident=ident, masks=masks, rope=rope, k_ones=k_ones, e_count=rows(E), s_count=rows(SLOTS),
                tok_ids=tok_ids, earlier_t=earlier)


def _layout(np, i):
    w = i["L0_attn_W_qkv"].reshape(3, G, HG, DH, D)
    even_odd = w.reshape(3, G, HG, DH // 2, 2, D).transpose(0, 1, 2, 4, 3, 5).reshape(3, G, HG, DH, D)
    w = np.concatenate([even_odd[:2], w[2:]], 0).transpose(1, 0, 2, 3, 4).reshape(3 * D, D)
    chunks = lambda a: np.ascontiguousarray(a.reshape(C, P, *a.shape[1:]).transpose(1, 0, *range(2, a.ndim + 1)))
    return dict(
        x=np.ascontiguousarray(i["L0_attn_x"]),
        w_qkv_t=chunks(w.T), w_o_t=chunks(i["L0_attn_W_o"].T), wg_t=chunks(i["L0_ffn_Wg"].T),
        bal=np.ascontiguousarray(i["L0_ffn_balance_bias"].reshape(1, E)),
        w1=np.ascontiguousarray(i["L0_ffn_W1"].reshape(E, C, P, F).transpose(2, 0, 1, 3)),
        w2=np.ascontiguousarray(i["L0_ffn_W2"].reshape(E, F // P, P, D).transpose(2, 0, 1, 3)),
        c_t=chunks(i["L0_c"].T), w_mod=chunks(i["L0_wmod"].reshape(D, 6, D)))


def kernel(**inputs):
    import numpy as _np
    import concourse.bacc as _bacc
    from concourse import mybir as _mybir
    from concourse.bass_utils import run_bass_kernel_spmd as _run

    nc = _bacc.Bacc("TRN2", target_bir_lowering=False, num_devices=1)
    arrays = {**_layout(_np, {k: _np.asarray(v) for k, v in inputs.items()}), **_constants(_np)}
    aps = {name: nc.dram_tensor(name, a.shape, _mybir.dt.from_np(a.dtype), kind="ExternalInput").ap()
           for name, a in arrays.items()}
    out = nc.dram_tensor("out", [B, L, D], _mybir.dt.float32, kind="ExternalOutput").ap()
    adaln_block(nc, **aps, out=out)
    r = _run(nc, [arrays], core_ids=[0])
    return r.results[0]["out"]
```

```python
import concourse.bass as bass
from concourse import mybir
from contextlib import ExitStack

B, L, D, H = 4, 1024, 512, 16
DH = D // H
E, F = 16, 256
P = 128
NT = L // P
TT = B * NT
C = D // P
HG = 4
G = H // HG
QC = 512
NQC = L // QC
EPS = 1e-5
SCALE = 1.0 / float(DH) ** 0.5
PARTS = 3 * DH
MROW = PARTS
ST_TILES = sum(2 * 4 * (qc + 1) for qc in range(NQC))
SLOTS = -(-(2 * B * L + E * (P - 1)) // P)
assert SLOTS % 4 == 0
SA, CA, GA, SB, CB, GB = range(6)


def adaln_block(nc, x, w_qkv_t, w_o_t, wg_t, bal, w1, w2, c_t, w_mod, ident, masks, rope, k_ones,
                counts, tok_ids, earlier_t, out):
    f32, f32r, bf16 = mybir.dt.float32, mybir.dt.float32r, mybir.dt.bfloat16
    i32, u32 = mybir.dt.int32, mybir.dt.uint32
    ALU, ACT, AX = mybir.AluOpType, mybir.ActivationFunctionType, mybir.AxisListType
    ds = bass.ds

    mod_dram = nc.dram_tensor("mod_dram", [6, B, D], f32, kind="Internal").ap()
    w_dram = nc.dram_tensor("w_dram", [2, G, P, C, 384], f32, kind="Internal").ap()
    x1_dram = nc.dram_tensor("x1_dram", [TT, P, D], f32, kind="Internal").ap()
    h2_dram = nc.dram_tensor("h2_dram", [TT * P, D], f32, kind="Internal").ap()
    x_tiles = x.rearrange("b (t p) d -> (b t) p d", p=P)

    ctx = ExitStack()
    with ctx:
        def sem(name):
            return ctx.enter_context(nc.semaphore(name))

        def wait_apart(eng, semaphore, value):
            eng.wait_ge(semaphore, value)
            eng.sem_inc(waited, 1)

        waited = sem("waited")

        def keep(name, shape, dt=f32):
            return ctx.enter_context(nc.sbuf_tensor(name, shape, dt))

        ident_f = keep("ident_f", [P, P])
        logits = keep("logits", [P, TT, E])

        with ExitStack() as part:
            def sb(name, shape, dt=f32):
                return part.enter_context(nc.sbuf_tensor(name, shape, dt))

            w_parts = sb("w_parts", [P, 2, 2, C, 384], f32r)
            h_hi = sb("h_hi", [P, C, L], f32r)
            h_lo = sb("h_lo", [P, C, L], f32r)
            stack_t = sb("stack_t", [P, 2, 2, HG, L], f32r)
            v_tok = sb("v_tok", [P, 2, NT, HG, DH])
            probs = sb("probs", [P, 2, 2, QC])
            y_t = sb("y_t", [P, G, L])
            w_out = sb("w_out", [P, G, D])
            w_gate = sb("w_gate", [P, C, E])
            trig = sb("trig", [P, 2, NT, DH])
            masks_f = sb("masks_f", [P, 2, P])
            masks_b = sb("masks_b", [P, 2, P], bf16)
            ident_b = sb("ident_b", [P, P], bf16)
            k_ones_sb = sb("k_ones_sb", [P, HG])
            ones = sb("ones", [P, DH])
            neg_half = sb("neg_half", [P, 1])
            mod_b = sb("mod_b", [P, 5, D])
            x_in = sb("x_in", [P, 4, D])
            x_hat = sb("x_hat", [P, 2, D])
            stats = sb("stats", [P, 2, 6])
            mean_var = sb("mean_var", [P, 2, 2])
            rstd = sb("rstd", [P, 2, 2])
            rope_a, rope_b = x_hat[:, :, 0:256], x_hat[:, :, 256:512]
            parts_tok = sb("parts_tok", [P, 2, 2, HG, PARTS])
            neg_max = sb("neg_max", [P, NT, HG])
            neg_max2 = sb("neg_max2", [P, NT // 2, HG])
            max_tok = sb("max_tok", [P, NT, 32])
            r_den = sb("r_den", [P, QC])
            x1 = sb("x1", [P, 2, D])
            max_row = x1[:, :, :].rearrange("p a d -> p (a d)")
            x_hat_2 = probs[:, 0, :, :]
            h2_t = probs[:, 1, :, :].rearrange("p a (c n) -> p a c n", c=C)
            c_sb = sb("c_sb", [P, C, B])
            c_exp = sb("c_exp", [P, C, B])
            c_den = sb("c_den", [P, C, B])

            ring = part.enter_context(nc.psum_tensor("ring", [P, 2, 512], f32))
            pair = part.enter_context(nc.psum_tensor("pair", [P, 2, 2, 512], f32))
            y_ps = part.enter_context(nc.psum_tensor("y_ps", [P, QC], f32))
            den_ps = part.enter_context(nc.psum_tensor("den_ps", [P, QC], f32))
            o_acc = [y_ps[:, :], den_ps[:, :]]

            raw_w = y_t[:, :, :].rearrange("p g l -> p (g l)")[:, 0:2 * 1536].rearrange("p (c n) -> p c n", c=2)
            w_hi_stage = w_parts[:, :, :, :, :].rearrange("p a k c n -> p (a k c n)")\
                .rearrange("p (c n) -> p c n", c=C)
            w_lo_stage = [buf[:, :, :].rearrange("p c l -> p (c l)")[:, 0:2 * 1536].rearrange("p (c n) -> p c n", c=2)
                          for buf in (h_hi, h_lo)]
            raw_mod = [probs[:, :, :, :].rearrange("p a b q -> p (a b) q"),
                       mod_b[:, 0:4, :]]
            mod_row = [buf[0:B, k, :] for buf in (x_in, x_hat, x1) for k in range(2)]
            mod_sign, mod_size = r_den[0:B, :], parts_tok[0:B, :, :, :, :].rearrange("p a s h d -> p (a s h d)")[:, 0:D]

            const_in = sem("const_in")
            raw_w_in, w_split_hi, w_split = sem("raw_w_in"), sem("w_split_hi"), sem("w_split")
            raw_mod_in = [sem("raw_mod_in0"), sem("raw_mod_in1")]
            const_ready, w_lo_out, w_hi_out = sem("const_ready"), sem("w_lo_out"), sem("w_hi_out")
            silu_step, mod_ps, mod_step, mod_ready, mod_out = (
                sem("silu_step"), sem("mod_ps"), sem("mod_step"), sem("mod_ready"), sem("mod_out"))

            with nc.Block() as block:
                @block.sync
                def _(sp):
                    for k, (dst, src) in enumerate([(ident_f[:, :], ident), (masks_f[:, :, :], masks),
                                                    (trig[:, :, :, :], rope), (k_ones_sb[:, :], k_ones),
                                                    (w_out[:, :, :], w_o_t), (w_gate[:, :, :], wg_t),
                                                    (c_sb[:, :, :], c_t)]):
                        sp.dma_start(dst, src).then_inc(const_in, 16)
                    for k in range(6):
                        if k >= 2:
                            sp.wait_ge(mod_ps, k - 1)
                        sp.dma_start(raw_mod[k % 2], w_mod[:, :, k, :]).then_inc(raw_mod_in[k % 2], 16)
                    for k in range(6):
                        sp.wait_ge(mod_ready, k + 1)
                        sp.dma_start(mod_dram[k, :, :], mod_row[k]).then_inc(mod_out, 16)
                    sp.wait_ge(mod_out, 96)

                @block.gpsimd
                def _(pool):
                    nc.gpsimd.memset(ones[:, :], 1.0).then_inc(const_ready, 1)
                    nc.gpsimd.memset(neg_half[:, :], -0.5).then_inc(const_ready, 1)
                    for half in range(2):
                        if half:
                            pool.wait_ge(w_split, 1)
                        pool.dma_start(raw_w, w_qkv_t[:, 2 * half:2 * half + 2, :]).then_inc(raw_w_in, 16)
                        pool.wait_ge(w_split_hi, half + 1)
                        nc.gpsimd.tensor_tensor(w_lo_stage[half], raw_w,
                                                w_hi_stage[:, 2 * half:2 * half + 2, :].bitcast(f32),
                                                ALU.subtract).then_inc(w_split, 1)

                @block.scalar
                def _(act):
                    act.wait_ge(const_in, 112)
                    nc.scalar.activation(c_exp[:, :, :], c_sb[:, :, :], ACT.Exp, scale=-1.0).then_inc(silu_step, 1)
                    for half in range(2):
                        act.wait_ge(raw_w_in, 16 * (half + 1))
                        nc.scalar.copy(w_hi_stage[:, 2 * half:2 * half + 2, :], raw_w).then_inc(w_split_hi, 1)
                    act.wait_ge(w_split, 2)
                    for half in range(2):
                        for g in range(G):
                            act.dma_start(w_dram[1, g, :, 2 * half:2 * half + 2, :],
                                          w_lo_stage[half][:, :, 384 * g:384 * g + 384].bitcast(f32)).then_inc(w_lo_out, 16)
                    for g in range(G):
                        act.dma_start(w_dram[0, g, :, :, :],
                                      w_hi_stage[:, :, 384 * g:384 * g + 384].bitcast(f32)).then_inc(w_hi_out, 16)

                @block.vector
                def _(dve):
                    nc.vector.memset(max_tok[:, :, :], 0.0).then_inc(const_ready, 1)
                    for parity in range(2):
                        nc.vector.memset(stack_t[MROW:P, parity, 0, :, :].bitcast(u32), 0).then_inc(const_ready, 1)
                    dve.wait_ge(const_in, 112)
                    nc.vector.tensor_copy(masks_b[:, :, :], masks_f[:, :, :]).then_inc(const_ready, 1)
                    nc.vector.tensor_copy(ident_b[:, :], ident_f[:, :]).then_inc(const_ready, 1)
                    dve.wait_ge(silu_step, 1)
                    nc.vector.tensor_scalar_add(c_den[:, :, :], c_exp[:, :, :], 1.0).then_inc(silu_step, 1)
                    dve.wait_ge(silu_step, 2)
                    nc.vector.reciprocal(c_exp[:, :, :], c_den[:, :, :]).then_inc(silu_step, 1)
                    dve.wait_ge(silu_step, 3)
                    nc.vector.tensor_tensor(c_den[:, :, :], c_exp[:, :, :], c_sb[:, :, :], ALU.mult)\
                        .then_inc(silu_step, 1)
                    for h in range(HG):
                        for parity in range(2):
                            nc.vector.tensor_copy(stack_t[MROW:P, parity, 1, h, :],
                                                  k_ones_sb[MROW:P, h:h + 1].to_broadcast([P - MROW, L]))\
                                .then_inc(const_ready, 1)
                    step = 0
                    for k in range(6):
                        dve.wait_ge(mod_ps, k + 1)
                        row, ps = mod_row[k], ring[0:B, k % 2, :]
                        if k in (CA, CB):
                            nc.vector.tensor_scalar_add(row, ps, 1.0).then_inc(mod_ready, 1)
                        elif k in (SA, SB):
                            nc.vector.tensor_copy(row, ps).then_inc(mod_ready, 1)
                        else:
                            if step:
                                dve.wait_ge(mod_ready, k)
                            sign, size = mod_sign, mod_size
                            nc.vector.tensor_scalar(sign, ps, 0.0, 2.0, ALU.is_ge, ALU.mult).then_inc(mod_step, 1)
                            nc.vector.tensor_scalar(size, ps, -1.0, None, ALU.mult).then_inc(mod_step, 1)
                            step += 2
                            dve.wait_ge(mod_step, step)
                            nc.vector.scalar_tensor_tensor(out=size, in0=size, scalar=0.25, in1=ps,
                                                           op0=ALU.max, op1=ALU.max).then_inc(mod_step, 1)
                            step += 1
                            dve.wait_ge(mod_step, step)
                            nc.vector.scalar_tensor_tensor(out=row, in0=sign, scalar=-1.0, in1=size,
                                                           op0=ALU.add, op1=ALU.mult).then_inc(mod_ready, 1)
                @block.tensor
                def _(pe):
                    pe.wait_ge(silu_step, 4)
                    for k in range(6):
                        pe.wait_ge(raw_mod_in[k % 2], 16 * (k // 2 + 1))
                        if k >= 2:
                            pe.wait_ge(mod_ready, k - 1)
                        for c in range(C):
                            mm = nc.tensor.matmul(ring[0:B, k % 2, :], c_den[:, c, :], raw_mod[k % 2][:, c, :],
                                                  start=(c == 0), stop=(c == C - 1))
                        mm.then_inc(mod_ps, 1)

            PRIMED = 1
            mod1_in, mod2_in = sem("mod1_in"), sem("mod2_in")
            w_parts_in = [sem("w_parts_in0"), sem("w_parts_in1")]
            x_in_s = [sem(f"x_in{k}") for k in range(4)]
            stat_step, rstd_step, rstd_ready = sem("stat_step"), sem("rstd_step"), sem("rstd_ready")
            stat_ready, x_hat_ready, h_ready = sem("stat_ready"), sem("x_hat_ready"), sem("h_ready")
            ht_ps, ht_hi, ht_lo = sem("ht_ps"), sem("ht_hi"), sem("ht_lo")
            qkv_ps, rope_terms, v_ready = sem("qkv_ps"), sem("rope_terms"), sem("v_ready")
            roped, hi_ready, k_hi_ready, parts_ready = sem("roped"), sem("hi_ready"), sem("k_hi_ready"), sem("parts_ready")
            stack_ps, stack_ready = sem("stack_ps"), sem("stack_ready")
            s_ps, s_read, max_step, max_rows, max_in = (
                sem("s_ps"), sem("s_read"), sem("max_step"), sem("max_rows"), sem("max_in"))
            st_ps, exp_ready, pv_done, y_taken, den_step, y_ready = (
                sem("st_ps"), sem("exp_ready"), sem("pv_done"), sem("y_taken"), sem("den_step"), sem("y_ready"))
            o_ps, o_gated, x1_ready = sem("o_ps"), sem("o_gated"), sem("x1_ready")
            res_in = [sem(f"res_in{k}") for k in range(4)]
            stat2_step, stat2_ready, rstd2_step, rstd2_ready = (
                sem("stat2_step"), sem("stat2_ready"), sem("rstd2_step"), sem("rstd2_ready"))
            x_hat2, h2_ready = sem("x_hat2"), sem("h2_ready")
            h2t_ps, h2t_ready, logit_ps, logit_ready = (
                sem("h2t_ps"), sem("h2t_ready"), sem("logit_ps"), sem("logit_ready"))
            x1_out = [sem("x1_out0"), sem("x1_out1")]
            h2_out = [sem("h2_out0"), sem("h2_out1")]

            MAXES = [(h, qt, kc) for qt in range(NT) for h in range(HG) for kc in range(qt // 4 + 1)]
            NM = len(MAXES)
            PAIRS = [(qc, kt, hp) for qc in range(NQC) for kt in range(4 * (qc + 1)) for hp in range(2)]
            NP = len(PAIRS)
            PROJECT_AT = {t: t for t in range(NT)}
            TURN_AT = {t + 2: t for t in range(NT)}
            FIRST_MAX, LAST_MAX = NT + 2, NP - 3
            MAXES_AT = [range((n - FIRST_MAX) * NM // (LAST_MAX + 1 - FIRST_MAX),
                              (n + 1 - FIRST_MAX) * NM // (LAST_MAX + 1 - FIRST_MAX))
                        if FIRST_MAX <= n <= LAST_MAX else range(0) for n in range(NP)]
            NORM_AT = {3 * t + 2: t for t in range(NT)}
            NORM_LEAD = 2

            NORM2_STEPS = NT + 3

            def entries(eng, body):
                with eng.Fori(0, B - 1) as b:
                    body(b, True)
                body(B - 1, False)

            def first_group(eng, b):
                return b * G if isinstance(b, int) else eng.snap(b * G)

            def uses_of(n):
                return (([("stack", 2 * TURN_AT[n])] if n in TURN_AT else [])
                        + ([("qkv", PROJECT_AT[n])] if n in PROJECT_AT else [])
                        + ([("stack", 2 * TURN_AT[n] + 1)] if n in TURN_AT else [])
                        + [("max", u) for u in MAXES_AT[n]])

            RING = [use for n in range(NP) for use in uses_of(n)]
            BANK = {use: k % 2 for k, use in enumerate(RING)}
            assert len(RING) % 2 == 0

            with nc.Block() as block:
                @block.sync
                def _(sp):
                    def load_w(b, g):
                        for k in range(2):
                            sp.dma_start(w_parts[:, g % 2, k, :, :].bitcast(f32), w_dram[k, g, :, :, :])\
                                .then_inc(w_parts_in[g % 2], 16)

                    for primed in (max_in, *x1_out, *h2_out):
                        sp.sem_inc(primed, PRIMED)

                    def load_entry(b, first):
                        if not first:
                            sp.wait_ge(h_ready, b * NT)
                            sp.wait_ge(x1_ready, PRIMED + (b - 1) * NT)
                        for k in (SA, CA):
                            sp.dma_start(mod_b[:, k, :], mod_dram[k, ds(b, 1), :].to_broadcast([P, D]))\
                                .then_inc(mod1_in, 16)
                        for t in range(NT):
                            if t >= 4:
                                sp.wait_ge(x_hat_ready, b * NT + t - 3)
                            sp.dma_start(x_in[:, t % 4, :], x_tiles[ds(b * NT + t, 1), :, :].squeeze(0))\
                                .then_inc(x_in_s[t % 4], 16)
                            if t == 3 and first:
                                sp.wait_ge(w_lo_out, 16 * 2 * G)
                                sp.wait_ge(w_hi_out, 16 * G)
                                load_w(0, 0)

                    load_entry(0, True)

                    def entry(b, more):
                        sp.wait_ge(h2_ready, PRIMED + b * NT)
                        for k in (GA, SB, CB):
                            sp.dma_start(mod_b[:, k, :], mod_dram[k, ds(b, 1), :].to_broadcast([P, D]))\
                                .then_inc(mod2_in, 16)
                        for g in range(G):
                            if g + 1 < G or more:
                                sp.wait_ge(qkv_ps, PRIMED + (b * G + g) * NT)
                                load_w(b, (g + 1) % G)
                            sp.wait_ge(max_rows, 4 * (b * G + g) + 4)
                            sp.dma_start(stack_t[MROW:MROW + 2 * HG, g % 2, 0, :, :].bitcast(f32),
                                         max_row[MROW:MROW + 2 * HG, :].unsqueeze(1).to_broadcast([2 * HG, HG, L]))\
                                .then_inc(max_in, 16)
                        if more:
                            load_entry(b + 1, False)
                        for t in range(NT + 2):
                            if t < NT:
                                if t < 4:
                                    sp.wait_ge(x_hat_ready, (b + 1 + int(more)) * NT)
                                else:
                                    sp.wait_ge(x1_ready, PRIMED + b * NT + t - 3)
                                sp.dma_start(x_in[:, t % 4, :], x_tiles[ds(b * NT + t, 1), :, :].squeeze(0))\
                                    .then_inc(res_in[t % 4], 16)
                            if t >= 2:
                                u = t - 2
                                sp.wait_ge(x1_ready, PRIMED + b * NT + u + 1)
                                sp.dma_start(x1_dram[ds(b * NT + u, 1), :, :].squeeze(0), x1[:, u % 2, :])\
                                    .then_inc(x1_out[u % 2], 16)
                                sp.wait_ge(h2_ready, PRIMED + b * NT + u + 1)
                                sp.dma_start(h2_dram[ds((b * NT + u) * P, P), :], x_hat_2[:, u % 2, :])\
                                    .then_inc(h2_out[u % 2], 16)

                    entries(sp, entry)
                    for k in range(2):
                        sp.wait_ge(x1_out[k], PRIMED + 16 * (TT // 2))
                        sp.wait_ge(h2_out[k], PRIMED + 16 * (TT // 2))

                @block.vector
                def _(dve):
                    for primed in (x1_ready, s_read, y_ready, h2_ready):
                        dve.sem_inc(primed, PRIMED)

                    def first_norm(b, t):
                        def statistics(t):
                            if t >= 2:
                                dve.wait_ge(rstd_ready, b * NT + t - 1)
                                dve.wait_ge(x_hat_ready, b * NT + t - 1)
                            dve.wait_ge(x_in_s[t % 4], 16 * (b * (NT // 4) + t // 4 + 1))
                            nc.vector.bn_stats(stats[:, t % 2, :], x_in[:, t % 4, :]).then_inc(stat_step, 1)
                            wait_apart(dve, stat_step, b * NT + t + 1)
                            nc.vector.bn_aggr(mean_var[:, t % 2, :], stats[:, t % 2, :]).then_inc(stat_ready, 1)

                        def low_part(t):
                            dve.wait_ge(ht_hi, b * NT + t + 1)
                            cols = slice(t * P, t * P + P)
                            nc.vector.tensor_tensor(h_lo[:, :, cols], ring[:, t % 2, :].rearrange("p (c n) -> p c n", c=C),
                                                    h_hi[:, :, cols].bitcast(f32), ALU.subtract).then_inc(ht_lo, 1)

                        if t == 0:
                            dve.wait_ge(mod1_in, 32 * (b + 1))
                            statistics(0)
                        if t < NT:
                            if t + 1 < NT:
                                statistics(t + 1)
                            if t >= 2:
                                dve.wait_ge(ht_ps, b * NT + t - 1)
                            nc.vector.scalar_tensor_tensor(out=x_hat[:, t % 2, :], in0=x_in[:, t % 4, :],
                                                           scalar=mean_var[:, t % 2, 0:1], in1=mod_b[:, CA, :],
                                                           op0=ALU.subtract, op1=ALU.mult).then_inc(x_hat_ready, 1)
                            dve.wait_ge(rstd_ready, b * NT + t + 1)
                            dve.wait_ge(x_hat_ready, b * NT + t + 1)
                            nc.vector.scalar_tensor_tensor(out=x_hat[:, t % 2, :], in0=x_hat[:, t % 2, :],
                                                           scalar=rstd[:, t % 2, 1:2], in1=mod_b[:, SA, :],
                                                           op0=ALU.mult, op1=ALU.add).then_inc(h_ready, 1)
                        if t >= 1:
                            low_part(t - 1)

                    for t in range(NT + 1):
                        first_norm(0, t)

                    def rope(i, t):
                        dve.wait_ge(qkv_ps, PRIMED + i * NT + t + 1)
                        if t >= 2:
                            dve.wait_ge(parts_ready, 2 * (i * NT + t - 1))
                        qk = ring[:, BANK["qkv", t], 0:256].rearrange("p (h d) -> p h d", d=DH)
                        nc.vector.tensor_tensor(rope_a[:, t % 2, :].rearrange("p (h d) -> p h d", d=DH), qk,
                                                trig[:, 0, t, :].unsqueeze(1).to_broadcast([P, 2 * HG, DH]),
                                                ALU.mult).then_inc(rope_terms, 1)
                        for half in range(2):
                            lo, src = 16 * half, 16 * (1 - half)
                            nc.vector.tensor_tensor(
                                rope_b[:, t % 2, :].rearrange("p (h d) -> p h d", d=DH)[:, :, lo:lo + 16],
                                qk[:, :, src:src + 16],
                                trig[:, 1, t, lo:lo + 16].unsqueeze(1).to_broadcast([P, 2 * HG, 16]),
                                ALU.mult).then_inc(rope_terms, 1)

                    def maximum(i, u):
                        h, qt, kc = MAXES[u]
                        width = min((qt + 1) * P - kc * 512, 512)
                        dst = neg_max2[:, qt - 4, h:h + 1] if kc else neg_max[:, qt, h:h + 1]
                        dve.wait_ge(s_ps, i * NM + u + 1)
                        nc.vector.tensor_reduce(dst, ring[:, BANK["max", u], 0:width], AX.X, ALU.max, negate=True)\
                            .then_inc(s_read, 1)

                    def max_to_rows(b, i):
                        dve.wait_ge(s_read, PRIMED + i * NM + NM)
                        nc.vector.tensor_tensor(neg_max[:, NT // 2:NT, :], neg_max[:, NT // 2:NT, :],
                                                neg_max2[:, :, :], ALU.min).then_inc(max_step, 1)
                        dve.wait_ge(max_step, 3 * i + 1)
                        nc.vector.tensor_copy(max_tok[:, :, 0:2 * HG:2].bitcast(f32r), neg_max[:, :, :])\
                            .then_inc(max_step, 1)
                        dve.wait_ge(max_step, 3 * i + 2)
                        nc.vector.tensor_tensor(max_tok[:, :, 1:2 * HG:2], neg_max[:, :, :],
                                                max_tok[:, :, 0:2 * HG:2], ALU.subtract).then_inc(max_step, 1)
                        dve.wait_ge(max_step, 3 * i + 3)
                        dve.wait_ge(max_in, PRIMED + 16 * i)
                        for k in range(2):
                            dve.wait_ge(x1_out[k], PRIMED + 16 * b * (NT // 2))
                        for q in range(4):
                            nc.vector.transpose(
                                max_row[MROW:P, :].rearrange("p (t q n) -> p t q n", q=4, n=32)[:, :, q, :],
                                max_tok[32 * q:32 * q + 32, :, :]).then_inc(max_rows, 1)

                    def normalise(i, g, qc):
                        part_of_y = y_t[:, g, qc * QC:(qc + 1) * QC]
                        dve.wait_ge(y_taken, PRIMED + 3 * (i * NQC + qc + 1))
                        nc.vector.reciprocal(r_den[:, :], r_den[:, :]).then_inc(den_step, 1)
                        dve.wait_ge(den_step, i * NQC + qc + 1)
                        nc.vector.tensor_tensor(part_of_y, part_of_y, r_den[:, :], ALU.mult).then_inc(y_ready, 1)

                    def prepare(b, i, n):
                        for kind, u in uses_of(n):
                            if kind == "qkv":
                                rope(i, u)
                            elif kind == "max":
                                maximum(i, u)
                        if n == LAST_MAX:
                            max_to_rows(b, i)

                    for n in range(NP):
                        prepare(0, 0, n)

                    def entry(b, more):
                        i0 = first_group(dve, b)
                        for g in range(G):
                            for n in range(NP):
                                if g + 1 < G:
                                    prepare(b, i0 + g + 1, n)
                                if n in (NT, NP - 1):
                                    normalise(i0 + g, g, int(n == NP - 1))
                                if g == G - 1 and more and n + NORM_LEAD in NORM_AT:
                                    first_norm(b + 1, NORM_AT[n + NORM_LEAD])
                        if more:
                            first_norm(b + 1, NT)

                        def residual(t):
                            dve.wait_ge(o_ps, b * NT + t + 1)
                            if t >= 2:
                                dve.wait_ge(x1_out[t % 2], PRIMED + 16 * (b * (NT // 2) + t // 2))
                                dve.wait_ge(x_hat2, b * NT + t - 1)
                            else:
                                dve.wait_ge(x1_out[t % 2], PRIMED + 16 * (b * (NT // 2)))
                            nc.vector.tensor_tensor(x1[:, t % 2, :], o_acc[t % 2], mod_b[:, GA, :], ALU.mult)\
                                .then_inc(o_gated, 1)
                            dve.wait_ge(res_in[t % 4], 16 * (b * (NT // 4) + t // 4 + 1))
                            dve.wait_ge(o_gated, b * NT + t + 1)
                            nc.vector.tensor_tensor(x1[:, t % 2, :], x1[:, t % 2, :], x_in[:, t % 4, :], ALU.add)\
                                .then_inc(x1_ready, 1)
                            dve.wait_ge(x1_ready, PRIMED + b * NT + t + 1)
                            if t >= 2:
                                dve.wait_ge(rstd2_ready, b * NT + t - 1)
                            nc.vector.bn_stats(stats[:, t % 2, :], x1[:, t % 2, :]).then_inc(stat2_step, 1)
                            wait_apart(dve, stat2_step, b * NT + t + 1)
                            nc.vector.bn_aggr(mean_var[:, t % 2, :], stats[:, t % 2, :]).then_inc(stat2_ready, 1)

                        def second_norm(k):
                            if k < NT:
                                residual(k)
                            if not 1 <= k <= NT:
                                return
                            t = k - 1
                            if t >= 2:
                                dve.wait_ge(h2_out[t % 2], PRIMED + 16 * (b * (NT // 2) + t // 2))
                                dve.wait_ge(h2t_ps, b * NT + t - 1)
                            nc.vector.scalar_tensor_tensor(out=x_hat_2[:, t % 2, :], in0=x1[:, t % 2, :],
                                                           scalar=mean_var[:, t % 2, 0:1], in1=mod_b[:, CB, :],
                                                           op0=ALU.subtract, op1=ALU.mult).then_inc(x_hat2, 1)
                            dve.wait_ge(rstd2_ready, b * NT + t + 1)
                            dve.wait_ge(x_hat2, b * NT + t + 1)
                            nc.vector.scalar_tensor_tensor(out=x_hat_2[:, t % 2, :], in0=x_hat_2[:, t % 2, :],
                                                           scalar=rstd[:, t % 2, 1:2], in1=mod_b[:, SB, :],
                                                           op0=ALU.mult, op1=ALU.add).then_inc(h2_ready, 1)

                        dve.wait_ge(mod2_in, 48 * (b + 1))
                        for n in range(NP if more else NORM2_STEPS):
                            if n < NORM2_STEPS:
                                second_norm(n)
                            if more:
                                prepare(b + 1, i0 + G, n)

                    entries(dve, entry)

                @block.gpsimd
                def _(pool):
                    def inverse_deviation(b, t, got, step, done):
                        wait_apart(pool, got, b * NT + t + 1)
                        nc.gpsimd.tensor_scalar(rstd[:, t % 2, 0:1], mean_var[:, t % 2, 1:2], EPS, None, ALU.add)\
                            .then_inc(step, 1)
                        pool.wait_ge(step, b * NT + t + 1)
                        nc.gpsimd.tensor_tensor(rstd[:, t % 2, 1:2], rstd[:, t % 2, 0:1], neg_half[:, :], ALU.pow)\
                            .then_inc(done, 1)

                    def first_norm(b):
                        for t in range(NT):
                            inverse_deviation(b, t, stat_ready, rstd_step, rstd_ready)

                    def split(i, t):
                        qk = rope_a[:, t % 2, :].rearrange("p (s h d) -> p s h d", s=2, d=DH)
                        out_q = parts_tok[:, t % 2, 0, :, :].rearrange("p h (s d) -> p h s d", d=DH)
                        out_k = parts_tok[:, t % 2, 1, :, :].rearrange("p h (s d) -> p h s d", d=DH)
                        pool.wait_ge(rope_terms, 3 * (i * NT + t + 1))
                        nc.gpsimd.tensor_tensor(rope_a[:, t % 2, :], rope_a[:, t % 2, :], rope_b[:, t % 2, :],
                                                ALU.add).then_inc(roped, 1)
                        wait_apart(pool, roped, i * NT + t + 1)
                        if t >= 2:
                            wait_apart(pool, stack_ps, 2 * (i * NT + t - 1))
                        nc.gpsimd.tensor_copy(out_q[:, :, 0:2, :].bitcast(f32r),
                                              qk[:, 0, :, :].unsqueeze(2).to_broadcast([P, HG, 2, DH]))\
                            .then_inc(hi_ready, 1)
                        pool.wait_ge(hi_ready, i * NT + t + 1)
                        nc.gpsimd.tensor_tensor(out_q[:, :, 2, :], qk[:, 0, :, :],
                                                out_q[:, :, 0, :], ALU.subtract)\
                            .then_inc(parts_ready, 1)
                        pool.wait_ge(k_hi_ready, i * NT + t + 1)
                        nc.gpsimd.tensor_tensor(out_k[:, :, 1, :], qk[:, 1, :, :],
                                                out_k[:, :, 0, :], ALU.subtract)\
                            .then_inc(parts_ready, 1)

                    first_norm(0)
                    for t in range(NT):
                        split(0, t)

                    def entry(b, more):
                        i0 = first_group(pool, b)
                        for g in range(1, G):
                            for t in range(NT):
                                split(i0 + g, t)

                        if more:
                            first_norm(b + 1)
                        for n in range(NP if more else NORM2_STEPS):
                            if n < NT:
                                inverse_deviation(b, n, stat2_ready, rstd2_step, rstd2_ready)
                            if more and n in PROJECT_AT:
                                split(i0 + G, PROJECT_AT[n])

                    entries(pool, entry)

                @block.scalar
                def _(act):
                    for primed in (exp_ready, logit_ready, y_taken):
                        act.sem_inc(primed, PRIMED)

                    def first_norm(b, t):
                        act.wait_ge(ht_ps, b * NT + t + 1)
                        nc.scalar.copy(h_hi[:, :, t * P:t * P + P],
                                       ring[:, t % 2, :].rearrange("p (c n) -> p c n", c=C)).then_inc(ht_hi, 1)

                    act.wait_ge(w_lo_out, 16 * 2 * G)
                    for t in range(NT):
                        first_norm(0, t)

                    def stack_part(i, g, t, s):
                        act.wait_ge(stack_ps, 2 * (i * NT + t) + s + 1)
                        nc.scalar.copy(stack_t[0:PARTS, g % 2, s, :, t * P:t * P + P],
                                       ring[0:PARTS, BANK["stack", 2 * t + s], :].rearrange("p (h n) -> p h n", h=HG))\
                            .then_inc(stack_ready, 1)

                    def keys_hi(i, t):
                        act.wait_ge(roped, i * NT + t + 1)
                        if t >= 2:
                            act.wait_ge(stack_ps, 2 * (i * NT + t - 1))
                        out_k = parts_tok[:, t % 2, 1, :, :].rearrange("p h (s d) -> p h s d", d=DH)
                        nc.scalar.copy(out_k[:, :, 0:3:2, :].bitcast(f32r),
                                       rope_a[:, t % 2, 128:256].rearrange("p (h d) -> p h d", d=DH)
                                       .unsqueeze(2).to_broadcast([P, HG, 2, DH])).then_inc(k_hi_ready, 1)

                    def prepare(i, g, n):
                        for kind, u in uses_of(n):
                            if kind == "stack":
                                stack_part(i, g, u // 2, u % 2)
                            elif kind == "qkv":
                                act.wait_ge(qkv_ps, PRIMED + i * NT + u + 1)
                                act.wait_ge(rope_terms, 3 * (i * NT + u + 1))
                                nc.scalar.copy(v_tok[:, g % 2, u, :, :].rearrange("p h d -> p (h d)"),
                                               ring[:, BANK["qkv", u], 256:384]).then_inc(v_ready, 1)
                        if n in PROJECT_AT:
                            keys_hi(i, PROJECT_AT[n])

                    for n in range(NP):
                        prepare(0, 0, n)

                    def entry(b, more):
                        i0 = first_group(act, b)

                        def exponentials(i, g, n):
                            qc, kt, hp = PAIRS[n]
                            q0 = max(0, kt * P - qc * QC)
                            act.wait_ge(st_ps, i * NP + n + 1)
                            if n >= 2:
                                act.wait_ge(pv_done, i * NP + n - 1)
                            if g == 0 and n == 0:
                                for k in range(2):
                                    act.wait_ge(h2_out[k], PRIMED + 16 * b * (NT // 2))
                            nc.scalar.activation(probs[:, n % 2, :, q0:QC], pair[:, n % 2, :, q0:QC], ACT.Exp,
                                                 scale=SCALE).then_inc(exp_ready, 1)

                        def take_output(i, g, qc):
                            last = sum(1 for p in PAIRS if p[0] <= qc)
                            act.wait_ge(pv_done, i * NP + last)
                            act.wait_ge(y_ready, PRIMED + i * NQC + qc)
                            if g == 0 and qc == 0:
                                act.wait_ge(x1_ready, PRIMED + b * NT)
                            for k in range(2):
                                nc.scalar.copy(r_den[64 * k:64 * k + 64, :], den_ps[64 - 64 * k:128 - 64 * k, :])\
                                    .then_inc(y_taken, 1)
                            nc.scalar.copy(y_t[:, g, qc * QC:(qc + 1) * QC], y_ps[:, :]).then_inc(y_taken, 1)

                        for g in range(G):
                            for n in range(NP):
                                exponentials(i0 + g, g, n)
                                if n in (NT, NP - 1):
                                    take_output(i0 + g, g, int(n == NP - 1))
                                if g + 1 < G:
                                    prepare(i0 + g + 1, g + 1, n)
                                if g == G - 1 and more and n in NORM_AT:
                                    first_norm(b + 1, NORM_AT[n])

                        def second_norm(k):
                            t, u = k - 2, k - 3
                            if 0 <= t < NT:
                                act.wait_ge(h2t_ps, b * NT + t + 1)
                                if t >= 2:
                                    act.wait_ge(logit_ps, b * NT + t - 1)
                                nc.scalar.copy(h2_t[:, t % 2, :, :].rearrange("p c n -> p (c n)"),
                                               pair[:, t % 2, 0, :]).then_inc(h2t_ready, 1)
                            if u >= 0:
                                act.wait_ge(logit_ps, b * NT + u + 1)
                                nc.scalar.copy(logits[:, ds(b * NT + u, 1), :].squeeze(1), pair[:, u % 2, 1, 0:E])\
                                    .then_inc(logit_ready, 1)

                        for n in range(NP if more else NORM2_STEPS):
                            if n < NORM2_STEPS:
                                second_norm(n)
                            if more:
                                prepare(i0 + G, 0, n)

                    entries(act, entry)

                @block.tensor
                def _(pe):
                    pe.sem_inc(qkv_ps, PRIMED)

                    def first_norm(b, t, first):
                        pe.wait_ge(h_ready, b * NT + t + 1)
                        if t >= 2:
                            pe.wait_ge(ht_lo, b * NT + t - 1)
                        elif t == 0 and not first:
                            pe.wait_ge(s_read, PRIMED + b * G * NM)
                        for c in range(C):
                            mm = nc.tensor.transpose(ring[:, t % 2, c * P:c * P + P],
                                                     x_hat[:, t % 2, c * P:c * P + P], ident_f[:, :])
                        mm.then_inc(ht_ps, 1)

                    for t in range(NT):
                        first_norm(0, t, True)

                    def bank_free(i, use):
                        k = RING.index(use) - 2
                        kind, u = RING[k] if k >= 0 else ("before", 0)
                        if kind == "qkv":
                            pe.wait_ge(v_ready, i * NT + u + 1)
                        elif kind == "stack":
                            pe.wait_ge(stack_ready, i * 2 * NT + u + 1)
                        elif kind == "max":
                            pe.wait_ge(s_read, PRIMED + i * NM + u + 1)
                        else:
                            pe.wait_ge(s_read, PRIMED + i * NM)

                    def project(b, i, g, t):
                        bank_free(i, ("qkv", t))
                        if t == 0:
                            pe.wait_ge(w_parts_in[g % 2], 32 * (2 * b + g // 2 + 1))
                        w_hi, w_lo = w_parts[:, g % 2, 0, :, :], w_parts[:, g % 2, 1, :, :]
                        cols = slice(t * P, t * P + P)
                        products = [(lhs, rhs, c) for c in range(C)
                                    for lhs, rhs in ((h_hi, w_hi), (h_hi, w_lo), (h_lo, w_hi))]
                        for k, (lhs, rhs, c) in enumerate(products):
                            mm = nc.tensor.matmul(ring[:, BANK["qkv", t], 0:384], lhs[:, c, cols], rhs[:, c, :],
                                                  start=(k == 0), stop=(k == len(products) - 1))
                        mm.then_inc(qkv_ps, 1)

                    def turn_parts(i, t, s):
                        bank_free(i, ("stack", 2 * t + s))
                        pe.wait_ge(parts_ready, 2 * (i * NT + t + 1))
                        for h in range(HG):
                            mm = nc.tensor.transpose(ring[0:PARTS, BANK["stack", 2 * t + s], h * P:h * P + P],
                                                     parts_tok[:, t % 2, s, h, :], ident_f[:, :])
                        mm.then_inc(stack_ps, 1)

                    def score_rows(i, g, u):
                        h, qt, kc = MAXES[u]
                        width = min((qt + 1) * P - kc * 512, 512)
                        diagonal = kc == qt // 4
                        if u == 0 or MAXES[u - 1][1] < qt:
                            pe.wait_ge(stack_ready, i * 2 * NT + 2 * (qt + 1))
                        bank_free(i, ("max", u))
                        mm = nc.tensor.matmul(ring[:, BANK["max", u], 0:width],
                                              stack_t[0:PARTS, g % 2, 0, h, qt * P:qt * P + P],
                                              stack_t[0:PARTS, g % 2, 1, h, kc * 512:kc * 512 + width],
                                              start=True, stop=not diagonal)
                        if diagonal:
                            mm = nc.tensor.matmul(ring[:, BANK["max", u], width - P:width], ident_b[:, :],
                                                  masks_b[:, 0, :], start=False, stop=True)
                        mm.then_inc(s_ps, 1)

                    def prepare(b, i, g, use):
                        kind, u = use
                        if kind == "stack":
                            turn_parts(i, u // 2, u % 2)
                        elif kind == "qkv":
                            project(b, i, g, u)
                        else:
                            score_rows(i, g, u)

                    pe.wait_ge(ht_lo, NT)
                    for n in range(NP):
                        for use in uses_of(n):
                            prepare(0, 0, 0, use)

                    def entry(b, more):
                        wait_apart(pe, x1_ready, PRIMED + b * NT)
                        i0 = first_group(pe, b)

                        def score_columns(i, g, n):
                            qc, kt, hp = PAIRS[n]
                            q0 = max(0, kt * P - qc * QC)
                            diagonal = kt * P >= qc * QC
                            if n == 0:
                                pe.wait_ge(max_in, PRIMED + 16 * i + 16)
                                pe.wait_ge(v_ready, (i + 1) * NT)
                                if g == 0:
                                    pe.wait_ge(logit_ready, PRIMED + b * NT)
                            pe.wait_ge(exp_ready, PRIMED + i * NP + max(n - 1, 0))
                            for j in range(2):
                                h = 2 * hp + j
                                mm = nc.tensor.matmul(pair[:, n % 2, j, q0:QC],
                                                      stack_t[:, g % 2, 1, h, kt * P:kt * P + P],
                                                      stack_t[:, g % 2, 0, h, qc * QC + q0:(qc + 1) * QC],
                                                      start=True, stop=not diagonal)
                                if diagonal:
                                    mm = nc.tensor.matmul(pair[:, n % 2, j, q0:q0 + P], ident_b[:, :],
                                                          masks_b[:, 1, :], start=False, stop=True)
                            mm.then_inc(st_ps, 1)

                        def values(i, g, n):
                            qc, kt, hp = PAIRS[n]
                            q0 = max(0, kt * P - qc * QC)
                            first, last = kt == 0, kt == 4 * qc + 3
                            pe.wait_ge(exp_ready, PRIMED + i * NP + n + 1)
                            if kt == 0 and hp == 0:
                                pe.wait_ge(y_taken, PRIMED + 3 * (i * NQC + qc))
                            for j in range(2):
                                at = 32 * (2 * hp + j)
                                nc.tensor.matmul(y_ps[at:at + 32, q0:QC], v_tok[:, g % 2, kt, 2 * hp + j, :],
                                                 probs[:, n % 2, j, q0:QC], start=first, stop=last)
                            for j in range(2):
                                at = (32 * (2 * hp + j) + 64) % P
                                mm = nc.tensor.matmul(den_ps[at:at + 32, q0:QC], ones[:, :],
                                                      probs[:, n % 2, j, q0:QC], start=first, stop=last)
                            mm.then_inc(pv_done, 1)

                        for g in range(G):
                            for n in range(NP):
                                uses = uses_of(n) if g + 1 < G else []
                                if n == 0 and uses:
                                    prepare(b, i0 + g + 1, g + 1, uses.pop(0))
                                score_columns(i0 + g, g, n)
                                for use in uses[:2]:
                                    prepare(b, i0 + g + 1, g + 1, use)
                                if n >= 1:
                                    values(i0 + g, g, n - 1)
                                for use in uses[2:]:
                                    prepare(b, i0 + g + 1, g + 1, use)
                                if g == G - 1 and more and n in NORM_AT:
                                    first_norm(b + 1, NORM_AT[n], False)
                            values(i0 + g, g, NP - 1)

                        pe.wait_ge(y_taken, PRIMED + 3 * (b + 1) * G * NQC)
                        if more:
                            pe.wait_ge(ht_lo, (b + 2) * NT)

                        def logits_of(t):
                            pe.wait_ge(h2t_ready, b * NT + t + 1)
                            if t >= 2:
                                pe.wait_ge(logit_ready, PRIMED + b * NT + t - 1)
                            for c in range(C):
                                mm = nc.tensor.matmul(pair[:, t % 2, 1, 0:E], h2_t[:, t % 2, c, :], w_gate[:, c, :],
                                                      start=(c == 0), stop=(c == C - 1))
                            mm.then_inc(logit_ps, 1)

                        def second_norm(t):
                            if t < NT:
                                if t % (NT // NQC) == 0:
                                    pe.wait_ge(y_ready, PRIMED + (b + 1) * G * NQC - (NQC - 1 - t // (NT // NQC)))
                                if t >= 2:
                                    pe.wait_ge(o_gated, b * NT + t - 1)
                                for g in range(G):
                                    mm = nc.tensor.matmul(o_acc[t % 2], y_t[:, g, t * P:t * P + P], w_out[:, g, :],
                                                          start=(g == 0), stop=(g == G - 1))
                                mm.then_inc(o_ps, 1)
                            if 2 <= t < NT + 2:
                                u = t - 2
                                pe.wait_ge(h2_ready, PRIMED + b * NT + u + 1)
                                if u >= 2:
                                    pe.wait_ge(h2t_ready, b * NT + u - 1)
                                for c in range(C):
                                    mm = nc.tensor.transpose(pair[:, u % 2, 0, c * P:c * P + P],
                                                             x_hat_2[:, u % 2, c * P:c * P + P], ident_f[:, :])
                                mm.then_inc(h2t_ps, 1)
                            if t >= 3:
                                logits_of(t - 3)

                        for n in range(NP if more else NORM2_STEPS):
                            if n < NORM2_STEPS:
                                second_norm(n)
                            if more:
                                for use in uses_of(n):
                                    prepare(b + 1, i0 + G, 0, use)

                    entries(pe, entry)

        y_dram = nc.dram_tensor("y_dram", [SLOTS * P, D], f32, kind="Internal").ap()

        with ExitStack() as part:
            def sb(name, shape, dt=f32):
                return part.enter_context(nc.sbuf_tensor(name, shape, dt))

            def ps(name, shape):
                return part.enter_context(nc.psum_tensor(name, shape, f32))

            TE = TT * E
            w1_sb = sb("w1_sb", [P, E, C, F])
            w2_sb = sb("w2_sb", [P, E, F // P, D])
            slot_of = sb("slot_of", [P, TT, 2], i32)
            weight = sb("weight", [P, TT, 2])
            expert_of = sb("expert_of", [1, SLOTS], i32)
            tokens = sb("tokens", [P, SLOTS], i32)
            gb_b = sb("gb_b", [P, B, D])

            w_in = [sem("w1_in"), sem("w2_in")]
            tab_in, filled, gb_in = sem("tab_in"), sem("filled"), sem("gb_in")
            r_dve, r_act, r_pe, pos_ready, r_last = (
                sem("r_dve"), sem("r_act"), sem("r_pe"), sem("pos_ready"), sem("r_last"))
            row_selected, tile_selected, ids_ps = sem("row_selected"), sem("tile_selected"), sem("ids_ps")

            with ExitStack() as inner:
                def tmp(name, shape, dt=f32):
                    return inner.enter_context(nc.sbuf_tensor(name, shape, dt))

                bal_b = tmp("bal_b", [P, E])
                count = tmp("count", [P, P])
                count_e, count_s = count[:, 0:E], count[:, 0:SLOTS]
                ids = tmp("ids", [P, TT])
                sel_row = tmp("sel_row", [P, 4, 2, P])
                sel_tile = tmp("sel_tile", [P, 4, 2, SLOTS])
                earlier = tmp("earlier", [P, P])
                all_ones = tmp("all_ones", [P, P])
                restart = tmp("restart", [P, E, TT])
                z = tmp("z", [P, TT, E])
                score = tmp("score", [P, TT, E])
                top = tmp("top", [P, TT, 8])
                top_at = tmp("top_at", [P, TT, 8], u32)
                at_f = tmp("at_f", [P, TT, 2])
                pick = tmp("pick", [P, 2, TT, E])
                both = tmp("both", [P, TT, E])
                upto = tmp("upto", [P, E, TT])
                slot_e = tmp("slot_e", [P, E, TT])
                cnt_i = tmp("cnt_i", [P, E], i32)
                tiles = tmp("tiles", [P, E])
                upto_e = tmp("upto_e", [P, E])
                base = tmp("base", [P, E])
                total = tmp("total", [P, TT])
                slot_f = tmp("slot_f", [P, TT, 2])
                tile_i = tmp("tile_i", [P, TT, 2], i32)
                tile_f = tmp("tile_f", [P, TT, 2])
                row_f = tmp("row_f", [P, TT, 2])
                cmp = tmp("cmp", [1, SLOTS, E])
                exp_f = tmp("exp_f", [1, SLOTS])
                before_ps = inner.enter_context(nc.psum_tensor("before_ps", [P, E, TT], f32))
                all_ps = inner.enter_context(nc.psum_tensor("all_ps", [P, E, TT], f32))
                tok_ps = inner.enter_context(nc.psum_tensor("tok_ps", [P, SLOTS], f32))

                with nc.Block() as block:
                    @block.sync
                    def _(sp):
                        sp.dma_start(bal_b[:, :], bal.to_broadcast([P, E])).then_inc(tab_in, 16)
                        sp.dma_start(count[:, :], counts).then_inc(tab_in, 16)
                        sp.dma_start(ids[:, :], tok_ids).then_inc(tab_in, 16)
                        sp.dma_start(earlier[:, :], earlier_t).then_inc(tab_in, 16)
                        for b in range(B):
                            sp.dma_start(gb_b[:, b, :], mod_dram[GB, b:b + 1, :].to_broadcast([P, D]))\
                                .then_inc(gb_in, 16)
                        sp.wait_ge(gb_in, 16 * B)

                    @block.scalar
                    def _(act):
                        act.wait_ge(tab_in, 64)
                        act.dma_start(w1_sb[:, :, :, :], w1).then_inc(w_in[0], 16)
                        act.dma_start(w2_sb[:, :, :, :], w2).then_inc(w_in[1], 16)
                        act.wait_ge(r_dve, 1)
                        nc.scalar.activation(score[:, :, :], z[:, :, :], ACT.Exp, scale=-1.0).then_inc(r_act, 1)

                    @block.tensor
                    def _(pe):
                        pe.wait_ge(r_dve, 11)
                        pe.wait_ge(tab_in, 64)
                        pe.wait_ge(filled, 2)
                        nc.tensor.matmul(before_ps[:, :, :], earlier[:, :], both[:, :, :].rearrange("p t e -> p e t"),
                                         start=True, stop=True).then_inc(r_pe, 1)
                        nc.tensor.matmul(all_ps[:, :, :], all_ones[:, :], both[:, :, :].rearrange("p t e -> p e t"),
                                         start=True, stop=True).then_inc(r_pe, 1)
                        for t in range(TT):
                            pe.wait_ge(row_selected, t + 1)
                            pe.wait_ge(tile_selected, 3 * t + 3)
                            for k in range(2):
                                mm = nc.tensor.matmul(tok_ps[:, :], sel_row[:, t % 4, k, :], sel_tile[:, t % 4, k, :],
                                                      start=(t == 0 and k == 0), stop=(t == TT - 1 and k == 1))
                            mm.then_inc(ids_ps, 1)

                    @block.gpsimd
                    def _(pool):
                        nc.gpsimd.memset(all_ones[:, :], 1.0).then_inc(filled, 1)
                        nc.gpsimd.memset(restart[:, :, :], 1.0).then_inc(filled, 1)
                        pool.wait_ge(pos_ready, 1)
                        pool.wait_ge(tab_in, 64)
                        for t in range(TT):
                            if t >= 4:
                                pool.wait_ge(ids_ps, t - 3)
                            nc.gpsimd.tensor_scalar(sel_row[:, t % 4, 1, :], count[:, :], row_f[:, t, 1:2], None,
                                                    ALU.is_equal)\
                                .then_inc(row_selected, 1)

                    @block.vector
                    def _(dve):
                        step = [0]

                        def done(instruction):
                            step[0] += 1
                            instruction.then_inc(r_dve, 1)
                            dve.wait_ge(r_dve, step[0])

                        v = nc.vector
                        dve.wait_ge(tab_in, 64)
                        done(v.tensor_tensor(z[:, :, :], logits[:, :, :], bal_b[:, :].unsqueeze(1).to_broadcast([P, TT, E]),
                                             ALU.add))
                        dve.wait_ge(r_act, 1)
                        done(v.tensor_scalar_add(z[:, :, :], score[:, :, :], 1.0))
                        done(v.reciprocal(score[:, :, :], z[:, :, :]))
                        for t in range(TT):
                            last = v.max(top[:, t, :], score[:, t, :])
                        done(last)
                        for t in range(TT):
                            last = v.max_index(top_at[:, t, :], top[:, t, :], score[:, t, :])
                        done(last)
                        done(v.tensor_copy(at_f[:, :, :], top_at[:, :, 0:2]))
                        for k in range(2):
                            last = v.tensor_tensor(pick[:, k, :, :], count_e.unsqueeze(1).to_broadcast([P, TT, E]),
                                                   at_f[:, :, k:k + 1].to_broadcast([P, TT, E]), ALU.is_equal)
                        done(last)
                        done(v.tensor_tensor(total[:, :], top[:, :, 0], top[:, :, 1], ALU.add))
                        done(v.tensor_scalar_add(total[:, :], total[:, :], 1e-6))
                        done(v.reciprocal(total[:, :], total[:, :]))
                        done(v.tensor_tensor(both[:, :, :], pick[:, 0, :, :], pick[:, 1, :, :], ALU.add))
                        done(v.tensor_tensor(weight[:, :, :], top[:, :, 0:2], total[:, :].unsqueeze(2).to_broadcast([P, TT, 2]),
                                             ALU.mult))
                        dve.wait_ge(filled, 2)
                        done(v.memset(restart[:, :, 0:1], 0.0))
                        dve.wait_ge(r_pe, 2)
                        done(v.tensor_tensor_scan(upto[:, :, :].rearrange("p e t -> p (e t)"),
                                                  restart[:, :, :].rearrange("p e t -> p (e t)"),
                                                  all_ps[:, :, :].rearrange("p e t -> p (e t)"), 0.0, ALU.mult, ALU.add))
                        done(v.tensor_scalar_add(cnt_i[:, :], upto[:, :, TT - 1], float(P - 1)))
                        done(v.tensor_scalar(cnt_i[:, :], cnt_i[:, :], 7, None, ALU.arith_shift_right))
                        done(v.tensor_copy(tiles[:, :], cnt_i[:, :]))
                        done(v.tensor_tensor_scan(upto_e[:, :], all_ones[:, 0:E], tiles[:, :], 0.0, ALU.mult, ALU.add))
                        done(v.tensor_tensor(base[:, :], upto_e[:, :], tiles[:, :], ALU.subtract))
                        done(v.tensor_scalar(base[:, :], base[:, :], float(P), None, ALU.mult))
                        done(v.tensor_tensor(upto[:, :, :], upto[:, :, :], all_ps[:, :, :], ALU.subtract))
                        done(v.tensor_tensor(upto[:, :, :], upto[:, :, :], before_ps[:, :, :], ALU.add))
                        done(v.tensor_tensor(slot_e[:, :, :], upto[:, :, :],
                                             base[:, :].unsqueeze(2).to_broadcast([P, E, TT]), ALU.add))
                        for k in range(2):
                            done(v.tensor_tensor(pick[:, k, :, :], pick[:, k, :, :],
                                                 slot_e[:, :, :].rearrange("p e t -> p t e"), ALU.mult))
                            done(v.tensor_reduce(slot_f[:, :, k:k + 1], pick[:, k, :, :], AX.X, ALU.add))
                        done(v.tensor_copy(slot_of[:, :, :], slot_f[:, :, :]))
                        done(v.tensor_scalar(tile_i[:, :, :], slot_of[:, :, :], 7, None, ALU.arith_shift_right))
                        done(v.tensor_copy(tile_f[:, :, :], tile_i[:, :, :]))
                        done(v.scalar_tensor_tensor(out=row_f[:, :, :], in0=tile_f[:, :, :], scalar=float(-P),
                                                    in1=slot_f[:, :, :], op0=ALU.mult, op1=ALU.add))
                        v.engine_nop().then_inc(pos_ready, 1)
                        for t in range(TT):
                            if t >= 4:
                                dve.wait_ge(ids_ps, t - 3)
                            v.tensor_tensor(sel_row[:, t % 4, 0, :], count[:, :], row_f[:, t, 0:1].to_broadcast([P, P]),
                                            ALU.is_equal).then_inc(tile_selected, 1)
                            for k in range(2):
                                v.tensor_scalar(sel_tile[:, t % 4, k, :], count_s, tile_f[:, t, k:k + 1], ids[:, t:t + 1],
                                                ALU.is_equal, ALU.mult).then_inc(tile_selected, 1)
                        done(v.tensor_tensor(cmp[:, :, :], upto_e[0:1, :].unsqueeze(1).to_broadcast([1, SLOTS, E]),
                                             count_s[0:1, :].unsqueeze(2).to_broadcast([1, SLOTS, E]), ALU.is_le))
                        done(v.tensor_reduce(exp_f[:, :].unsqueeze(2), cmp[:, :, :], AX.X, ALU.add))
                        v.tensor_scalar_min(expert_of[:, :], exp_f[:, :], float(E - 1)).then_inc(r_last, 1)
                        dve.wait_ge(ids_ps, TT)
                        v.tensor_copy(tokens[:, :], tok_ps[:, :]).then_inc(r_last, 1)

            xg = sb("xg", [P, 4, D])
            idx = sb("idx", [P, 4], i32)
            xg_t = sb("xg_t", [P, 2, C, P])
            e_neg = sb("e_neg", [P, 2, F])
            den = sb("den", [P, 2, F])
            hid = sb("hid", [P, 2, F])
            hid_t = sb("hid_t", [P, 2, F // P, P])
            y_sb = sb("y_sb", [P, 4, D])

            idx_ready = sem("idx_ready")
            xg_in = [sem(f"xg_in{k}") for k in range(4)]
            y_out = [sem(f"y_out{k}") for k in range(4)]
            xt_ps_r, xt_read, up_r, exp_r, den_r, rec_r, hid_r, ht_ps_r, ht_read, y_ps_r, y_read = (
                sem(n) for n in ("xt_ps_r", "xt_read", "up_r", "exp_r", "den_r", "rec_r", "hid_r", "ht_ps_r", "ht_read",
                                 "y_ps_r", "y_read"))

            with ExitStack() as inner:
                def ips(name, shape):
                    return inner.enter_context(nc.psum_tensor(name, shape, f32))

                xt_ps = ips("xt_ps", [P, 2, 512])
                up_ps = ips("up_ps", [P, 2, 512])
                ht_ps_ = ips("ht_ps_", [P, 2, 512])
                yo_ps = ips("yo_ps", [P, 2, 512])

                LAST = 3

                def steps(eng, body):
                    for s in range(4):
                        body(s, s, range(s + 1))
                    with eng.Fori(1, SLOTS // 4) as i:
                        s0 = eng.snap(i * 4)
                        for k in range(4):
                            body(s0 + k, k, range(4))
                    for s in range(SLOTS, SLOTS + LAST):
                        body(s, s % 4, range(s - SLOTS + 1, 4))

                with nc.Block() as block:
                    @block.gpsimd
                    def _(pool):
                        def body(s, k, ages):
                            if 0 in ages:
                                if 3 in ages:
                                    wait_apart(pool, xt_ps_r, s - 3)
                                nc.gpsimd.tensor_copy(idx[:, k:k + 1], tokens[:, ds(s, 1)]).then_inc(idx_ready, 1)
                                wait_apart(pool, idx_ready, s + 1)
                                pool.indirect_dma_start(
                                    out=xg[:, k, :], out_offset=None, in_=h2_dram,
                                    in_offset=bass.IndirectOffsetOnAxis(ap=idx[:, k:k + 1], axis=0))\
                                    .then_inc(xg_in[k], 16)
                        steps(pool, body)

                    @block.tensor
                    def _(pe):
                        for k in range(2):
                            pe.wait_ge(w_in[k], 16)

                        def body(s, k, ages):
                            if 0 in ages:
                                pe.wait_ge(xg_in[k], 4 * (s - k) + 16)
                                if 2 in ages:
                                    pe.wait_ge(xt_read, s - 1)
                                for c in range(C):
                                    mm = nc.tensor.transpose(xt_ps[:, k % 2, c * P:c * P + P], xg[:, k, c * P:c * P + P],
                                                             ident_f[:, :])
                                mm.then_inc(xt_ps_r, 1)
                            if 1 in ages:
                                e = pe.value_load(expert_of[0:1, ds(s - 1, 1)], min_val=0, max_val=E - 1)
                                j = (k + 1) % 2
                                pe.wait_ge(xt_read, s)
                                if 3 in ages:
                                    pe.wait_ge(hid_r, s - 2)
                                for c in range(C):
                                    mm = nc.tensor.matmul(up_ps[:, j, 0:F], xg_t[:, j, c, :],
                                                          w1_sb[:, ds(e, 1), c, :].squeeze(1),
                                                          start=(c == 0), stop=(c == C - 1))
                                mm.then_inc(up_r, 1)
                            if 2 in ages:
                                j = k % 2
                                pe.wait_ge(hid_r, s - 1)
                                for c in range(F // P):
                                    mm = nc.tensor.transpose(ht_ps_[:, j, c * P:c * P + P], hid[:, j, c * P:c * P + P],
                                                             ident_f[:, :])
                                mm.then_inc(ht_ps_r, 1)
                            if 3 in ages:
                                e = pe.value_load(expert_of[0:1, ds(s - 3, 1)], min_val=0, max_val=E - 1)
                                j = (k + 1) % 2
                                pe.wait_ge(ht_read, s - 2)
                                pe.wait_ge(y_read, PRIMED + s - 4)
                                for c in range(F // P):
                                    mm = nc.tensor.matmul(yo_ps[:, j, :], hid_t[:, j, c, :],
                                                          w2_sb[:, ds(e, 1), c, :].squeeze(1),
                                                          start=(c == 0), stop=(c == F // P - 1))
                                mm.then_inc(y_ps_r, 1)
                        steps(pe, body)

                    @block.scalar
                    def _(act):
                        def body(s, k, ages):
                            if 0 in ages:
                                j = k % 2
                                act.wait_ge(xt_ps_r, s + 1)
                                if 2 in ages:
                                    act.wait_ge(up_r, s - 1)
                                nc.scalar.copy(xg_t[:, j, :, :].rearrange("p c n -> p (c n)"), xt_ps[:, j, :])\
                                    .then_inc(xt_read, 1)
                            if 1 in ages:
                                j = (k + 1) % 2
                                act.wait_ge(up_r, s)
                                if 3 in ages:
                                    act.wait_ge(den_r, s - 2)
                                nc.scalar.activation(e_neg[:, j, :], up_ps[:, j, 0:F], ACT.Exp, scale=-1.0)\
                                    .then_inc(exp_r, 1)
                            if 2 in ages:
                                j = k % 2
                                act.wait_ge(ht_ps_r, s - 1)
                                if 3 in ages:
                                    act.wait_ge(y_ps_r, PRIMED + s - 4)
                                nc.scalar.copy(hid_t[:, j, :, :].rearrange("p c n -> p (c n)"), ht_ps_[:, j, 0:F])\
                                    .then_inc(ht_read, 1)
                        steps(act, body)

                    @block.vector
                    def _(dve):
                        dve.sem_inc(y_read, PRIMED)

                        def body(s, k, ages):
                            if 1 in ages:
                                j = (k + 1) % 2
                                dve.wait_ge(exp_r, s)
                                nc.vector.tensor_scalar_add(den[:, j, :], e_neg[:, j, :], 1.0).then_inc(den_r, 1)
                                dve.wait_ge(den_r, s)
                                nc.vector.reciprocal(den[:, j, :], den[:, j, :]).then_inc(rec_r, 1)
                                dve.wait_ge(rec_r, s)
                                if 3 in ages:
                                    dve.wait_ge(ht_ps_r, s - 2)
                                nc.vector.tensor_tensor(hid[:, j, :], den[:, j, :], up_ps[:, j, 0:F], ALU.mult)\
                                    .then_inc(hid_r, 1)
                            if 3 in ages:
                                dve.wait_ge(y_ps_r, PRIMED + s - 3)
                                dve.wait_ge(y_out[(k + 1) % 4], PRIMED + 4 * (s - 3 - (k + 1) % 4))
                                nc.vector.tensor_copy(y_sb[:, (k + 1) % 4, :], yo_ps[:, (k + 1) % 2, :])\
                                    .then_inc(y_read, 1)
                        steps(dve, body)

                    @block.sync
                    def _(sp):
                        for k in range(4):
                            sp.sem_inc(y_out[k], PRIMED)
                        with sp.Fori(0, SLOTS // 4) as i:
                            for k in range(4):
                                sp.wait_ge(y_read, PRIMED + i * 4 + k + 1)
                                sp.dma_start(y_dram[ds((i * 4 + k) * P, P), :], y_sb[:, k, :]).then_inc(y_out[k], 16)
                        for k in range(4):
                            sp.wait_ge(y_out[k], PRIMED + 16 * (SLOTS // 4))

            ya = sb("ya", [P, 4, D])
            yb = sb("yb", [P, 4, D])
            xr = sb("xr", [P, 4, D])
            res = sb("res", [P, 4, D])
            yab_in = [[sem(f"y{n}_in{k}") for k in range(4)] for n in "ab"]
            xr_in = [sem(f"xr_in{k}") for k in range(4)]
            out_s = [sem(f"out_s{k}") for k in range(4)]
            m_a, m_b, m_g, m_x = sem("m_a"), sem("m_b"), sem("m_g"), sem("m_x")
            out_tiles = out.rearrange("b (t p) d -> (b t) p d", p=P)

            with nc.Block() as block:
                @block.gpsimd
                def _(pool):
                    for t in range(TT):
                        for n, dst in enumerate((ya, yb)):
                            if t >= 4:
                                pool.wait_ge(m_b, t - 3)
                            pool.indirect_dma_start(
                                out=dst[:, t % 4, :], out_offset=None, in_=y_dram,
                                in_offset=bass.IndirectOffsetOnAxis(ap=slot_of[:, t, n:n + 1], axis=0))\
                                .then_inc(yab_in[n][t % 4], 16)

                @block.sync
                def _(sp):
                    for t in range(TT):
                        if t >= 4:
                            sp.wait_ge(m_x, t - 3)
                        sp.dma_start(xr[:, t % 4, :], x1_dram[t, :, :]).then_inc(xr_in[t % 4], 16)

                @block.scalar
                def _(act):
                    for t in range(TT):
                        act.wait_ge(m_x, t + 1)
                        act.dma_start(out_tiles[t, :, :], res[:, t % 4, :]).then_inc(out_s[t % 4], 16)
                    for k in range(4):
                        act.wait_ge(out_s[k], 16 * (TT // 4))

                @block.vector
                def _(dve):
                    for t in range(TT):
                        k = t % 4
                        dve.wait_ge(yab_in[0][k], 16 * (t // 4 + 1))
                        if t >= 4:
                            dve.wait_ge(out_s[k], 16 * (t // 4))
                        nc.vector.tensor_scalar(res[:, k, :], ya[:, k, :], weight[:, t, 0:1], None, ALU.mult)\
                            .then_inc(m_a, 1)
                        dve.wait_ge(yab_in[1][k], 16 * (t // 4 + 1))
                        dve.wait_ge(m_a, t + 1)
                        nc.vector.scalar_tensor_tensor(out=res[:, k, :], in0=yb[:, k, :], scalar=weight[:, t, 1:2],
                                                       in1=res[:, k, :], op0=ALU.mult, op1=ALU.add).then_inc(m_b, 1)
                        dve.wait_ge(m_b, t + 1)
                        nc.vector.tensor_tensor(res[:, k, :], res[:, k, :], gb_b[:, t // NT, :], ALU.mult)\
                            .then_inc(m_g, 1)
                        dve.wait_ge(m_g, t + 1)
                        dve.wait_ge(xr_in[k], 16 * (t // 4 + 1))
                        nc.vector.tensor_tensor(res[:, k, :], res[:, k, :], xr[:, k, :], ALU.add).then_inc(m_x, 1)


def _constants(np):
    ident = np.eye(P, dtype=np.float32)
    later = np.triu(np.ones((P, P), np.float32), 1) * np.float32(-1e30)
    masks = np.ascontiguousarray(np.stack([later, later.T], 1))
    inv = np.float32(1.0) / np.float32(10000.0) ** (np.arange(0, DH, 2, dtype=np.float32) / np.float32(DH))
    angle = np.arange(L, dtype=np.float32)[:, None] * inv[None, :]
    cos, sin = np.cos(angle), np.sin(angle)
    rope = np.stack([np.concatenate([cos, cos], 1), np.concatenate([-sin, sin], 1)])
    rope = np.ascontiguousarray(rope.reshape(2, NT, P, DH).transpose(2, 0, 1, 3).astype(np.float32))
    k_ones = np.zeros((P, HG), np.float32)
    for h in range(HG):
        k_ones[MROW + 2 * h:MROW + 2 * h + 2, h] = 1.0
    rows = lambda n: np.ascontiguousarray(np.broadcast_to(np.arange(n, dtype=np.float32), (P, n)))
    tok_ids = np.ascontiguousarray(np.arange(TT * P, dtype=np.float32).reshape(TT, P).T)
    earlier = np.triu(np.ones((P, P), np.float32), 1)
    return dict(ident=ident, masks=masks, rope=rope, k_ones=k_ones, counts=rows(P),
                tok_ids=tok_ids, earlier_t=earlier)


def _layout(np, i):
    w = i["L0_attn_W_qkv"].reshape(3, G, HG, DH, D)
    even_odd = w.reshape(3, G, HG, DH // 2, 2, D).transpose(0, 1, 2, 4, 3, 5).reshape(3, G, HG, DH, D)
    w = np.concatenate([even_odd[:2], w[2:]], 0).transpose(1, 0, 2, 3, 4).reshape(3 * D, D)
    chunks = lambda a: np.ascontiguousarray(a.reshape(C, P, *a.shape[1:]).transpose(1, 0, *range(2, a.ndim + 1)))
    return dict(
        x=np.ascontiguousarray(i["L0_attn_x"]),
        w_qkv_t=chunks(w.T), w_o_t=chunks(i["L0_attn_W_o"].T), wg_t=chunks(i["L0_ffn_Wg"].T),
        bal=np.ascontiguousarray(i["L0_ffn_balance_bias"].reshape(1, E)),
        w1=np.ascontiguousarray(i["L0_ffn_W1"].reshape(E, C, P, F).transpose(2, 0, 1, 3)),
        w2=np.ascontiguousarray(i["L0_ffn_W2"].reshape(E, F // P, P, D).transpose(2, 0, 1, 3)),
        c_t=chunks(i["L0_c"].T), w_mod=chunks(i["L0_wmod"].reshape(D, 6, D)))


def kernel(**inputs):
    import numpy as _np
    import concourse.bacc as _bacc
    from concourse import mybir as _mybir
    from concourse.bass_utils import run_bass_kernel_spmd as _run

    nc = _bacc.Bacc("TRN2", target_bir_lowering=False, num_devices=1)
    arrays = {**_layout(_np, {k: _np.asarray(v) for k, v in inputs.items()}), **_constants(_np)}
    aps = {name: nc.dram_tensor(name, a.shape, _mybir.dt.from_np(a.dtype), kind="ExternalInput").ap()
           for name, a in arrays.items()}
    out = nc.dram_tensor("out", [B, L, D], _mybir.dt.float32, kind="ExternalOutput").ap()
    adaln_block(nc, **aps, out=out)
    r = _run(nc, [arrays], core_ids=[0])
    return r.results[0]["out"]
```
